# Optimizing a Trainium2 kernel written in Bass

```python
import numpy as np
import jax
import jax.numpy as jnp

def _softmax(x, axis=-1):
    return jax.nn.softmax(x, axis=axis)

def _gelu(x):
    return jax.nn.gelu(x, approximate=True)

def _silu(x):
    return jax.nn.silu(x)

def _sigmoid(x):
    return jax.nn.sigmoid(x)

def _layernorm(x, axis=-1, eps=1e-05):
    m = jnp.mean(x, axis=axis, keepdims=True)
    v = jnp.var(x, axis=axis, keepdims=True)
    return (x - m) / jnp.sqrt(v + eps)

def _scatter_add(tgt, idx, src, axis=0):
    return tgt.at[idx].add(src)

def _segment_sum(src, seg, n):
    return jax.ops.segment_sum(src, seg, n)
kernel_name = 'mk_hybrid_d1_jaxref_r8_59cd37'

def setup_inputs(seed: int=0):
    np.random.seed(seed)
    _w = jnp.asarray

    def _L0_attn_a_setup():
        import jax, jax.numpy as jnp
        import numpy as np
        from jax import lax
        B, L, D = (2, 256, 128)
        E, N, D_DELTA, D_CONV = (256, 16, 64, 4)
        EPS = 1e-05
        key = jax.random.key(seed)
        ks = jax.random.split(key, 16)
        s = lambda fan_in: 1.0 / np.sqrt(fan_in)
        return {'resid': jax.random.normal(ks[0], (B, L, D), jnp.float32), 'norm_w': jnp.ones((D,), jnp.float32), 'skip_w': jax.random.normal(ks[1], (E, D), jnp.float32) * s(D), 'in_w': jax.random.normal(ks[2], (E, D), jnp.float32) * s(D), 'conv_w': jax.random.normal(ks[3], (E, 1, D_CONV), jnp.float32) * s(D_CONV), 'conv_b': jnp.zeros((E,), jnp.float32), 'wd1': jax.random.normal(ks[4], (D_DELTA, E), jnp.float32) * s(E), 'wd2': jax.random.normal(ks[5], (E, D_DELTA), jnp.float32) * s(D_DELTA), 'wd2_b': jnp.zeros((E,), jnp.float32), 'wb': jax.random.normal(ks[6], (N, E), jnp.float32) * s(E), 'wc': jax.random.normal(ks[7], (N, E), jnp.float32) * s(E), 'A_log': jnp.log(jax.random.uniform(ks[8], (E, N), jnp.float32, 0.5, 1.5)), 'W_D': jnp.ones((E,), jnp.float32), 'out_w': jax.random.normal(ks[9], (D, E), jnp.float32) * s(E)}
    _L0_attn_a_in = _L0_attn_a_setup()

    def _L0_attn_b_setup():
        import jax, jax.numpy as jnp
        import numpy as np
        import math
        N_HEAD = 16
        DEG = 2
        EPS = 1e-07
        key = jax.random.key(seed)
        k1, k2 = jax.random.split(key)
        B, T, C = (2, 256, 128)
        x = jax.random.normal(k1, (B, T, C), dtype=jnp.float32)
        W = jax.random.normal(k2, (3 * C + N_HEAD, C), dtype=jnp.float32) * (1.0 / math.sqrt(C))
        return {'x': x, 'W': W}
    _L0_attn_b_in = _L0_attn_b_setup()

    def _L0_ffn_setup():
        import jax, jax.numpy as jnp
        import numpy as np
        DIM = 128
        DEPTH = 2
        HEADS = 8
        DIM_HEAD = 64
        WINDOW = 64
        INNER = HEADS * DIM_HEAD
        HID = int(DIM * 4 * 2 / 3)
        B, N = (2, 1024)
        QK_SCALE = 8.0

        def shift_token(t):
            t1, t2 = jnp.split(t, 2, axis=-1)
            t2 = jnp.pad(t2, ((0, 0), (1, 0), (0, 0)))[:, :-1]
            return jnp.concatenate([t1, t2], axis=-1)

        def l2norm(t):
            return t / jnp.clip(jnp.linalg.norm(t, axis=-1, keepdims=True), 1e-12)

        def rotate_half(x):
            x1, x2 = jnp.split(x, 2, axis=-1)
            return jnp.concatenate([-x2, x1], axis=-1)

        def rotary_xpos(q, k):
            n = q.shape[-2]
            half_idx = jnp.arange(0, DIM_HEAD, 2, dtype=jnp.float32)
            inv_freq = 1.0 / 10000.0 ** (half_idx / DIM_HEAD)
            t = jnp.arange(n, dtype=jnp.float32)
            freqs = t[:, None] * inv_freq[None, :]
            freqs = jnp.concatenate([freqs, freqs], axis=-1)
            base = (half_idx + 0.4 * DIM_HEAD) / (1.4 * DIM_HEAD)
            power = (t - n // 2) / float(WINDOW // 2)
            scale = base[None, :] ** power[:, None]
            scale = jnp.concatenate([scale, scale], axis=-1)
            cos, sin = (jnp.cos(freqs), jnp.sin(freqs))
            q = q * cos * scale + rotate_half(q) * sin * scale
            k = k * cos / scale + rotate_half(k) * sin / scale
            return (q, k)

        def local_attention(q, k, v):
            b, h, n, d = q.shape
            w = n // WINDOW
            bq = q.reshape(b, h, w, WINDOW, d) * QK_SCALE
            bk = k.reshape(b, h, w, WINDOW, d)
            bv = v.reshape(b, h, w, WINDOW, d)

            def look_around(t):
                p = jnp.pad(t, ((0, 0), (0, 0), (1, 0), (0, 0), (0, 0)))
                return jnp.concatenate([p[:, :, :w], p[:, :, 1:]], axis=3)
            bk, bv = (look_around(bk), look_around(bv))
            bt = jnp.arange(n).reshape(w, WINDOW)
            btp = jnp.pad(bt, ((1, 0), (0, 0)), constant_values=-1)
            btk = jnp.concatenate([btp[:w], btp[1:]], axis=1)
            sim = jnp.einsum('bhwid,bhwjd->bhwij', bq, bk)
            i = bt[:, :, None]
            j = btk[:, None, :]
            mask = (i < j) | (i > j + WINDOW) | (j == -1)
            sim = jnp.where(mask, -jnp.finfo(sim.dtype).max, sim)
            attn = jax.nn.softmax(sim, axis=-1)
            out = jnp.einsum('bhwij,bhwjd->bhwid', attn, bv)
            return out.reshape(b, h, n, d)

        def _layer(x, wqkv, qs, ksc, wo, lg, lb, w1, b1, w2, b2):
            b, n, _ = x.shape
            h = shift_token(x)
            qkv = h @ wqkv
            q, k, v = jnp.split(qkv, 3, axis=-1)
            to_heads = lambda t: t.reshape(b, n, HEADS, DIM_HEAD).transpose(0, 2, 1, 3)
            q, k, v = (to_heads(q), to_heads(k), to_heads(v))
            q = l2norm(q) * qs
            k = l2norm(k) * ksc
            q, k = rotary_xpos(q, k)
            o = local_attention(q, k, v)
            o = o.transpose(0, 2, 1, 3).reshape(b, n, INNER)
            x = x + o @ wo
            h = shift_token(x)
            mu = h.mean(-1, keepdims=True)
            var = h.var(-1, keepdims=True)
            h = (h - mu) / jnp.sqrt(var + 1e-05) * lg + lb
            h = h @ w1 + b1
            a, g = jnp.split(h, 2, axis=-1)
            h = a * jax.nn.gelu(g, approximate=False)
            x = x + h @ w2 + b2
            return x
        key = jax.random.key(seed)
        ks = jax.random.split(key, 6)
        return {'x': jax.random.normal(ks[0], (B, N, DIM), jnp.float32), 'wqkv': jax.random.normal(ks[1], (DEPTH, DIM, 3 * INNER), jnp.float32) * 0.02, 'q_scale': jnp.ones((DEPTH, DIM_HEAD), jnp.float32), 'k_scale': jnp.ones((DEPTH, DIM_HEAD), jnp.float32), 'wo': jax.random.normal(ks[2], (DEPTH, INNER, DIM), jnp.float32) * 0.02, 'ln_g': jnp.ones((DEPTH, DIM), jnp.float32), 'ln_b': jnp.zeros((DEPTH, DIM), jnp.float32), 'w1': jax.random.normal(ks[3], (DEPTH, DIM, 2 * HID), jnp.float32) * 0.02, 'b1': jnp.zeros((DEPTH, 2 * HID), jnp.float32), 'w2': jax.random.normal(ks[4], (DEPTH, HID, DIM), jnp.float32) * 0.02, 'b2': jnp.zeros((DEPTH, DIM), jnp.float32)}
    _L0_ffn_in = _L0_ffn_setup()
    _d = {'L0_attn_a_resid': _L0_attn_a_in['resid'], 'L0_attn_a_norm_w': _L0_attn_a_in['norm_w'], 'L0_attn_a_skip_w': _L0_attn_a_in['skip_w'], 'L0_attn_a_in_w': _L0_attn_a_in['in_w'], 'L0_attn_a_conv_w': _L0_attn_a_in['conv_w'], 'L0_attn_a_conv_b': _L0_attn_a_in['conv_b'], 'L0_attn_a_wd1': _L0_attn_a_in['wd1'], 'L0_attn_a_wd2': _L0_attn_a_in['wd2'], 'L0_attn_a_wd2_b': _L0_attn_a_in['wd2_b'], 'L0_attn_a_wb': _L0_attn_a_in['wb'], 'L0_attn_a_wc': _L0_attn_a_in['wc'], 'L0_attn_a_A_log': _L0_attn_a_in['A_log'], 'L0_attn_a_W_D': _L0_attn_a_in['W_D'], 'L0_attn_a_out_w': _L0_attn_a_in['out_w'], 'L0_attn_b_W': _L0_attn_b_in['W'], 'L0_ffn_wqkv': _L0_ffn_in['wqkv'], 'L0_ffn_q_scale': _L0_ffn_in['q_scale'], 'L0_ffn_k_scale': _L0_ffn_in['k_scale'], 'L0_ffn_wo': _L0_ffn_in['wo'], 'L0_ffn_ln_g': _L0_ffn_in['ln_g'], 'L0_ffn_ln_b': _L0_ffn_in['ln_b'], 'L0_ffn_w1': _L0_ffn_in['w1'], 'L0_ffn_b1': _L0_ffn_in['b1'], 'L0_ffn_w2': _L0_ffn_in['w2'], 'L0_ffn_b2': _L0_ffn_in['b2']}
    _x0 = _d['L0_attn_a_resid']
    _d['L0_attn_a_resid'] = jax.random.normal(jax.random.fold_in(jax.random.key(seed), 1), (16, 256, 128), dtype=_x0.dtype)
    del _x0
    return _d

def reference(L0_attn_a_resid, L0_attn_a_norm_w, L0_attn_a_skip_w, L0_attn_a_in_w, L0_attn_a_conv_w, L0_attn_a_conv_b, L0_attn_a_wd1, L0_attn_a_wd2, L0_attn_a_wd2_b, L0_attn_a_wb, L0_attn_a_wc, L0_attn_a_A_log, L0_attn_a_W_D, L0_attn_a_out_w, L0_attn_b_W, L0_ffn_wqkv, L0_ffn_q_scale, L0_ffn_k_scale, L0_ffn_wo, L0_ffn_ln_g, L0_ffn_ln_b, L0_ffn_w1, L0_ffn_b1, L0_ffn_w2, L0_ffn_b2):

    def _L0_attn_a_ref(resid, norm_w, skip_w, in_w, conv_w, conv_b, wd1, wd2, wd2_b, wb, wc, A_log, W_D, out_w):
        import jax, jax.numpy as jnp
        import numpy as np
        from jax import lax
        B, L, D = (2, 256, 128)
        E, N, D_DELTA, D_CONV = (256, 16, 64, 4)
        EPS = 1e-05
        Bt, Lt, Dt = resid.shape
        x = resid * lax.rsqrt(jnp.mean(resid * resid, -1, keepdims=True) + EPS) * norm_w
        skip = x @ skip_w.T
        xe = x @ in_w.T
        xt = xe.transpose(0, 2, 1)
        xc = lax.conv_general_dilated(xt, conv_w, window_strides=(1,), padding=[(D_CONV - 1, 0)], feature_group_count=conv_w.shape[0])
        xc = xc + conv_b[None, :, None]
        xs = jax.nn.silu(xc.transpose(0, 2, 1))
        delta = jax.nn.softplus(xs @ wd1.T @ wd2.T + wd2_b)
        A = -jnp.exp(A_log)
        Bm = xs @ wb.T
        Cm = xs @ wc.T

        def step(h, inp):
            d_l, b_l, c_l, x_l = inp
            h = jnp.exp(d_l[:, :, None] * A) * h + (d_l * x_l)[:, :, None] * b_l[:, None, :]
            y_l = jnp.einsum('ben,bn->be', h, c_l)
            return (h, y_l)
        h0 = jnp.zeros((Bt, xs.shape[-1], A.shape[-1]), xs.dtype)
        _, ys = lax.scan(step, h0, (delta.transpose(1, 0, 2), Bm.transpose(1, 0, 2), Cm.transpose(1, 0, 2), xs.transpose(1, 0, 2)))
        y = ys.transpose(1, 0, 2)
        y = y + xs * W_D
        y = y * jax.nn.silu(skip)
        y = y @ out_w.T
        return resid + y

    def _L0_attn_b_ref(x, W):
        import jax, jax.numpy as jnp
        import numpy as np
        import math
        N_HEAD = 16
        DEG = 2
        EPS = 1e-07
        B, T, C = x.shape
        nh = N_HEAD
        hs = C // nh
        scale = 1.0 / math.sqrt(hs)
        qkvgr = jnp.einsum('btc,oc->bto', x, W)
        q, k, v = (qkvgr[..., :C], qkvgr[..., C:2 * C], qkvgr[..., 2 * C:3 * C])
        log_g = jax.nn.log_sigmoid(qkvgr[..., 3 * C:].astype(jnp.float32))
        log_G = jnp.cumsum(log_g, axis=1).transpose(0, 2, 1)

        def heads(a):
            return a.reshape(B, T, nh, hs).transpose(0, 2, 1, 3)
        Q, K, V = (heads(q), heads(k), heads(v))
        S = jnp.einsum('bhtd,bhsd->bhts', Q, K)
        Tm = DEG * jnp.log(jnp.abs(S) + EPS) + jnp.log(jnp.float32(scale))
        Z = Tm + log_G[..., :, None] - log_G[..., None, :]
        mask = jnp.tril(jnp.ones((T, T), dtype=bool))
        Z = jnp.where(mask, Z, -jnp.inf)
        Z_rowmax = jax.lax.stop_gradient(jnp.max(Z, axis=-1, keepdims=True))
        P = jnp.exp(Z - Z_rowmax)
        norm = jnp.sum(P, axis=-1)
        O = jnp.einsum('bhts,bhsd->bhtd', P, V)
        y = O / norm[..., None]
        return y.transpose(0, 2, 1, 3).reshape(B, T, C)

    def _L0_ffn_ref(x, wqkv, q_scale, k_scale, wo, ln_g, ln_b, w1, b1, w2, b2):
        import jax, jax.numpy as jnp
        import numpy as np
        DIM = 128
        DEPTH = 2
        HEADS = 8
        DIM_HEAD = 64
        WINDOW = 64
        INNER = HEADS * DIM_HEAD
        HID = int(DIM * 4 * 2 / 3)
        B, N = (2, 1024)
        QK_SCALE = 8.0

        def shift_token(t):
            t1, t2 = jnp.split(t, 2, axis=-1)
            t2 = jnp.pad(t2, ((0, 0), (1, 0), (0, 0)))[:, :-1]
            return jnp.concatenate([t1, t2], axis=-1)

        def l2norm(t):
            return t / jnp.clip(jnp.linalg.norm(t, axis=-1, keepdims=True), 1e-12)

        def rotate_half(x):
            x1, x2 = jnp.split(x, 2, axis=-1)
            return jnp.concatenate([-x2, x1], axis=-1)

        def rotary_xpos(q, k):
            n = q.shape[-2]
            half_idx = jnp.arange(0, DIM_HEAD, 2, dtype=jnp.float32)
            inv_freq = 1.0 / 10000.0 ** (half_idx / DIM_HEAD)
            t = jnp.arange(n, dtype=jnp.float32)
            freqs = t[:, None] * inv_freq[None, :]
            freqs = jnp.concatenate([freqs, freqs], axis=-1)
            base = (half_idx + 0.4 * DIM_HEAD) / (1.4 * DIM_HEAD)
            power = (t - n // 2) / float(WINDOW // 2)
            scale = base[None, :] ** power[:, None]
            scale = jnp.concatenate([scale, scale], axis=-1)
            cos, sin = (jnp.cos(freqs), jnp.sin(freqs))
            q = q * cos * scale + rotate_half(q) * sin * scale
            k = k * cos / scale + rotate_half(k) * sin / scale
            return (q, k)

        def local_attention(q, k, v):
            b, h, n, d = q.shape
            w = n // WINDOW
            bq = q.reshape(b, h, w, WINDOW, d) * QK_SCALE
            bk = k.reshape(b, h, w, WINDOW, d)
            bv = v.reshape(b, h, w, WINDOW, d)

            def look_around(t):
                p = jnp.pad(t, ((0, 0), (0, 0), (1, 0), (0, 0), (0, 0)))
                return jnp.concatenate([p[:, :, :w], p[:, :, 1:]], axis=3)
            bk, bv = (look_around(bk), look_around(bv))
            bt = jnp.arange(n).reshape(w, WINDOW)
            btp = jnp.pad(bt, ((1, 0), (0, 0)), constant_values=-1)
            btk = jnp.concatenate([btp[:w], btp[1:]], axis=1)
            sim = jnp.einsum('bhwid,bhwjd->bhwij', bq, bk)
            i = bt[:, :, None]
            j = btk[:, None, :]
            mask = (i < j) | (i > j + WINDOW) | (j == -1)
            sim = jnp.where(mask, -jnp.finfo(sim.dtype).max, sim)
            attn = jax.nn.softmax(sim, axis=-1)
            out = jnp.einsum('bhwij,bhwjd->bhwid', attn, bv)
            return out.reshape(b, h, n, d)

        def _layer(x, wqkv, qs, ksc, wo, lg, lb, w1, b1, w2, b2):
            b, n, _ = x.shape
            h = shift_token(x)
            qkv = h @ wqkv
            q, k, v = jnp.split(qkv, 3, axis=-1)
            to_heads = lambda t: t.reshape(b, n, HEADS, DIM_HEAD).transpose(0, 2, 1, 3)
            q, k, v = (to_heads(q), to_heads(k), to_heads(v))
            q = l2norm(q) * qs
            k = l2norm(k) * ksc
            q, k = rotary_xpos(q, k)
            o = local_attention(q, k, v)
            o = o.transpose(0, 2, 1, 3).reshape(b, n, INNER)
            x = x + o @ wo
            h = shift_token(x)
            mu = h.mean(-1, keepdims=True)
            var = h.var(-1, keepdims=True)
            h = (h - mu) / jnp.sqrt(var + 1e-05) * lg + lb
            h = h @ w1 + b1
            a, g = jnp.split(h, 2, axis=-1)
            h = a * jax.nn.gelu(g, approximate=False)
            x = x + h @ w2 + b2
            return x
        for l in range(DEPTH):
            x = _layer(x, wqkv[l], q_scale[l], k_scale[l], wo[l], ln_g[l], ln_b[l], w1[l], b1[l], w2[l], b2[l])
        return x
    x = L0_attn_a_resid
    x = x + _L0_attn_a_ref(_layernorm(x, axis=-1), L0_attn_a_norm_w, L0_attn_a_skip_w, L0_attn_a_in_w, L0_attn_a_conv_w, L0_attn_a_conv_b, L0_attn_a_wd1, L0_attn_a_wd2, L0_attn_a_wd2_b, L0_attn_a_wb, L0_attn_a_wc, L0_attn_a_A_log, L0_attn_a_W_D, L0_attn_a_out_w)
    x = x + _L0_ffn_ref(_layernorm(x, axis=-1), L0_ffn_wqkv, L0_ffn_q_scale, L0_ffn_k_scale, L0_ffn_wo, L0_ffn_ln_g, L0_ffn_ln_b, L0_ffn_w1, L0_ffn_b1, L0_ffn_w2, L0_ffn_b2)
    x = x + _L0_attn_b_ref(_layernorm(x, axis=-1), L0_attn_b_W)
    x = x + _L0_ffn_ref(_layernorm(x, axis=-1), L0_ffn_wqkv, L0_ffn_q_scale, L0_ffn_k_scale, L0_ffn_wo, L0_ffn_ln_g, L0_ffn_ln_b, L0_ffn_w1, L0_ffn_b1, L0_ffn_w2, L0_ffn_b2)
    return x

_drawn_inputs = setup_inputs


def setup_inputs(seed=0):
    import zlib

    import numpy as np

    out = dict(_drawn_inputs(seed))
    spreads = {'L0_attn_a_norm_w': (1.0, 0.2),
     'L0_attn_a_conv_b': (0.0, 0.1),
     'L0_attn_a_wd2_b': (0.0, 0.475),
     'L0_attn_a_W_D': (1.0, 0.2),
     'L0_ffn_q_scale': (1.0, 0.6),
     'L0_ffn_k_scale': (1.0, 0.6),
     'L0_ffn_ln_g': (1.0, 0.6),
     'L0_ffn_ln_b': (0.0, 0.8),
     'L0_ffn_b1': (0.0, 0.8),
     'L0_ffn_b2': (0.0, 0.1)}
    factors = {'L0_ffn_wqkv': 2.895, 'L0_ffn_wo': 2.914, 'L0_ffn_w1': 5.449, 'L0_ffn_w2': 5.371}
    for name, (base, spread) in spreads.items():
        noise = np.random.default_rng([zlib.crc32(name.encode()), seed]).standard_normal(out[name].shape)
        drawn = base * np.exp(spread * noise) if base else spread * noise
        out[name] = jnp.asarray(drawn.astype(out[name].dtype))
    for name, factor in factors.items():
        out[name] = (out[name] * factor).astype(out[name].dtype)
    return out
```

```python
from contextlib import ExitStack

import concourse.bass as bass
from concourse import mybir

P = 128
F32 = mybir.dt.float32
BF16 = mybir.dt.bfloat16
ALU = mybir.AluOpType
ACT = mybir.ActivationFunctionType
AX = mybir.AxisListType

NSEQ, L, D = 16, 256, 128
T = L // P
E, NS, DD, CONV = 256, 16, 64, 4
EC = E // P
GN = 2
NG = NS // GN
H, DH, W = 8, 64, 64
INNER = H * DH
HID = int(D * 4 * 2 / 3)
HC = (HID + P - 1) // P
HR = [min(P, HID - c * P) for c in range(HC)]
PH, PS = 16, 8
PG = PH // 4
LN_EPS = 1e-5
AHEAD = 2
PHASES = 4


class Stream:

    def __init__(self, sem, steps):
        self.sem, self.steps = sem, steps
        self.index = {s: n for n, s in enumerate(steps)}
        assert len(self.index) == len(steps)
        self.at = 0
        self.credit = AHEAD * len(steps)

    def __call__(self, i, step):
        return (i + (AHEAD - 1)) * len(self.steps) + (self.index[step] + 1)

    def all(self, i):
        return (i + AHEAD) * len(self.steps)

    def done(self, step):
        assert self.steps[self.at % len(self.steps)] == step, (self.steps[self.at % len(self.steps)], step)
        self.at += 1
        return self.sem, 1


def build(nc, ins, out):
    with ExitStack() as ctx:
        def sb(name, shape, dt=F32):
            return ctx.enter_context(nc.sbuf_tensor(name, shape, dt))

        m_ctx = ExitStack()

        def m_sb(name, shape, dt=F32):
            return m_ctx.enter_context(nc.sbuf_tensor(name, shape, dt))

        def sem(name):
            return ctx.enter_context(nc.semaphore(name))

        bank = [ctx.enter_context(nc.psum_tensor(f"bank{n}", [P, 512], F32)) for n in range(2)]
        pair = [ctx.enter_context(nc.psum_tensor(f"pair{n}", [P, 1024], F32)) for n in range(3)]

        X = sb("X", [P, NSEQ, L])
        Z = sb("Z", [P, NSEQ, L])
        ident = sb("ident", [P, P])
        identb = sb("identb", [P, P], BF16)
        sel = sb("sel", [96, 32, P], BF16)
        band = sb("band", [P, L], BF16)
        tri = sb("tri", [P, P], BF16)
        shift = sb("shift", [P, P])
        carry = sb("carry", [P, P])
        ones = sb("ones", [P, L])
        mhalf = sb("mhalf", [P, 2 * H])
        eps = sb("eps", [P, T])
        eps_sum = sb("eps_sum", [P, T])
        carrier = sb("carrier", [P, 1])
        lst = sb("lst", [P, T, 6])
        lmv = sb("lmv", [P, T, 2])
        lve = sb("lve", [P, T])
        lrs = sb("lrs", [P, T])

        loaded = sem("loaded")
        x_loaded = sem("x_loaded")
        const_set = sem("const_set")
        stored = sem("stored")

        consts = [(ident[:], "ident"), (identb[:], "identb"), (sel[:], "sel"), (band[:], "band"), (tri[:], "tri"),
                  (shift[:], "shift"), (carry[:], "carry")]

        mw = dict(
            in_w=sb("m_in_w", [P, E]), skip_w=sb("m_skip_w", [P, E]), wd1=sb("m_wd1", [P, EC, DD]),
            wbc=sb("m_wbc", [P, EC, 2 * NS]), wd2=sb("m_wd2", [DD, E]), out_w=sb("m_out_w", [P, EC, D]),
            norm_w=sb("m_norm_w", [P, 1]), conv_w=sb("m_conv_w", [P, EC, CONV]), conv_b=sb("m_conv_b", [P, EC]),
            wd2_b=sb("m_wd2_b", [P, EC]), A_log=sb("m_A_log", [P, EC, NS]), W_D=sb("m_W_D", [P, EC]))
        consts += [(t[:], "m_" + n) for n, t in mw.items()]
        m_A = sb("m_A", [P, EC, NS])
        m_pad = sb("m_pad", [P, EC, CONV - 1 + L])
        m_a = sb("m_a", [P, 2, GN, EC, L])

        grp = range(NG)
        pe_mp = Stream(sem("pe_mp"), ["xT", "xe", "skip", "u", "bc", "z"])
        act_mp = Stream(sem("act_mp"), ["sq", "xT", "xe", "gate", "xs", "abs", "exp", "ln"])
        dve_mp = Stream(sem("dve_mp"), ["xr", "c0", "c1", "c2", "c3", "u", "hi", "r1", "mid", "mid2", "lo",
                                        "pos", "delta"])
        pool_mp = Stream(sem("pool_mp"), ["me", "rr", "xx", "dx"])
        pe_mh = Stream(sem("pe_mh"), [f"{s}{g}" for g in grp for s in ("bc", "y")] + ["out"])
        act_mh = Stream(sem("act_mh"), [f"{s}{g}" for g in grp for s in ("a", "c")])
        dve_mh = Stream(sem("dve_mh"), [f"{s}{g}" for g in grp for s in ("bx", "h")] + ["y", "yg", "x"])
        pool_mh = Stream(sem("pool_mh"), [f"hc{g}" for g in grp])

        dve_ln = Stream(sem("dve_ln"), ["st", "mv", "z"])
        pool_ln = Stream(sem("pool_ln"), ["ve", "rs"])

        fw = dict(
            wqkv=sb("f_wqkv", [P, 3 * INNER]), wo=sb("f_wo", [P, INNER // P, D]), w1=sb("f_w1", [P, 2 * HID]),
            w2=sb("f_w2", [P, HC, D]), b2=sb("f_b2", [P, D]), qs=sb("f_qs", [P, 2, DH]), lg=sb("f_lg", [P, 1]),
            lb=sb("f_lb", [P, 1]), b1=sb("f_b1", [P, 2, HC]))
        rot = sb("rot", [P, T, 2, 2, DH])
        consts += [(rot[:], "rot")]
        f_tab = sb("f_tab", [P, T, 2, 2, DH])
        f_hT = sb("f_hT", [P, L])
        f_v = sb("f_v", [P, T, H, DH + 1])
        f_p = sb("f_p", [P, T, 4, L])

        parts = [(t, g) for t in range(T) for g in range(2)]
        pe_f = Stream(sem("pe_f"), ["xT"] + [f"{s}{t}" for t in range(T) for s in ("qkv", "qkT")]
                      + [f"{s}{t}{g}" for t, g in parts for s in ("s", "pT", "o")]
                      + ["oT0", "oT1", "wo", "sh", "hnT", "w1", "w2"])
        act_f = Stream(sem("act_f"), [f"{s}{t}" for t in range(T) for s in ("sq", "v", "qkT")]
                       + [f"{s}{t}{g}" for t, g in parts for s in ("p", "pT")] + ["oT0", "oT1", "hb", "hnT", "g"])
        dve_f = Stream(sem("dve_f"), ["zc", "hT"] + [f"{s}{t}" for t in range(T) for s in ("ss", "qa", "cl", "qb")]
                       + [f"{s}{t}{g}" for t, g in parts for s in ("nm", "rs", "o")]
                       + ["z1", "st", "mv", "hn", "u", "z2"])
        pool_f = Stream(sem("pool_f"), [f"{s}{t}" for t in range(T) for s in ("rn", "add", "qk")]
                        + ["ve", "rv", "zb"])
        f_loaded = sem("f_loaded")
        f_table = sem("f_table")
        x_done = sem("x_done")

        pw = dict(wqk=sb("p_wqk", [P, 2, PG, P]), wv=sb("p_wv", [P, D]), wg=sb("p_wg", [P, PH]))
        consts += [(t[:], "p_" + n) for n, t in pw.items()]
        p_v = sb("p_v", [P, T, PH, PS + 1])
        p_g3 = sb("p_g3", [96, L], BF16)
        m_sq = m_sb("m_sq", [P, T, P])
        m_ss = m_sb("m_ss", [P, T])
        m_rr = m_sb("m_rr", [P, T])
        m_xr = m_sb("m_xr", [P, T, P])
        m_xT = m_sb("m_xT", [P, L])
        m_xc = m_sb("m_xc", [P, 2, EC, L])
        m_xs = m_sb("m_xs", [P, 2, EC, L])
        m_gate = m_sb("m_gate", [P, 2, EC, L])
        m_u = m_sb("m_u", [DD, L])
        m_r = m_sb("m_r", [32, 2, L])
        m_mid = m_sb("m_mid", [32, L], BF16)
        m_bc = m_sb("m_bc", [96, 2, L], BF16)
        m_t = m_sb("m_t", [P, 3, EC, L])
        m_pos = m_sb("m_pos", [P, EC, L])
        m_delta = m_sb("m_delta", [P, 2, EC, L])
        m_dx = m_sb("m_dx", [P, 2, EC, L])
        m_xx = m_sb("m_xx", [P, 2, L])
        m_bx = m_sb("m_bx", [P, 2, GN, EC, L])
        m_h = m_sb("m_h", [P, 2, GN, EC, L])
        m_c = m_sb("m_c", [P, 2, GN, L])
        m_hc = m_sb("m_hc", [P, 2, GN, EC, L])
        m_y = m_sb("m_y", [P, EC, L])
        m_yg = m_sb("m_yg", [P, EC, L])
        m_ctx.close()
        f_zc = sb("f_zc", [P, L])
        f_z1 = sb("f_z1", [P, L])
        f_sq = sb("f_sq", [P, 2 * INNER])
        f_ss = sb("f_ss", [P, 2 * H])
        f_cs = sb("f_cs", [P, 2 * H])
        f_rn = sb("f_rn", [P, 2 * H])
        f_qa = sb("f_qa", [P, 2, 2 * H, DH])
        f_qb = sb("f_qb", [P, 2, 2 * H, DH])
        f_qkT = sb("f_qkT", [P, H, L])
        f_nm = sb("f_nm", [P, 2, 4])
        f_pT = sb("f_pT", [P, 2, 8, P])
        f_rs = sb("f_rs", [P, 4])
        f_o = sb("f_o", [P, T, H, DH])
        f_oT = sb("f_oT", [P, INNER // P, L])
        f_hb = sb("f_hb", [P, T, P])
        f_st = sb("f_st", [P, T, 6])
        f_mv = sb("f_mv", [P, T, 2])
        f_ve = sb("f_ve", [P, T])
        f_rv = sb("f_rv", [P, T])
        f_hn = sb("f_hn", [P, T, P])
        f_hnT = sb("f_hnT", [P, L])
        f_g = sb("f_g", [P, HC, L])
        f_u = sb("f_u", [P, HC, L])
        f_zb = sb("f_zb", [P, L])
        p_zc = sb("p_zc", [P, L])
        p_xT = sb("p_xT", [P, L])
        p_qT = sb("p_qT", [P, PG, L])
        p_kT = sb("p_kT", [P, PG, L])
        p_t = sb("p_t", [PH, 5, L])
        p_hg = sb("p_hg", [PH, L])
        p_hgT = sb("p_hgT", [P, T, PH])
        p_mid = sb("p_mid", [PH, L], BF16)
        p_e = sb("p_e", [P, 4, L])
        p_a = sb("p_a", [P, 4, L])
        p_s = sb("p_s", [P, 4, L])
        p_m = sb("p_m", [P, 4])
        p_rm = sb("p_rm", [P, 4])
        p_p = sb("p_p", [P, 4, L])
        p_pT = sb("p_pT", [P, 8, P])
        p_rn = sb("p_rn", [P, T, PH])
        p_y = sb("p_y", [P, T, PH, PS])
        pparts = [(t, g) for t in range(T) for g in range(PG)]
        pe_p = Stream(sem("pe_p"), ["xT", "g", "q", "k", "v", "hgT"]
                      + [f"{s}{t}{g}" for t, g in pparts for s in ("bc", "s", "pT", "o")])
        act_p = Stream(sem("act_p"), ["xT", "abs", "exp", "ln", "q"]
                       + [f"{s}{t}{g}" for t, g in pparts for s in ("e", "abs", "p", "pT")])
        dve_p = Stream(sem("dve_p"), ["zc", "min", "lg", "cum", "hg", "hi", "r1", "mid", "mid2", "lo", "k", "v", "hgT"]
                       + [f"{s}{t}{g}" for t, g in pparts for s in ("u", "m", "rm")] + ["rn", "y", "x"])

        def credit(eng, *streams):
            for s in streams:
                eng.sem_inc(s.sem, s.credit)

        def half(t, k):
            return t[:, 512 * k:512 * k + 512]

        m_xe_ps = half(pair[0], 0).rearrange("p (c l) -> p c l", c=EC)
        m_sk_ps = half(pair[0], 1).rearrange("p (c l) -> p c l", c=EC)
        m_xT_ps = bank[0][:, 0:L]
        m_u_ps = bank[0][0:DD, 0:L]
        m_bc_ps = bank[0][0:2 * NS, L:2 * L]
        m_y_ps = bank[1][:].rearrange("p (c l) -> p c l", c=EC)

        def m_bcast(g, k):
            return half(pair[1 + g % 2], k).rearrange("p (n l) -> p n l", n=GN)

        def seq(t, i):
            return t[:, i - 1, :]

        def tiles(ap):
            return ap.rearrange("p (t d) -> p t d", t=T)

        def m_pe_prefix(pe, i, b):
            pe.wait_ge(dve_mp.sem, dve_mp(i, "xr"))
            pe.wait_ge(dve_mp.sem, dve_mp.all(i - 1))
            for t in range(T):
                ins_ = nc.tensor.transpose(m_xT_ps[:, t * P:t * P + P], m_xr[:, t, :], ident[:])
            ins_.then_inc(*pe_mp.done("xT"))
            pe.wait_ge(act_mp.sem, act_mp(i, "xT"))
            for c in range(EC):
                ins_ = nc.tensor.matmul(m_xe_ps[:, c, :], mw["in_w"][:, c * P:c * P + P], m_xT[:], start=True, stop=True)
            ins_.then_inc(*pe_mp.done("xe"))
            for c in range(EC):
                ins_ = nc.tensor.matmul(m_sk_ps[:, c, :], mw["skip_w"][:, c * P:c * P + P], m_xT[:], start=True, stop=True)
            ins_.then_inc(*pe_mp.done("skip"))
            pe.wait_ge(act_mp.sem, act_mp(i, "xs"))
            for c in range(EC):
                ins_ = nc.tensor.matmul(m_u_ps, mw["wd1"][:, c, :], m_xs[:, b, c, :], start=c == 0, stop=c == EC - 1)
            ins_.then_inc(*pe_mp.done("u"))
            for c in range(EC):
                ins_ = nc.tensor.matmul(m_bc_ps, mw["wbc"][:, c, :], m_xs[:, b, c, :], start=c == 0, stop=c == EC - 1)
            ins_.then_inc(*pe_mp.done("bc"))
            pe.wait_ge(dve_mp.sem, dve_mp(i, "u"))
            for c in range(EC):
                ins_ = nc.tensor.matmul(m_xe_ps[:, c, :], mw["wd2"][:, c * P:c * P + P], m_u[:], start=True, stop=True)
            ins_.then_inc(*pe_mp.done("z"))

        def m_act_prefix(act, i, b):
            for t in range(T):
                if t == 0:
                    act.wait_ge(dve_mp.sem, dve_mp.all(i - 1))
                    act.wait_ge(pool_mp.sem, pool_mp.all(i - 1))
                ins_ = nc.scalar.activation(m_sq[:, t, :], tiles(seq(Z, i))[:, t, :], ACT.Square, accum_out=m_ss[:, t:t + 1])
            ins_.then_inc(*act_mp.done("sq"))
            act.wait_ge(pe_mp.sem, pe_mp(i, "xT"))
            nc.scalar.activation(m_xT[:], m_xT_ps, ACT.Copy, scale=mw["norm_w"][:]).then_inc(*act_mp.done("xT"))
            act.wait_ge(pe_mp.sem, pe_mp(i, "xe"))
            nc.scalar.activation(m_pad[:, :, CONV - 1:], m_xe_ps, ACT.Copy).then_inc(*act_mp.done("xe"))
            act.wait_ge(pe_mp.sem, pe_mp(i, "skip"))
            act.wait_ge(dve_mh.sem, dve_mh.all(i - 2))
            nc.scalar.activation(m_gate[:, b], m_sk_ps, ACT.Silu).then_inc(*act_mp.done("gate"))
            act.wait_ge(dve_mp.sem, dve_mp(i, "c3"))
            nc.scalar.activation(m_xs[:, b], m_xc[:, 1], ACT.Silu).then_inc(*act_mp.done("xs"))
            act.wait_ge(pe_mp.sem, pe_mp(i, "z"))
            for c in range(EC):
                ins_ = nc.scalar.activation(m_t[:, 0, c, :], m_xe_ps[:, c, :], ACT.Abs, bias=mw["wd2_b"][:, c:c + 1])
            ins_.then_inc(*act_mp.done("abs"))
            act.wait_ge(act_mp.sem, act_mp(i, "abs"))
            nc.scalar.activation(m_t[:, 1], m_t[:, 0], ACT.Exp, scale=-1.0).then_inc(*act_mp.done("exp"))
            act.wait_ge(act_mp.sem, act_mp(i, "exp"))
            nc.scalar.activation(m_t[:, 2], m_t[:, 1], ACT.Ln, bias=ones[:, 0:1]).then_inc(*act_mp.done("ln"))

        def m_dve_prefix(dve, i, b):
            dve.wait_ge(pool_mp.sem, pool_mp(i, "rr"))
            for t in range(T):
                ins_ = nc.vector.tensor_scalar(m_xr[:, t, :], tiles(seq(Z, i))[:, t, :], m_rr[:, t:t + 1], float(D) ** 0.5,
                                               ALU.mult, ALU.mult)
            ins_.then_inc(*dve_mp.done("xr"))
            dve.wait_ge(act_mp.sem, act_mp(i, "xe"))
            for k in range(CONV):
                if k:
                    dve.wait_ge(dve_mp.sem, dve_mp(i, f"c{k - 1}"))
                for c in range(EC):
                    tap, x = mw["conv_w"][:, c, k:k + 1], m_pad[:, c, k:k + L]
                    if k == 0:
                        ins_ = nc.vector.tensor_scalar(m_xc[:, 0, c, :], x, tap, mw["conv_b"][:, c:c + 1], ALU.mult, ALU.add)
                    else:
                        ins_ = nc.vector.scalar_tensor_tensor(out=m_xc[:, k % 2, c, :], in0=x, scalar=tap,
                                                              in1=m_xc[:, (k + 1) % 2, c, :], op0=ALU.mult, op1=ALU.add)
                ins_.then_inc(*dve_mp.done(f"c{k}"))
            dve.wait_ge(pe_mp.sem, pe_mp(i, "bc"))
            nc.vector.tensor_copy(m_u[:], m_u_ps).then_inc(*dve_mp.done("u"))
            dve.wait_ge(pe_mh.sem, pe_mh.all(i - 2))
            nc.vector.tensor_copy(m_bc[0:32, b], m_bc_ps).then_inc(*dve_mp.done("hi"))
            dve.wait_ge(dve_mp.sem, dve_mp(i, "hi"))
            nc.vector.tensor_tensor(m_r[:, 0], m_bc_ps, m_bc[0:32, b], ALU.subtract).then_inc(*dve_mp.done("r1"))
            dve.wait_ge(dve_mp.sem, dve_mp(i, "r1"))
            nc.vector.tensor_copy(m_mid[:], m_r[:, 0]).then_inc(*dve_mp.done("mid"))
            nc.vector.tensor_copy(m_bc[32:64, b], m_r[:, 0]).then_inc(*dve_mp.done("mid2"))
            dve.wait_ge(dve_mp.sem, dve_mp(i, "mid"))
            nc.vector.tensor_tensor(m_bc[64:96, b], m_r[:, 0], m_mid[:], ALU.subtract).then_inc(*dve_mp.done("lo"))
            dve.wait_ge(act_mp.sem, act_mp(i, "abs"))
            for c in range(EC):
                ins_ = nc.vector.tensor_scalar(m_pos[:, c, :], m_xe_ps[:, c, :], mw["wd2_b"][:, c:c + 1], 0.0, ALU.add, ALU.max)
            ins_.then_inc(*dve_mp.done("pos"))
            dve.wait_ge(dve_mp.sem, dve_mp(i, "pos"))
            dve.wait_ge(act_mp.sem, act_mp(i, "ln"))
            dve.wait_ge(act_mh.sem, act_mh.all(i - 2))
            nc.vector.tensor_tensor(m_delta[:, b], m_pos[:], m_t[:, 2], ALU.add).then_inc(*dve_mp.done("delta"))

        def m_pool_prefix(pool, i, b):
            pool.wait_ge(act_mp.sem, act_mp(i, "sq"))
            nc.gpsimd.tensor_tensor(m_rr[:], m_ss[:], eps_sum[:], ALU.add).then_inc(*pool_mp.done("me"))
            pool.wait_ge(pool_mp.sem, pool_mp(i, "me"))
            nc.gpsimd.tensor_tensor(m_rr[:], m_rr[:], mhalf[:, 0:T], ALU.pow).then_inc(*pool_mp.done("rr"))
            pool.wait_ge(dve_mh.sem, dve_mh.all(i - 2))
            nc.gpsimd.tensor_tensor(m_xx[:, b], seq(X, i), seq(Z, i), ALU.add).then_inc(*pool_mp.done("xx"))
            pool.wait_ge(dve_mp.sem, dve_mp(i, "delta"))
            nc.gpsimd.tensor_tensor(m_dx[:, b], m_delta[:, b], m_xs[:, b], ALU.mult).then_inc(*pool_mp.done("dx"))

        def m_pe_heavy(pe, i, b, g):
            def sum_states(g):
                pe.wait_ge(pool_mh.sem, pool_mh(i, f"hc{g}"))
                if g == 0:
                    pe.wait_ge(dve_mh.sem, dve_mh.all(i - 1))
                for n in range(GN):
                    ins_ = nc.tensor.matmul(bank[1][:], ident[:], m_hc[:, g % 2, n].rearrange("p c l -> p (c l)"),
                                            start=g == 0 and n == 0, stop=g == NG - 1 and n == GN - 1)
                ins_.then_inc(*pe_mh.done(f"y{g}"))

            if g == 0:
                pe.wait_ge(dve_mp.sem, dve_mp(i, "lo"))
            pe.wait_ge(dve_mh.sem, dve_mh(i, f"bx{g - 2}") if g >= 2 else dve_mh(i - 1, f"bx{NG - 2 + g}"))
            pe.wait_ge(act_mh.sem, act_mh(i, f"c{g - 2}") if g >= 2 else act_mh(i - 1, f"c{NG - 2 + g}"))
            for k in range(2):
                for n in range(GN):
                    ins_ = nc.tensor.matmul(m_bcast(g, k)[:, n, :], sel[:, k * NS + g * GN + n, :], m_bc[:, b, :],
                                            start=True, stop=True)
            ins_.then_inc(*pe_mh.done(f"bc{g}"))
            sum_states(g)
            if g == NG - 1:
                pe.wait_ge(dve_mh.sem, dve_mh(i, "yg"))
                for t in range(T):
                    for c in range(EC):
                        ins_ = nc.tensor.matmul(bank[1][:, t * P:t * P + P], m_yg[:, c, t * P:t * P + P],
                                                mw["out_w"][:, c, :], start=c == 0, stop=c == EC - 1)
                ins_.then_inc(*pe_mh.done("out"))

        def m_act_heavy(act, i, b, g):
            if g == 0:
                act.wait_ge(dve_mp.sem, dve_mp(i, "delta"))
            act.wait_ge(dve_mh.sem, dve_mh(i, f"h{g - 2}") if g >= 2 else dve_mh(i - 1, f"h{NG - 2 + g}"))
            for n in range(GN):
                for c in range(EC):
                    ins_ = nc.scalar.activation(m_a[:, g % 2, n, c, 1:L], m_delta[:, b, c, 1:L], ACT.Exp,
                                                scale=m_A[:, c, g * GN + n:g * GN + n + 1])
            ins_.then_inc(*act_mh.done(f"a{g}"))
            act.wait_ge(pe_mh.sem, pe_mh(i, f"bc{g}"))
            act.wait_ge(pool_mh.sem, pool_mh(i, f"hc{g - 2}") if g >= 2 else pool_mh(i - 1, f"hc{NG - 2 + g}"))
            nc.scalar.activation(m_c[:, g % 2], m_bcast(g, 1), ACT.Copy).then_inc(*act_mh.done(f"c{g}"))

        def m_dve_heavy(dve, i, b, g):
            if g == 0:
                dve.wait_ge(pool_mp.sem, pool_mp(i, "dx"))
            dve.wait_ge(pe_mh.sem, pe_mh(i, f"bc{g}"))
            nc.vector.tensor_tensor(m_bx[:, g % 2],
                                    m_dx[:, b].unsqueeze(1).broadcast_to([P, GN, EC, L]),
                                    m_bcast(g, 0).unsqueeze(2).broadcast_to([P, GN, EC, L]),
                                    ALU.mult).then_inc(*dve_mh.done(f"bx{g}"))
            dve.wait_ge(dve_mh.sem, dve_mh(i, f"bx{g}"))
            dve.wait_ge(act_mh.sem, act_mh(i, f"a{g}"))
            dve.wait_ge(pool_mh.sem, pool_mh(i, f"hc{g - 2}") if g >= 2 else pool_mh(i - 1, f"hc{NG - 2 + g}"))
            flat = "p n c l -> p (n c l)"
            nc.vector.tensor_tensor_scan(m_h[:, g % 2].rearrange(flat), m_a[:, g % 2].rearrange(flat),
                                         m_bx[:, g % 2].rearrange(flat), 0.0, ALU.mult,
                                         ALU.add).then_inc(*dve_mh.done(f"h{g}"))
            if g == NG - 1:
                dve.wait_ge(pe_mh.sem, pe_mh(i, f"y{g}"))
                for c in range(EC):
                    ins_ = nc.vector.scalar_tensor_tensor(out=m_y[:, c, :], in0=m_xs[:, b, c, :], scalar=mw["W_D"][:, c:c + 1],
                                                          in1=m_y_ps[:, c, :], op0=ALU.mult, op1=ALU.add)
                ins_.then_inc(*dve_mh.done("y"))
                dve.wait_ge(dve_mh.sem, dve_mh(i, "y"))
                nc.vector.tensor_tensor(m_yg[:], m_y[:], m_gate[:, b], ALU.mult).then_inc(*dve_mh.done("yg"))
                dve.wait_ge(pe_mh.sem, pe_mh(i, "out"))
                nc.vector.tensor_tensor(seq(X, i), m_xx[:, b], bank[1][:, 0:L], ALU.add).then_inc(*dve_mh.done("x"))

        def m_pool_heavy(pool, i, b, g):
            pool.wait_ge(dve_mh.sem, dve_mh(i, f"h{g}"))
            pool.wait_ge(act_mh.sem, act_mh(i, f"c{g}"))
            pool.wait_ge(pe_mh.sem, pe_mh(i, f"y{g - 2}") if g >= 2 else pe_mh(i - 1, f"y{NG - 2 + g}"))
            for n in range(GN):
                ins_ = nc.gpsimd.tensor_tensor(m_hc[:, g % 2, n], m_h[:, g % 2, n],
                                               m_c[:, g % 2, n].unsqueeze(1).broadcast_to([P, EC, L]), ALU.mult)
            ins_.then_inc(*pool_mh.done(f"hc{g}"))

        def ln_dve(dve, i, k, ready, n):
            j = k * NSEQ + i
            dve.wait_ge(*ready)
            for t in range(T):
                ins_ = nc.vector.bn_stats(lst[:, t, :], tiles(seq(X, i))[:, t, :])
            ins_.then_inc(*dve_ln.done("st"))
            dve.wait_ge(dve_ln.sem, dve_ln(j, "st"))
            dve.wait_ge(pool_ln.sem, pool_ln(j - 1, "ve"))
            nc.vector.tensor_copy(carrier[:], eps[:, 0:1])
            for t in range(T):
                ins_ = nc.vector.bn_aggr(lmv[:, t, :], lst[:, t, :])
            ins_.then_inc(*dve_ln.done("mv"))
            dve.wait_ge(pool_ln.sem, pool_ln(j, "rs"))
            for t in range(T):
                ins_ = nc.vector.tensor_scalar(tiles(seq(Z, i))[:, t, :], tiles(seq(X, i))[:, t, :], lmv[:, t, 0:1],
                                               lrs[:, t:t + 1], ALU.subtract, ALU.mult)
            ins_.then_inc(*dve_ln.done("z"))

        def ln_pool(pool, i, k):
            j = k * NSEQ + i
            pool.wait_ge(dve_ln.sem, dve_ln(j, "mv"))
            nc.gpsimd.tensor_tensor(lve[:], lmv[:, :, 1], eps[:], ALU.add).then_inc(*pool_ln.done("ve"))
            pool.wait_ge(pool_ln.sem, pool_ln(j, "ve"))
            nc.gpsimd.tensor_tensor(lrs[:], lve[:], mhalf[:, 0:T], ALU.pow).then_inc(*pool_ln.done("rs"))

        QK = pair[0][:].rearrange("p (x h d) -> p x h d", x=2, h=H)
        SC = pair[1][:].rearrange("p (j k) -> p j k", j=4)
        KEYS = [(0, P), (P - W, L)]

        def slot(h):
            return (h % 2) * 2 + (h // 2) % 2

        def f_pe(pe, i, loads):
            pe.wait_ge(dve_f.sem, dve_f(i, "zc"))
            pe.wait_ge(f_loaded, loads)
            for t in range(T):
                ins_ = nc.tensor.transpose(bank[0][:, t * P:t * P + P], tiles(f_zc[:])[:, t, :], ident[:])
            ins_.then_inc(*pe_f.done("xT"))
            pe.wait_ge(dve_f.sem, dve_f(i, "hT"))
            for t in range(T):
                if t:
                    pe.wait_ge(dve_f.sem, dve_f(i, f"qb{t - 1}"))
                    pe.wait_ge(act_f.sem, act_f(i, f"v{t - 1}"))
                else:
                    pe.wait_ge(dve_f.sem, dve_f.all(i - 1))
                for n in range(3):
                    o = half(pair[0], n) if n < 2 else half(pair[2], 0)
                    ins_ = nc.tensor.matmul(o, f_hT[:, t * P:t * P + P], fw["wqkv"][:, n * 512:n * 512 + 512],
                                            start=True, stop=True)
                ins_.then_inc(*pe_f.done(f"qkv{t}"))
                pe.wait_ge(pool_f.sem, pool_f(i, f"qk{t}"))
                if t:
                    pe.wait_ge(act_f.sem, act_f(i, f"qkT{t - 1}"))
                for c in range(8):
                    ins_ = nc.tensor.transpose(pair[1][:, c * P:c * P + P],
                                               f_qa[:, t, 2 * c:2 * c + 2, :].rearrange("p h d -> p (h d)"), ident[:])
                ins_.then_inc(*pe_f.done(f"qkT{t}"))
            for t in range(T):
                k0, k1 = KEYS[t]
                for g in range(2):
                    pe.wait_ge(act_f.sem, act_f(i, "qkT1") if (t, g) == (0, 0) else act_f(i, f"p{parts[2 * t + g - 1][0]}{parts[2 * t + g - 1][1]}"))
                    for h in range(4 * g, 4 * g + 4):
                        r = slice(DH * (h % 2), DH * (h % 2) + DH)
                        o = SC[:, slot(h), k0:k1]
                        nc.tensor.matmul(o, f_qkT[r, h // 2, t * P:t * P + P], f_qkT[r, 4 + h // 2, k0:k1],
                                         start=True, stop=False, skip_group_check=True)
                        m0 = k0 - t * P + P
                        ins_ = nc.tensor.matmul(o, identb[:], band[:, m0:m0 + k1 - k0], start=False, stop=True,
                                                skip_group_check=True)
                    ins_.then_inc(*pe_f.done(f"s{t}{g}"))
                    pe.wait_ge(act_f.sem, act_f(i, f"p{t}{g}"))
                    if (t, g) != (0, 0):
                        a, c = parts[2 * t + g - 1]
                        pe.wait_ge(act_f.sem, act_f(i, f"pT{a}{c}"))
                    for j in range(4):
                        for k in range(t + 1):
                            ins_ = nc.tensor.transpose(pair[0][:, (4 * k + j) * P:(4 * k + j) * P + P],
                                                       f_p[:, t, j, k * P:k * P + P], ident[:])
                    ins_.then_inc(*pe_f.done(f"pT{t}{g}"))
                    pe.wait_ge(act_f.sem, act_f(i, f"pT{t}{g}"))
                    if (t, g) != (0, 0):
                        a, c = parts[2 * t + g - 1]
                        pe.wait_ge(dve_f.sem, dve_f(i, f"o{a}{c}"))
                    for h in range(4 * g, 4 * g + 4):
                        o = half(pair[2], 1)[:, (h % 4) * (DH + 1):(h % 4 + 1) * (DH + 1)]
                        for k in range(t + 1):
                            ins_ = nc.tensor.matmul(o, f_pT[:, g, 4 * k + slot(h), :], f_v[:, k, h, :],
                                                    start=k == 0, stop=k == t)
                    ins_.then_inc(*pe_f.done(f"o{t}{g}"))
            for t in range(T):
                pe.wait_ge(dve_f.sem, dve_f(i, f"o{t}1"))
                if t:
                    pe.wait_ge(act_f.sem, act_f(i, "oT0"))
                for c in range(4):
                    ins_ = nc.tensor.transpose(bank[0][:, c * P:c * P + P],
                                               f_o[:, t, 2 * c:2 * c + 2, :].rearrange("p h d -> p (h d)"), ident[:])
                ins_.then_inc(*pe_f.done(f"oT{t}"))
            pe.wait_ge(act_f.sem, act_f(i, "oT1"))
            for t in range(T):
                for c in range(4):
                    ins_ = nc.tensor.matmul(bank[1][:, t * P:t * P + P], f_oT[:, c, t * P:t * P + P], fw["wo"][:, c, :],
                                            start=c == 0, stop=c == 3)
            ins_.then_inc(*pe_f.done("wo"))
            pe.wait_ge(dve_f.sem, dve_f(i, "z1"))
            zt = tiles(f_z1[:])
            nc.tensor.matmul(bank[1][:, 256:320], shift[:], zt[:, 0, 64:128], start=True, stop=True)
            nc.tensor.matmul(bank[1][:, 320:384], shift[:], zt[:, 1, 64:128], start=True, stop=False)
            nc.tensor.matmul(bank[1][:, 320:384], carry[:], zt[:, 0, 64:128], start=False,
                             stop=True).then_inc(*pe_f.done("sh"))
            pe.wait_ge(dve_f.sem, dve_f(i, "hn"))
            for t in range(T):
                ins_ = nc.tensor.transpose(bank[0][:, t * P:t * P + P], f_hn[:, t, :], ident[:])
            ins_.then_inc(*pe_f.done("hnT"))
            pe.wait_ge(act_f.sem, act_f(i, "hnT"))
            for x in range(2):
                for c in range(HC):
                    ins_ = nc.tensor.matmul(pair[x][0:HR[c], c * L:c * L + L],
                                            fw["w1"][:, x * HID + c * P:x * HID + c * P + HR[c]], f_hnT[:],
                                            start=True, stop=True)
            ins_.then_inc(*pe_f.done("w1"))
            pe.wait_ge(dve_f.sem, dve_f(i, "u"))
            for t in range(T):
                for c in range(HC):
                    ins_ = nc.tensor.matmul(bank[1][:, t * P:t * P + P], f_u[0:HR[c], c, t * P:t * P + P],
                                            fw["w2"][0:HR[c], c, :], start=c == 0, stop=c == HC - 1)
            ins_.then_inc(*pe_f.done("w2"))

        def f_act(act, i, loads):
            for t in range(T):
                act.wait_ge(pe_f.sem, pe_f(i, f"qkv{t}"))
                if t:
                    act.wait_ge(dve_f.sem, dve_f(i, f"ss{t - 1}"))
                nc.scalar.activation(f_sq[:], pair[0][:], ACT.Square).then_inc(*act_f.done(f"sq{t}"))
                nc.scalar.activation(f_v[:, t, :, 0:DH], half(pair[2], 0).rearrange("p (h d) -> p h d", h=H),
                                     ACT.Copy).then_inc(*act_f.done(f"v{t}"))
                act.wait_ge(pe_f.sem, pe_f(i, f"qkT{t}"))
                nc.scalar.activation(f_qkT[:, :, t * P:t * P + P], pair[1][:].rearrange("p (c k) -> p c k", c=8),
                                     ACT.Copy).then_inc(*act_f.done(f"qkT{t}"))
            for t in range(T):
                k0, k1 = KEYS[t]
                for g in range(2):
                    act.wait_ge(dve_f.sem, dve_f(i, f"nm{t}{g}"))
                    if g:
                        act.wait_ge(pe_f.sem, pe_f(i, f"pT{t}{0}"))
                    for j in range(4):
                        ins_ = nc.scalar.activation(f_p[:, t, j, k0:k1], SC[:, j, k0:k1], ACT.Exp,
                                                    bias=f_nm[:, g, j:j + 1])
                    ins_.then_inc(*act_f.done(f"p{t}{g}"))
                    act.wait_ge(pe_f.sem, pe_f(i, f"pT{t}{g}"))
                    if t:
                        act.wait_ge(pe_f.sem, pe_f(i, f"o{t - 1}{g}"))
                    n = 4 * (t + 1)
                    nc.scalar.activation(f_pT[:, g, 0:n, :], pair[0][:, 0:n * P].rearrange("p (c k) -> p c k", c=n),
                                         ACT.Copy).then_inc(*act_f.done(f"pT{t}{g}"))
            for t in range(T):
                act.wait_ge(pe_f.sem, pe_f(i, f"oT{t}"))
                nc.scalar.activation(f_oT[:, :, t * P:t * P + P], bank[0][:].rearrange("p (c k) -> p c k", c=4),
                                     ACT.Copy).then_inc(*act_f.done(f"oT{t}"))
            act.wait_ge(pe_f.sem, pe_f(i, "sh"))
            nc.scalar.activation(f_hb[:, :, 0:64], tiles(f_z1[:])[:, :, 0:64], ACT.Copy)
            nc.scalar.activation(f_hb[:, :, 64:128], bank[1][:, 256:384].rearrange("p (t d) -> p t d", t=T),
                                 ACT.Copy).then_inc(*act_f.done("hb"))
            act.wait_ge(pe_f.sem, pe_f(i, "hnT"))
            act.wait_ge(f_loaded, loads)
            nc.scalar.activation(f_hnT[:], bank[0][:, 0:L], ACT.Identity, bias=fw["lb"][:],
                                 scale=fw["lg"][:]).then_inc(*act_f.done("hnT"))
            act.wait_ge(pe_f.sem, pe_f(i, "w1"))
            for c in range(HC):
                ins_ = nc.scalar.activation(f_g[0:HR[c], c, :], pair[1][0:HR[c], c * L:c * L + L], ACT.Gelu,
                                            bias=fw["b1"][0:HR[c], 1, c:c + 1])
            ins_.then_inc(*act_f.done("g"))

        def f_dve(dve, i, f_i, zdone, tables):
            dve.wait_ge(dve_f.sem, dve_f.all(i - 1))
            dve.wait_ge(*zdone)
            dve.wait_ge(f_table, tables)
            nc.vector.tensor_scalar(f_zc[:], seq(Z, f_i), 1.0, None, ALU.mult).then_inc(*dve_f.done("zc"))
            dve.wait_ge(pe_f.sem, pe_f(i, "xT"))
            nc.vector.tensor_copy(f_hT[0:64, :], bank[0][0:64, 0:L])
            nc.vector.tensor_copy(f_hT[64:128, 1:L], bank[0][64:128, 0:L - 1]).then_inc(*dve_f.done("hT"))
            for t in range(T):
                dve.wait_ge(act_f.sem, act_f(i, f"sq{t}"))
                nc.vector.tensor_reduce(f_ss[:], f_sq[:].rearrange("p (h d) -> p h d", h=2 * H), AX.X,
                                        ALU.add).then_inc(*dve_f.done(f"ss{t}"))
                for x in range(2):
                    ins_ = nc.vector.tensor_tensor(f_qa[:, t, x * H:x * H + H, :], QK[:, x],
                                                   f_tab[:, t, x, 0].unsqueeze(1).broadcast_to([P, H, DH]), ALU.mult)
                ins_.then_inc(*dve_f.done(f"qa{t}"))
                dve.wait_ge(dve_f.sem, dve_f(i, f"ss{t}"))
                dve.wait_ge(pool_f.sem, pool_f(i, f"rn{t - 1}") if t else pool_f.all(i - 1))
                nc.vector.tensor_scalar(f_cs[:], f_ss[:], 1e-24, None, ALU.max).then_inc(*dve_f.done(f"cl{t}"))
                for x in range(2):
                    for e in range(2):
                        ins_ = nc.vector.tensor_tensor(
                            f_qb[:, t, x * H:x * H + H, 32 * e:32 * e + 32], QK[:, x, :, 32 - 32 * e:64 - 32 * e],
                            f_tab[:, t, x, 1, 32 * e:32 * e + 32].unsqueeze(1).broadcast_to([P, H, 32]), ALU.mult)
                ins_.then_inc(*dve_f.done(f"qb{t}"))
            for t in range(T):
                k0, k1 = KEYS[t]
                for g in range(2):
                    dve.wait_ge(pe_f.sem, pe_f(i, f"s{t}{g}"))
                    if t:
                        dve.wait_ge(act_f.sem, act_f(i, f"p0{g}"))
                    nc.vector.tensor_reduce(f_nm[:, g, :], SC[:, :, k0:k1], AX.X, ALU.max,
                                            negate=True).then_inc(*dve_f.done(f"nm{t}{g}"))
                    dve.wait_ge(pe_f.sem, pe_f(i, f"o{t}{g}"))
                    o = half(pair[2], 1)[:, 0:4 * (DH + 1)].rearrange("p (h d) -> p h d", h=4)
                    nc.vector.reciprocal(f_rs[:], o[:, :, DH]).then_inc(*dve_f.done(f"rs{t}{g}"))
                    dve.wait_ge(dve_f.sem, dve_f(i, f"rs{t}{g}"))
                    nc.vector.tensor_tensor(f_o[:, t, 4 * g:4 * g + 4, :], o[:, :, 0:DH],
                                            f_rs[:].unsqueeze(2).broadcast_to([P, 4, DH]),
                                            ALU.mult).then_inc(*dve_f.done(f"o{t}{g}"))
            dve.wait_ge(pe_f.sem, pe_f(i, "wo"))
            nc.vector.tensor_tensor(f_z1[:], f_zc[:], bank[1][:, 0:L], ALU.add).then_inc(*dve_f.done("z1"))
            dve.wait_ge(act_f.sem, act_f(i, "hb"))
            for t in range(T):
                ins_ = nc.vector.bn_stats(f_st[:, t, :], f_hb[:, t, :])
            ins_.then_inc(*dve_f.done("st"))
            dve.wait_ge(dve_f.sem, dve_f(i, "st"))
            nc.vector.tensor_copy(carrier[:], eps[:, 0:1])
            for t in range(T):
                ins_ = nc.vector.bn_aggr(f_mv[:, t, :], f_st[:, t, :])
            ins_.then_inc(*dve_f.done("mv"))
            dve.wait_ge(pool_f.sem, pool_f(i, "rv"))
            for t in range(T):
                ins_ = nc.vector.tensor_scalar(f_hn[:, t, :], f_hb[:, t, :], f_mv[:, t, 0:1], f_rv[:, t:t + 1],
                                               ALU.subtract, ALU.mult)
            ins_.then_inc(*dve_f.done("hn"))
            dve.wait_ge(act_f.sem, act_f(i, "g"))
            for c in range(HC):
                r = HR[c]
                ins_ = nc.vector.scalar_tensor_tensor(out=f_u[0:r, c, :], in0=pair[0][0:r, c * L:c * L + L],
                                                      scalar=fw["b1"][0:r, 0, c:c + 1], in1=f_g[0:r, c, :],
                                                      op0=ALU.add, op1=ALU.mult)
            ins_.then_inc(*dve_f.done("u"))
            dve.wait_ge(pe_f.sem, pe_f(i, "w2"))
            dve.wait_ge(pool_f.sem, pool_f(i, "zb"))
            nc.vector.tensor_tensor(seq(Z, f_i), f_zb[:], bank[1][:, 0:L], ALU.add).then_inc(*dve_f.done("z2"))

        def f_pool(pool, i, loads):
            for t in range(T):
                pool.wait_ge(dve_f.sem, dve_f(i, f"cl{t}"))
                nc.gpsimd.tensor_tensor(f_rn[:], f_cs[:], mhalf[:], ALU.pow).then_inc(*pool_f.done(f"rn{t}"))
                pool.wait_ge(dve_f.sem, dve_f(i, f"qb{t}"))
                nc.gpsimd.tensor_tensor(f_qb[:, t], f_qa[:, t], f_qb[:, t], ALU.add).then_inc(*pool_f.done(f"add{t}"))
                pool.wait_ge(pool_f.sem, pool_f(i, f"add{t}"))
                nc.gpsimd.tensor_tensor(f_qa[:, t], f_qb[:, t], f_rn[:].unsqueeze(2).broadcast_to([P, 2 * H, DH]),
                                        ALU.mult).then_inc(*pool_f.done(f"qk{t}"))
            pool.wait_ge(dve_f.sem, dve_f(i, "mv"))
            nc.gpsimd.tensor_tensor(f_ve[:], f_mv[:, :, 1], eps[:], ALU.add).then_inc(*pool_f.done("ve"))
            pool.wait_ge(pool_f.sem, pool_f(i, "ve"))
            pool.wait_ge(f_loaded, loads)
            nc.gpsimd.tensor_tensor(f_rv[:], f_ve[:], mhalf[:, 0:T], ALU.pow).then_inc(*pool_f.done("rv"))
            nc.gpsimd.tensor_tensor(tiles(f_zb[:]), tiles(f_z1[:]), fw["b2"][:].unsqueeze(1).broadcast_to([P, T, D]),
                                    ALU.add).then_inc(*pool_f.done("zb"))

        def p_head(g, j):
            return 4 * (2 * (g // 2) + j % 2) + 2 * (g % 2) + j // 2

        def p_pe(pe, i):
            pe.wait_ge(dve_p.sem, dve_p(i, "zc"))
            for t in range(T):
                ins_ = nc.tensor.transpose(bank[0][:, t * P:t * P + P], tiles(p_zc[:])[:, t, :], ident[:])
            ins_.then_inc(*pe_p.done("xT"))
            pe.wait_ge(act_p.sem, act_p(i, "xT"))
            nc.tensor.matmul(bank[1][0:PH, 0:L], pw["wg"][:], p_xT[:], start=True, stop=True).then_inc(*pe_p.done("g"))
            for x, s in ((0, "q"), (1, "k")):
                for g in range(PG):
                    ins_ = nc.tensor.matmul(pair[x][:, g * L:g * L + L], pw["wqk"][:, x, g, :], p_xT[:],
                                            start=True, stop=True)
                ins_.then_inc(*pe_p.done(s))
            for t in range(T):
                ins_ = nc.tensor.matmul(bank[0][:, t * P:t * P + P], p_xT[:, t * P:t * P + P], pw["wv"][:],
                                        start=True, stop=True)
            ins_.then_inc(*pe_p.done("v"))
            pe.wait_ge(dve_p.sem, dve_p(i, "v"))
            for t in range(T):
                ins_ = nc.tensor.matmul(bank[0][:, L + t * PH:L + t * PH + PH], p_hg[:, t * P:t * P + P],
                                        ident[0:PH, 0:PH], start=True, stop=True)
            ins_.then_inc(*pe_p.done("hgT"))
            for t in range(T):
                n = P * (t + 1)
                for g in range(PG):
                    first = (t, g) == (0, 0)
                    if not first:
                        a, c = pparts[PG * t + g - 1]
                    if first:
                        pe.wait_ge(act_p.sem, act_p(i, "q"))
                        pe.wait_ge(dve_p.sem, dve_p(i, "k"))
                        pe.wait_ge(dve_p.sem, dve_p(i, "lo"))
                    else:
                        pe.wait_ge(act_p.sem, act_p(i, f"e{a}{c}"))
                    for j in range(4):
                        o = pair[0][:, j * L:j * L + n]
                        nc.tensor.matmul(o, sel[:, p_head(g, j), :], p_g3[:, 0:n], start=True, stop=False,
                                         skip_group_check=True)
                        ins_ = nc.tensor.matmul(o[:, n - P:n], identb[:], tri[:], start=False, stop=True,
                                                skip_group_check=True)
                    ins_.then_inc(*pe_p.done(f"bc{t}{g}"))
                    if not first:
                        pe.wait_ge(act_p.sem, act_p(i, f"abs{a}{c}"))
                    for j in range(4):
                        h = p_head(g, j)
                        r0 = 32 * (h % 4)
                        ins_ = nc.tensor.matmul(pair[1][:, j * L:j * L + n], p_qT[r0:r0 + PS, h // 4, t * P:t * P + P],
                                                p_kT[r0:r0 + PS, h // 4, 0:n], start=True, stop=True,
                                                tile_position=(r0, 0))
                    ins_.then_inc(*pe_p.done(f"s{t}{g}"))
                    pe.wait_ge(act_p.sem, act_p(i, f"p{t}{g}"))
                    if not first:
                        pe.wait_ge(act_p.sem, act_p(i, f"pT{a}{c}"))
                    for j in range(4):
                        for k in range(t + 1):
                            ins_ = nc.tensor.transpose(pair[2][:, (4 * k + j) * P:(4 * k + j) * P + P],
                                                       p_p[:, j, k * P:k * P + P], ident[:])
                    ins_.then_inc(*pe_p.done(f"pT{t}{g}"))
                    pe.wait_ge(act_p.sem, act_p(i, f"pT{t}{g}"))
                    for j in range(4):
                        h = p_head(g, j)
                        for k in range(t + 1):
                            ins_ = nc.tensor.matmul(bank[1][:, (t * PH + h) * (PS + 1):(t * PH + h + 1) * (PS + 1)],
                                                    p_pT[:, 4 * k + j, :], p_v[:, k, h, :], start=k == 0, stop=k == t)
                    ins_.then_inc(*pe_p.done(f"o{t}{g}"))

        def p_act(act, i):
            act.wait_ge(pe_p.sem, pe_p(i, "xT"))
            nc.scalar.activation(p_xT[:], bank[0][:, 0:L], ACT.Copy).then_inc(*act_p.done("xT"))
            act.wait_ge(pe_p.sem, pe_p(i, "g"))
            nc.scalar.activation(p_t[:, 0], bank[1][0:PH, 0:L], ACT.Abs).then_inc(*act_p.done("abs"))
            act.wait_ge(act_p.sem, act_p(i, "abs"))
            nc.scalar.activation(p_t[:, 1], p_t[:, 0], ACT.Exp, scale=-1.0).then_inc(*act_p.done("exp"))
            act.wait_ge(act_p.sem, act_p(i, "exp"))
            nc.scalar.activation(p_t[:, 2], p_t[:, 1], ACT.Ln, bias=ones[0:PH, 0:1]).then_inc(*act_p.done("ln"))
            act.wait_ge(pe_p.sem, pe_p(i, "q"))
            nc.scalar.activation(p_qT[:], pair[0][:].rearrange("p (g l) -> p g l", g=PG), ACT.Copy).then_inc(*act_p.done("q"))
            act.wait_ge(dve_p.sem, dve_p(i, "hgT"))
            for t in range(T):
                n = P * (t + 1)
                for g in range(PG):
                    first = (t, g) == (0, 0)
                    if not first:
                        a, c = pparts[PG * t + g - 1]
                        act.wait_ge(dve_p.sem, dve_p(i, f"u{a}{c}"))
                    act.wait_ge(pe_p.sem, pe_p(i, f"bc{t}{g}"))
                    for j in range(4):
                        ins_ = nc.scalar.activation(p_e[:, j, 0:n], pair[0][:, j * L:j * L + n], ACT.Exp, scale=-1.0,
                                                    bias=p_hgT[:, t, p_head(g, j):p_head(g, j) + 1])
                    ins_.then_inc(*act_p.done(f"e{t}{g}"))
                    act.wait_ge(pe_p.sem, pe_p(i, f"s{t}{g}"))
                    nc.scalar.activation(p_a[:, :, 0:n], pair[1][:].rearrange("p (j l) -> p j l", j=4)[:, :, 0:n],
                                         ACT.Abs).then_inc(*act_p.done(f"abs{t}{g}"))
                    act.wait_ge(dve_p.sem, dve_p(i, f"rm{t}{g}"))
                    if not first:
                        act.wait_ge(pe_p.sem, pe_p(i, f"pT{a}{c}"))
                    for j in range(4):
                        ins_ = nc.scalar.activation(p_p[:, j, 0:n], p_s[:, j, 0:n], ACT.Square, scale=p_rm[:, j:j + 1])
                    ins_.then_inc(*act_p.done(f"p{t}{g}"))
                    act.wait_ge(pe_p.sem, pe_p(i, f"pT{t}{g}"))
                    m = 4 * (t + 1)
                    if not first:
                        act.wait_ge(pe_p.sem, pe_p(i, f"o{a}{c}"))
                    nc.scalar.activation(p_pT[:, 0:m, :], pair[2][:, 0:m * P].rearrange("p (c k) -> p c k", c=m),
                                         ACT.Copy).then_inc(*act_p.done(f"pT{t}{g}"))

        def p_dve(dve, i):
            dve.wait_ge(dve_ln.sem, dve_ln(3 * NSEQ, "z"))
            dve.wait_ge(dve_p.sem, dve_p.all(i - 1))
            dve.wait_ge(act_p.sem, act_p.all(i - 1))
            nc.vector.tensor_scalar(p_zc[:], seq(Z, i), 1.0, None, ALU.mult).then_inc(*dve_p.done("zc"))
            dve.wait_ge(act_p.sem, act_p(i, "abs"))
            nc.vector.tensor_scalar(p_t[:, 3], bank[1][0:PH, 0:L], 0.0, None, ALU.min).then_inc(*dve_p.done("min"))
            dve.wait_ge(act_p.sem, act_p(i, "ln"))
            dve.wait_ge(dve_p.sem, dve_p(i, "min"))
            nc.vector.tensor_tensor(p_t[:, 4], p_t[:, 3], p_t[:, 2], ALU.subtract).then_inc(*dve_p.done("lg"))
            dve.wait_ge(dve_p.sem, dve_p(i, "lg"))
            nc.vector.tensor_tensor_scan(p_t[:, 3], ones[0:PH, :], p_t[:, 4], 0.0, ALU.mult,
                                         ALU.add).then_inc(*dve_p.done("cum"))
            dve.wait_ge(dve_p.sem, dve_p(i, "cum"))
            nc.vector.tensor_scalar(p_hg[:], p_t[:, 3], 0.5, None, ALU.mult).then_inc(*dve_p.done("hg"))
            dve.wait_ge(dve_p.sem, dve_p(i, "hg"))
            nc.vector.tensor_copy(p_g3[0:PH, :], p_hg[:]).then_inc(*dve_p.done("hi"))
            dve.wait_ge(dve_p.sem, dve_p(i, "hi"))
            nc.vector.tensor_tensor(p_t[:, 4], p_hg[:], p_g3[0:PH, :], ALU.subtract).then_inc(*dve_p.done("r1"))
            dve.wait_ge(dve_p.sem, dve_p(i, "r1"))
            nc.vector.tensor_copy(p_mid[:], p_t[:, 4]).then_inc(*dve_p.done("mid"))
            nc.vector.tensor_copy(p_g3[32:32 + PH, :], p_t[:, 4]).then_inc(*dve_p.done("mid2"))
            dve.wait_ge(dve_p.sem, dve_p(i, "mid"))
            nc.vector.tensor_tensor(p_g3[64:64 + PH, :], p_t[:, 4], p_mid[:], ALU.subtract).then_inc(*dve_p.done("lo"))
            dve.wait_ge(pe_p.sem, pe_p(i, "k"))
            nc.vector.tensor_copy(p_kT[:], pair[1][:].rearrange("p (g l) -> p g l", g=PG)).then_inc(*dve_p.done("k"))
            dve.wait_ge(pe_p.sem, pe_p(i, "v"))
            for t in range(T):
                ins_ = nc.vector.tensor_copy(p_v[:, t, :, 0:PS],
                                             bank[0][:, t * P:t * P + P].rearrange("p (h d) -> p h d", h=PH))
            ins_.then_inc(*dve_p.done("v"))
            dve.wait_ge(pe_p.sem, pe_p(i, "hgT"))
            nc.vector.tensor_copy(p_hgT[:], bank[0][:, L:L + T * PH].rearrange("p (t h) -> p t h", t=T)).then_inc(*dve_p.done("hgT"))
            for t in range(T):
                n = P * (t + 1)
                for g in range(PG):
                    if (t, g) != (0, 0):
                        a, c = pparts[PG * t + g - 1]
                        dve.wait_ge(act_p.sem, act_p(i, f"p{a}{c}"))
                    dve.wait_ge(act_p.sem, act_p(i, f"abs{t}{g}"))
                    nc.vector.scalar_tensor_tensor(out=p_s[:, :, 0:n], in0=p_a[:, :, 0:n], scalar=1e-7, in1=p_e[:, :, 0:n],
                                                   op0=ALU.add, op1=ALU.mult).then_inc(*dve_p.done(f"u{t}{g}"))
                    dve.wait_ge(dve_p.sem, dve_p(i, f"u{t}{g}"))
                    nc.vector.tensor_reduce(p_m[:], p_s[:, :, 0:n], AX.X, ALU.max).then_inc(*dve_p.done(f"m{t}{g}"))
                    dve.wait_ge(dve_p.sem, dve_p(i, f"m{t}{g}"))
                    nc.vector.reciprocal(p_rm[:], p_m[:]).then_inc(*dve_p.done(f"rm{t}{g}"))
            dve.wait_ge(pe_p.sem, pe_p(i, f"o{T - 1}{PG - 1}"))
            o = bank[1][:, 0:T * PH * (PS + 1)].rearrange("p (t h d) -> p t h d", t=T, h=PH)
            nc.vector.reciprocal(p_rn[:], o[:, :, :, PS]).then_inc(*dve_p.done("rn"))
            dve.wait_ge(dve_p.sem, dve_p(i, "rn"))
            nc.vector.tensor_tensor(p_y[:], o[:, :, :, 0:PS], p_rn[:].unsqueeze(3).broadcast_to([P, T, PH, PS]),
                                    ALU.mult).then_inc(*dve_p.done("y"))
            dve.wait_ge(dve_p.sem, dve_p(i, "y"))
            nc.vector.tensor_tensor(seq(X, i), seq(X, i), p_y[:].rearrange("p t h d -> p (t h d)"),
                                    ALU.add).then_inc(*dve_p.done("x"))

        block = ctx.enter_context(nc.Block())
        NF = len(fw)

        def weights_of_layer(name, layer):
            return ins["f_" + name][layer]

        FCALLS = [0, 1] if PHASES >= 4 else ([0] if PHASES >= 2 else [])

        @block.sync
        def _(sp):
            for t, name in consts:
                sp.dma_start(t, ins[name]).then_inc(loaded, 16)
            xv = ins["x"].rearrange("b (t p) d -> p b t d", p=P)
            for c in range(4):
                n = NSEQ // 4
                for b in range(n * c, n * c + n):
                    sp.dma_start(tiles(X[:, b, :]), xv[:, b]).then_inc(x_loaded, 16)
            for call in FCALLS:
                with sp.Fori(0, 2) as layer:
                    w = call * 2 * NSEQ
                    sp.wait_ge(dve_f.sem, dve_f.all(layer * NSEQ + w))
                    for name, t in fw.items():
                        sp.dma_start(t[:], weights_of_layer(name, layer)).then_inc(f_loaded, 16)
            ov = out.rearrange("b (t p) d -> p b t d", p=P)
            sp.wait_ge(x_done, NSEQ * max(1, len(FCALLS)))
            for b in range(NSEQ):
                sp.dma_start(ov[:, b], tiles(X[:, b, :])).then_inc(stored, 16)
            sp.wait_ge(stored, 16 * NSEQ)

        NC = len(consts)

        @block.tensor
        def _(pe):
            credit(pe, pe_mp, pe_mh, pe_f, pe_p)
            pe.wait_ge(loaded, 16 * NC)
            with pe.Fori(0, NSEQ // 2) as p:
                for b in range(2):
                    i = 2 * p + 1 + b
                    m_pe_prefix(pe, i, b)
                    for g in grp:
                        m_pe_heavy(pe, i, b, g)
            for call in FCALLS:
                if call:
                    with pe.Fori(1, NSEQ + 1) as i:
                        p_pe(pe, i)
                with pe.Fori(0, 2) as layer:
                    with pe.Fori(1, NSEQ + 1) as i:
                        f_pe(pe, (call * 2 + layer) * NSEQ + i, (call * 2 + layer + 1) * 16 * NF)

        @block.scalar
        def _(act):
            credit(act, act_mp, act_mh, act_f, act_p)
            act.wait_ge(loaded, 16 * NC)
            act.wait_ge(const_set, 11)
            nc.scalar.activation(m_A[:], mw["A_log"][:], ACT.Exp).then_inc(const_set, 1)
            with act.Fori(0, NSEQ // 2) as p:
                for b in range(2):
                    i = 2 * p + 1 + b
                    act.wait_ge(dve_ln.sem, dve_ln(NSEQ, "z"))
                    m_act_prefix(act, i, b)
                    if True:
                        act.wait_ge(const_set, 13)
                    for g in grp:
                        m_act_heavy(act, i, b, g)
            for call in FCALLS:
                if call:
                    with act.Fori(1, NSEQ + 1) as i:
                        p_act(act, i)
                with act.Fori(0, 2) as layer:
                    with act.Fori(1, NSEQ + 1) as i:
                        f_act(act, (call * 2 + layer) * NSEQ + i, (call * 2 + layer + 1) * 16 * NF)

        @block.vector
        def _(dve):
            credit(dve, dve_mp, dve_mh, dve_ln, dve_f, dve_p)
            dve.wait_ge(loaded, 16 * NC)
            dve.wait_ge(const_set, 12)
            nc.vector.tensor_scalar(m_A[:], m_A[:], -1.0, None, ALU.mult).then_inc(const_set, 1)
            with dve.Fori(1, NSEQ + 1) as i:
                ln_dve(dve, i, 0, (x_loaded, 16 * NSEQ), 0)
            with dve.Fori(0, NSEQ // 2) as p:
                for b in range(2):
                    i = 2 * p + 1 + b
                    m_dve_prefix(dve, i, b)
                    for g in grp:
                        m_dve_heavy(dve, i, b, g)
            with dve.Fori(1, NSEQ + 1) as i:
                ln_dve(dve, i, 1, (dve_mh.sem, dve_mh.all(NSEQ)), 0)
            for call in FCALLS:
                if call:
                    with dve.Fori(1, NSEQ + 1) as i:
                        p_dve(dve, i)
                    with dve.Fori(1, NSEQ + 1) as i:
                        ln_dve(dve, i, 3, (dve_p.sem, dve_p.all(NSEQ)), 0)
                with dve.Fori(0, 2) as layer:
                    dve.wait_ge(f_loaded, (call * 2 + layer + 1) * 16 * NF)
                    for t in range(T):
                        for x in range(2):
                            qs = fw["qs"][:, x, :]
                            nc.vector.tensor_tensor(f_tab[:, t, x, 0], rot[:, t, x, 0], qs, ALU.mult)
                            for e in range(2):
                                o = slice(32 * e, 32 * e + 32)
                                ins_ = nc.vector.tensor_tensor(f_tab[:, t, x, 1, o], rot[:, t, x, 1, o],
                                                               qs[:, 32 - 32 * e:64 - 32 * e], ALU.mult)
                    ins_.then_inc(f_table, 1)
                    with dve.Fori(1, NSEQ + 1) as i:
                        f_dve(dve, (call * 2 + layer) * NSEQ + i, i, (dve_ln.sem, dve_ln((2 + 2 * call) * NSEQ, "z")),
                              call * 2 + layer + 1)
                dve.wait_ge(dve_f.sem, dve_f.all((call + 1) * 2 * NSEQ))
                with dve.Fori(1, NSEQ + 1) as i:
                    nc.vector.tensor_tensor(seq(X, i), seq(X, i), seq(Z, i), ALU.add).then_inc(x_done, 1)
                if call == 0 and PHASES > 2:
                    with dve.Fori(1, NSEQ + 1) as i:
                        ln_dve(dve, i, 2, (x_done, NSEQ), 0)
            if not FCALLS:
                dve.wait_ge(dve_ln.sem, dve_ln.all(2 * NSEQ))
                dve.drain().then_inc(x_done, NSEQ)

        @block.gpsimd
        def _(pool):
            credit(pool, pool_mp, pool_mh, pool_ln, pool_f)
            nc.gpsimd.memset(ones[:], 1.0).then_inc(const_set, 1)
            nc.gpsimd.memset(mhalf[:], -0.5).then_inc(const_set, 1)
            nc.gpsimd.memset(m_pad[:, :, 0:CONV - 1], 0.0).then_inc(const_set, 1)
            nc.gpsimd.memset(m_a[:, :, :, :, 0:1], 0.0).then_inc(const_set, 1)
            nc.gpsimd.memset(f_hT[:, 0:1], 0.0).then_inc(const_set, 1)
            nc.gpsimd.memset(f_v[:, :, :, DH:DH + 1], 1.0).then_inc(const_set, 1)
            nc.gpsimd.memset(f_p[:], 0.0).then_inc(const_set, 1)
            nc.gpsimd.memset(p_v[:, :, :, PS:PS + 1], 1.0).then_inc(const_set, 1)
            nc.gpsimd.memset(p_g3[:], 0.0).then_inc(const_set, 1)
            nc.gpsimd.memset(eps[:], LN_EPS).then_inc(const_set, 1)
            nc.gpsimd.memset(eps_sum[:], LN_EPS * D).then_inc(const_set, 1)
            pool.wait_ge(const_set, 11)
            with pool.Fori(1, NSEQ + 1) as i:
                ln_pool(pool, i, 0)
            with pool.Fori(0, NSEQ // 2) as p:
                for b in range(2):
                    i = 2 * p + 1 + b
                    m_pool_prefix(pool, i, b)
                    for g in grp:
                        m_pool_heavy(pool, i, b, g)
            with pool.Fori(1, NSEQ + 1) as i:
                ln_pool(pool, i, 1)
            for call in FCALLS:
                if call:
                    with pool.Fori(1, NSEQ + 1) as i:
                        ln_pool(pool, i, 3)
                with pool.Fori(0, 2) as layer:
                    with pool.Fori(1, NSEQ + 1) as i:
                        f_pool(pool, (call * 2 + layer) * NSEQ + i, (call * 2 + layer + 1) * 16 * NF)
                if call == 0 and PHASES > 2:
                    with pool.Fori(1, NSEQ + 1) as i:
                        ln_pool(pool, i, 2)


def shape_constants(np, bf16):
    k = np.arange(P)
    big = 1e30
    sel = np.zeros((96, 32, P), np.float32)
    for r in range(96):
        sel[r, r % 32, :] = 1
    kk = np.arange(L)
    band = np.where((kk[None] > k[:, None] + P) | (kk[None] < k[:, None] + P - W), -big, 0.0)
    tri = np.where(k[None] > k[:, None], big, 0.0)
    half_idx = np.arange(0, DH, 2, dtype=np.float32)
    inv = (1.0 / np.float32(10000.0) ** (half_idx / np.float32(DH))).astype(np.float32)
    t = np.arange(L, dtype=np.float32)
    f = t[:, None] * inv[None]
    f = np.concatenate([f, f], -1)
    base = (half_idx + np.float32(0.4 * DH)) / np.float32(1.4 * DH)
    power = (t - L // 2) / np.float32(W // 2)
    scale = (base[None] ** power[:, None]).astype(np.float32)
    scale = np.concatenate([scale, scale], -1)
    cos, sin = np.cos(f), np.sin(f)
    sgn = np.concatenate([-np.ones(DH // 2), np.ones(DH // 2)])
    rot = np.stack([np.stack([8 * cos * scale, 8 * sin * scale * sgn], 1),
                    np.stack([cos / scale, sin / scale * sgn], 1)], 1)
    rot = rot.reshape(T, P, 2, 2, DH).transpose(1, 0, 2, 3, 4)
    f32 = np.float32
    return {"ident": np.eye(P, dtype=f32), "identb": np.eye(P, dtype=f32).astype(bf16), "sel": sel.astype(bf16),
            "band": band.astype(f32).astype(bf16), "tri": tri.astype(f32).astype(bf16),
            "shift": np.eye(P, k=1, dtype=f32), "carry": np.where((k[:, None] == P - 1) & (k[None] == 0), 1, 0).astype(f32),
            "rot": np.ascontiguousarray(rot.astype(f32))}


def lay_out(np, a):
    def chunks(w):
        return w.reshape(-1, P, w.shape[-1]).transpose(1, 0, 2)

    def col(v):
        return v.reshape(-1, P).T

    m, f = "L0_attn_a_", "L0_ffn_"
    out = {"x": a[m + "resid"]}
    out["m_in_w"] = a[m + "in_w"].T
    out["m_skip_w"] = a[m + "skip_w"].T
    out["m_wd1"] = chunks(a[m + "wd1"].T)
    out["m_wbc"] = chunks(np.concatenate([a[m + "wb"], a[m + "wc"]], 0).T)
    out["m_wd2"] = a[m + "wd2"].T
    out["m_out_w"] = chunks(a[m + "out_w"].T)
    out["m_norm_w"] = a[m + "norm_w"][:, None]
    out["m_conv_w"] = chunks(a[m + "conv_w"][:, 0, :])
    out["m_conv_b"] = col(a[m + "conv_b"])
    out["m_wd2_b"] = col(a[m + "wd2_b"])
    out["m_A_log"] = chunks(a[m + "A_log"])
    out["m_W_D"] = col(a[m + "W_D"])
    w = a["L0_attn_b_W"]
    qk = np.zeros((P, 2, PG, P), w.dtype)
    for x in range(2):
        for h in range(PH):
            qk[:, x, h // 4, 32 * (h % 4):32 * (h % 4) + PS] = w[x * D + h * PS:x * D + (h + 1) * PS].T
    out["p_wqk"] = qk
    out["p_wv"] = w[2 * D:3 * D].T
    out["p_wg"] = w[3 * D:].T
    out["f_wqkv"] = a[f + "wqkv"]
    out["f_wo"] = np.stack([chunks(x) for x in a[f + "wo"]])
    out["f_w1"] = a[f + "w1"]
    pad = np.zeros((2, HC * P - HID, D), w.dtype)
    out["f_w2"] = np.stack([chunks(x) for x in np.concatenate([a[f + "w2"], pad], 1)])
    out["f_b2"] = np.broadcast_to(a[f + "b2"][:, None, :], (2, P, D))
    qs = np.stack([a[f + "q_scale"], a[f + "k_scale"]], 1)
    out["f_qs"] = np.broadcast_to(qs[:, None], (2, P, 2, DH))
    out["f_lg"] = a[f + "ln_g"][:, :, None]
    out["f_lb"] = a[f + "ln_b"][:, :, None]
    b1 = a[f + "b1"].reshape(2, 2, HID)
    b1 = np.concatenate([b1, np.zeros((2, 2, HC * P - HID), b1.dtype)], -1)
    out["f_b1"] = b1.reshape(2, 2, HC, P).transpose(0, 3, 1, 2)
    return out


def kernel(**inputs):
    import numpy as np
    import concourse.bacc as bacc
    from concourse import mybir as mb
    from concourse.bass_utils import run_bass_kernel_spmd as run

    nc = bacc.Bacc("TRN2", target_bir_lowering=False, num_devices=1)
    arrays = lay_out(np, {k: np.asarray(v) for k, v in inputs.items()})
    arrays.update(shape_constants(np, mb.dt.np(mb.dt.bfloat16)))
    feeds, ins = {}, {}
    for name, v in arrays.items():
        v = np.ascontiguousarray(v)
        feeds[f"in_{name}"] = v
        ins[name] = nc.dram_tensor(f"in_{name}", v.shape, mb.dt.from_np(v.dtype), kind="ExternalInput").ap()
    out = nc.dram_tensor("out_x", (NSEQ, L, D), F32, kind="ExternalOutput").ap()
    build(nc, ins, out)
    r = run(nc, [feeds], core_ids=[0])
    return r.results[0]["out_x"]
```

```python
from contextlib import ExitStack

import concourse.bass as bass
from concourse import mybir

P = 128
F32 = mybir.dt.float32
BF16 = mybir.dt.bfloat16
ALU = mybir.AluOpType
ACT = mybir.ActivationFunctionType
AX = mybir.AxisListType

NSEQ, L, D = 16, 256, 128
T = L // P
E, NS, DD, CONV = 256, 16, 64, 4
EC = E // P
GN = 2
NG = NS // GN
H, DH, W = 8, 64, 64
INNER = H * DH
HID = int(D * 4 * 2 / 3)
HC = (HID + P - 1) // P
HR = [min(P, HID - c * P) for c in range(HC)]
PH, PS = 16, 8
PG = PH // 4
LN_EPS = 1e-5
AHEAD = 2
PHASES = 4


class Stream:

    def __init__(self, sem, steps):
        self.sem, self.steps = sem, steps
        self.index = {s: n for n, s in enumerate(steps)}
        assert len(self.index) == len(steps)
        self.at = 0
        self.credit = AHEAD * len(steps)

    def __call__(self, i, step):
        return (i + (AHEAD - 1)) * len(self.steps) + (self.index[step] + 1)

    def all(self, i):
        return (i + AHEAD) * len(self.steps)

    def done(self, step):
        assert self.steps[self.at % len(self.steps)] == step, (self.steps[self.at % len(self.steps)], step)
        self.at += 1
        return self.sem, 1


class Stages:

    def __init__(self, new_sem, name, order, stages):
        self.order = order.split()
        self.stage = {s: n for n, st in enumerate(stages) for s in st.split()}
        self.streams = [Stream(new_sem(f"{name}_{n}"), mine) if mine else None for n, mine in
                        enumerate([[s for s in self.order if self.stage[s] == n] for n in range(len(stages))])]

    def at(self, i, step):
        stream = self.streams[self.stage[step]]
        return stream.sem, stream(i, step)

    def done(self, step):
        return self.streams[self.stage[step]].done(step)


def run_windows(eng, stages, step, count):
    n = 1 + max(stages.stage.values())

    def window(k, parity, live):
        for s in stages.order:
            lag = stages.stage[s]
            if lag in live:
                step(s, k - lag, (parity - lag) % 2)

    odd = (count - n + 1) % 2
    for k in range(1, n + odd):
        window(k, k % 2, range(min(k, n)))
    with eng.Fori(0, (count - n + 1) // 2) as p:
        for b in range(2):
            window(2 * p + (n + odd + b), (n + odd + b) % 2, range(n))
    for k in range(count + 1, count + n):
        window(k, k % 2, range(k - count, n))


F_STAGES = [
    "zc xT hT qk0 v0 sq0 ve0 v1 ve1 ss0 cl0 rn0 kn0 qa0 qb0 qk1 sq1 ss1 cl1 rn1 kn1 qa1 qb1 T00 Te00 T01 "
    "Te01 T10 Te10 T11 Te11",
    "s00 nm00 p00 pT000 pe000 o00 rs00 on00 s01 nm01 p01 pT010 pe010 o01 rs01 on01 s10 nm10 p10 pT100 "
    "pe100 pT101 pe101 o10 rs10 on10 s11 nm11 p11 pT110 pe110 pT111 pe111 o11 rs11 on11",
    "oT0 oe0 oT1 oe1 wo z1 sh hb st mv vv rv zb hn hnT he w1a g0 w1b g1 u1 w1c u0 w2 z2"]
F_ORDER = {
    "dve": "zc nm00 hT ss0 cl0 nm01 z1 kn0 nm10 st mv qa0 hn ss1 cl1 rs00 nm11 on00 pe101 rs01 on01 kn1 rs10 qa1 "
        "u1 pe111 on10 u0 rs11 on11 z2",
    "pe": "s00 oT0 xT qk0 oT1 s01 pT000 v0 wo s10 sh o00 qk1 pT010 s11 pT100 hnT v1 pT101 w1a o01 T00 o10 pT110 "
        "w1b T01 pT111 w1c T10 o11 T11 w2",
    "act": "oe0 p00 sq0 oe1 p01 pe000 hb p10 sq1 pe010 ve0 pe100 he ve1 p11 g0 Te00 pe110 g1 Te01 Te10 Te11",
    "pool": "rn0 vv rv qb0 zb rn1 qb1"}

P_STAGES = [
    "zc xT xTe g abs min exp ln lg cum hg hi r1 mid mid2 lo hgT he v vc q0 qc0 q1 qc1 k0 kc0 k1 kc1",
    "bc00 e00 s00 ab00 u00 m00 rm00 p00 pT00 pe00 o00 bc01 e01 s01 ab01 u01 m01 rm01 p01 pT01 pe01 o01 "
    "bc02 e02 s02 ab02 u02 m02 rm02 p02 pT02 pe02 o02 bc03 e03 s03 ab03 u03 m03 rm03 p03 pT03 pe03 o03 "
    "bc10 e10 s10 ab10 u10 m10 rm10 p10 pT10 pe10 o10 bc11 e11 s11 ab11 u11 m11 rm11 p11 pT11 pe11 o11 "
    "bc12 e12 s12 ab12 u12 m12 rm12 p12 pT12 pe12 o12 bc13 e13 s13 ab13 u13 m13 rm13 p13 pT13 pe13 o13 rn "
    "y x"]
P_ORDER = {
    "dve": "zc u00 u01 min m00 rm00 m01 rm01 u02 m02 lg rm02 pe00 cum u03 hg m03 rm03 pe01 he pe02 u10 m10 rm10 "
        "vc pe03 u11 m11 hi rm11 pe10 u12 m12 pe11 rm12 u13 r1 m13 rm13 mid pe12 mid2 kc0 lo pe13 kc1 rn y",
    "pe": "bc00 s00 xT bc01 s01 g bc02 s02 bc03 s03 s10 pT00 bc10 s11 hgT pT01 o00 pT02 v bc11 pT03 o01 o02 s12 "
        "bc12 pT10 o03 s13 bc13 pT11 q0 q1 o10 pT12 k0 o11 pT13 o12 k1 o13",
    "act": "e00 ab00 xTe e01 ab01 abs e02 ab02 exp p00 ab03 e03 ln ab10 p01 p02 e10 p03 ab11 e11 p10 ab12 e12 "
        "p11 ab13 e13 qc0 p12 qc1 p13",
    "pool": "x"}

M_STAGES = [
    "sq me rr xr xT xTe xe pad skip gate cv0 cv1 cv2 cv3 xs u bc ue hi r1 mid mid2 lo z abs exp ln pos "
    "delta xx dx",
    "bc0 a0 c0 bx0 h0 hc0 y0 bc1 a1 c1 bx1 h1 hc1 y1 bc2 a2 c2 bx2 h2 hc2 y2 bc3 a3 c3 bx3 h3 hc3 y3 bc4 "
    "a4 c4 bx4 h4 hc4 y4 bc5 a5 c5 bx5 h5 hc5 y5 bc6 a6 c6 bx6 h6 hc6 y6 bc7 a7 c7 bx7 h7 hc7 y7 ys yg "
    "out x"]
M_ORDER = {
    "dve": "bx0 xr bx1 h0 h1 bx2 cv0 bx3 h2 h3 bx4 cv1 h4 bx5 cv2 h5 cv3 bx6 h6 bx7 ue h7 hi r1 mid2 pos mid lo "
        "delta ys yg x",
    "pe": "bc0 bc1 bc2 xT xe bc3 skip y0 bc4 bc5 y1 y2 y3 bc6 bc7 y4 u bc y5 z y6 y7 out",
    "act": "sq a0 c0 a1 c1 xTe a2 pad c2 a3 c3 a4 c4 a5 a6 c5 gate c6 xs a7 c7 abs exp ln",
    "pool": "me rr hc0 hc1 hc2 hc3 hc4 hc5 hc6 hc7 xx dx"}


def build(nc, ins, out):
    with ExitStack() as ctx:
        def sb(name, shape, dt=F32):
            return ctx.enter_context(nc.sbuf_tensor(name, shape, dt))

        m_ctx = ExitStack()

        def m_sb(name, shape, dt=F32):
            return m_ctx.enter_context(nc.sbuf_tensor(name, shape, dt))

        def sem(name):
            return ctx.enter_context(nc.semaphore(name))

        bank = [ctx.enter_context(nc.psum_tensor(f"bank{n}", [P, 512], F32)) for n in range(2)]
        pair = [ctx.enter_context(nc.psum_tensor(f"pair{n}", [P, 1024], F32)) for n in range(3)]

        X = sb("X", [P, NSEQ, L])
        Z = sb("Z", [P, NSEQ, L])
        ident = sb("ident", [P, P])
        identb = sb("identb", [P, P], BF16)
        sel = sb("sel", [96, 32, P], BF16)
        band = sb("band", [P, L], BF16)
        tri = sb("tri", [P, P], BF16)
        shift = sb("shift", [P, P])
        carry = sb("carry", [P, P])
        ones = sb("ones", [P, L])
        mhalf = sb("mhalf", [P, 2 * H])
        eps = sb("eps", [P, T])
        eps_sum = sb("eps_sum", [P, T])
        carrier = sb("carrier", [P, 1])
        lst = sb("lst", [P, T, 6])
        lmv = sb("lmv", [P, T, 2])
        lve = sb("lve", [P, T])
        lrs = sb("lrs", [P, T])

        loaded = sem("loaded")
        x_loaded = sem("x_loaded")
        const_set = sem("const_set")
        stored = sem("stored")

        consts = [(ident[:], "ident"), (identb[:], "identb"), (sel[:], "sel"), (band[:], "band"), (tri[:], "tri"),
                  (shift[:], "shift"), (carry[:], "carry")]

        mw = dict(
            in_w=sb("m_in_w", [P, E]), skip_w=sb("m_skip_w", [P, E]), wd1=sb("m_wd1", [P, EC, DD]),
            wbc=sb("m_wbc", [P, EC, 2 * NS]), wd2=sb("m_wd2", [DD, E]), out_w=sb("m_out_w", [P, EC, D]),
            norm_w=sb("m_norm_w", [P, 1]), conv_w=sb("m_conv_w", [P, EC, CONV]), conv_b=sb("m_conv_b", [P, EC]),
            wd2_b=sb("m_wd2_b", [P, EC]), A_log=sb("m_A_log", [P, EC, NS]), W_D=sb("m_W_D", [P, EC]))
        consts += [(t[:], "m_" + n) for n, t in mw.items()]
        m_A = sb("m_A", [P, EC, NS])
        m_pad = sb("m_pad", [P, EC, CONV - 1 + L])
        m_a = sb("m_a", [P, 2, GN, EC, L])

        pe_m, act_m, dve_m, pool_m = (Stages(sem, "m_" + e, M_ORDER[e], M_STAGES) for e in ("pe", "act", "dve", "pool"))

        dve_ln = Stream(sem("dve_ln"), ["st", "mv", "z"])
        pool_ln = Stream(sem("pool_ln"), ["ve", "rs"])

        fw = dict(
            wqkv=sb("f_wqkv", [P, 3 * INNER]), wo=sb("f_wo", [P, INNER // P, D]), w1=sb("f_w1", [P, 2 * HID]),
            w2=sb("f_w2", [P, HC, D]), b2=sb("f_b2", [P, D]), qs=sb("f_qs", [P, 2, DH]), lg=sb("f_lg", [P, 1]),
            lb=sb("f_lb", [P, 1]), b1=sb("f_b1", [P, 2, HC]))
        rot = sb("rot", [P, T, 2, 2, DH])
        consts += [(rot[:], "rot")]
        f_tab = sb("f_tab", [P, T, 2, 2, DH])
        f_hT = sb("f_hT", [P, L])
        f_v = sb("f_v", [P, 2, T, H, DH + 1])
        f_p = sb("f_p", [P, T, 4, L])

        pe_f, act_f, dve_f, pool_f = (Stages(sem, "f_" + e, F_ORDER[e], F_STAGES) for e in ("pe", "act", "dve", "pool"))
        f_loaded = sem("f_loaded")
        f_table = sem("f_table")
        x_done = sem("x_done")

        pw = dict(wqk=sb("p_wqk", [P, 2, PG, P]), wv=sb("p_wv", [P, D]), wg=sb("p_wg", [P, PH]))
        consts += [(t[:], "p_" + n) for n, t in pw.items()]
        p_v = sb("p_v", [P, 2, T, PH, PS + 1])
        p_g3 = sb("p_g3", [96, 2, L], BF16)
        m_sq = m_sb("m_sq", [P, T, P])
        m_ss = m_sb("m_ss", [P, T])
        m_rr = m_sb("m_rr", [P, T])
        m_xr = m_sb("m_xr", [P, T, P])
        m_xT = m_sb("m_xT", [P, L])
        m_xc = m_sb("m_xc", [P, 2, EC, L])
        m_xs = m_sb("m_xs", [P, 2, EC, L])
        m_gate = m_sb("m_gate", [P, 2, EC, L])
        m_u = m_sb("m_u", [DD, L])
        m_r = m_sb("m_r", [32, 2, L])
        m_mid = m_sb("m_mid", [32, L], BF16)
        m_bc = m_sb("m_bc", [96, 2, L], BF16)
        m_t = m_sb("m_t", [P, 3, EC, L])
        m_pos = m_sb("m_pos", [P, EC, L])
        m_delta = m_sb("m_delta", [P, 2, EC, L])
        m_dx = m_sb("m_dx", [P, 2, EC, L])
        m_xx = m_sb("m_xx", [P, 2, L])
        m_bx = m_sb("m_bx", [P, 2, GN, EC, L])
        m_h = m_sb("m_h", [P, 2, GN, EC, L])
        m_c = m_sb("m_c", [P, 2, GN, L])
        m_hc = m_sb("m_hc", [P, 2, GN, EC, L])
        m_y = m_sb("m_y", [P, EC, L])
        m_yg = m_sb("m_yg", [P, EC, L])
        m_ctx.close()
        f_zc = m_sb("f_zc", [P, L])
        f_z1 = m_sb("f_z1", [P, L])
        f_sq = m_sb("f_sq", [P, 2 * INNER])
        f_ss = m_sb("f_ss", [P, 2 * H])
        f_cs = m_sb("f_cs", [P, 2 * H])
        f_rn = m_sb("f_rn", [P, 2 * H])
        f_kn = m_sb("f_kn", [P, 2, 2 * H, DH])
        f_qa = m_sb("f_qa", [P, 2, 2 * H, DH])
        f_qb = m_sb("f_qb", [P, 2, 2 * H, DH])
        f_qkT = m_sb("f_qkT", [P, 2, H, L])
        f_nm = m_sb("f_nm", [P, 2, 4])
        f_pT = m_sb("f_pT", [P, 2, 8, P])
        f_rs = m_sb("f_rs", [P, 4])
        f_o = m_sb("f_o", [P, 2, T, H, DH])
        f_oT = m_sb("f_oT", [P, INNER // P, L])
        f_hb = m_sb("f_hb", [P, T, P])
        f_st = m_sb("f_st", [P, T, 6])
        f_mv = m_sb("f_mv", [P, T, 2])
        f_ve = m_sb("f_ve", [P, T])
        f_rv = m_sb("f_rv", [P, T])
        f_hn = m_sb("f_hn", [P, T, P])
        f_hnT = m_sb("f_hnT", [P, L])
        f_g = m_sb("f_g", [P, HC, L])
        f_u = m_sb("f_u", [P, HC, L])
        f_zb = m_sb("f_zb", [P, L])
        m_ctx.close()
        p_zc = sb("p_zc", [P, L])
        p_xT = sb("p_xT", [P, L])
        p_qT = sb("p_qT", [P, 2, PG, L])
        p_kT = sb("p_kT", [P, 2, PG, L])
        p_t = sb("p_t", [PH, 5, L])
        p_hg = sb("p_hg", [PH, L])
        p_hgT = sb("p_hgT", [P, 2, T, PH])
        p_mid = sb("p_mid", [PH, L], BF16)
        p_e = sb("p_e", [P, 2, 4, L])
        p_a = sb("p_a", [P, 2, 4, L])
        p_s = sb("p_s", [P, 2, 4, L])
        p_m = sb("p_m", [P, 2, 4])
        p_rm = sb("p_rm", [P, 2, 4])
        p_p = sb("p_p", [P, 2, 4, L])
        p_pT = sb("p_pT", [P, 2, 8, P])
        p_rn = sb("p_rn", [P, T, PH])
        p_y = sb("p_y", [P, T, PH, PS])
        pe_p, act_p, dve_p, pool_p = (Stages(sem, "p_" + e, P_ORDER[e], P_STAGES) for e in ("pe", "act", "dve", "pool"))

        def credit(eng, *streams):
            for s in streams:
                for t in s.streams if isinstance(s, Stages) else [s]:
                    if t:
                        eng.sem_inc(t.sem, t.credit)

        def half(t, k):
            return t[:, 512 * k:512 * k + 512]

        m_xe_ps = half(pair[0], 0).rearrange("p (c l) -> p c l", c=EC)
        m_sk_ps = half(pair[0], 1).rearrange("p (c l) -> p c l", c=EC)
        m_xT_ps = bank[0][:, 0:L]
        m_u_ps = bank[0][0:DD, 0:L]
        m_bc_ps = bank[0][0:2 * NS, L:2 * L]
        m_y_ps = bank[1][:].rearrange("p (c l) -> p c l", c=EC)

        def m_bcast(g, k):
            return half(pair[1 + g % 2], k).rearrange("p (n l) -> p n l", n=GN)

        def seq(t, i):
            return t[:, i - 1, :]

        def tiles(ap):
            return ap.rearrange("p (t d) -> p t d", t=T)

        def m_before(stages, i, step, g, back):
            return stages.at(i if g >= back else i - 1, f"{step}{(g - back) % NG}")

        M_LAST = NG - 1

        def m_pe(pe, s, i, b):
            k, g = s.rstrip("0123456789"), int("0" + s[len(s.rstrip("0123456789")):])
            if s == "xT":
                pe.wait_ge(*dve_m.at(i, "xr"))
                pe.wait_ge(*dve_m.at(i - 1, "lo"))
                for t in range(T):
                    mm = nc.tensor.transpose(m_xT_ps[:, t * P:t * P + P], m_xr[:, t, :], ident[:])
            elif s == "xe" or s == "skip":
                pe.wait_ge(*act_m.at(i, "xTe"))
                pe.wait_ge(*(dve_m.at(i - 1, "pos") if s == "xe" else act_m.at(i - 1, "gate")))
                o, w = (m_xe_ps, mw["in_w"]) if s == "xe" else (m_sk_ps, mw["skip_w"])
                for c in range(EC):
                    mm = nc.tensor.matmul(o[:, c, :], w[:, c * P:c * P + P], m_xT[:], start=True, stop=True)
            elif s == "u" or s == "bc":
                pe.wait_ge(*act_m.at(i, "xs"))
                o, w = (m_u_ps, mw["wd1"]) if s == "u" else (m_bc_ps, mw["wbc"])
                for c in range(EC):
                    mm = nc.tensor.matmul(o, w[:, c, :], m_xs[:, b, c, :], start=c == 0, stop=c == EC - 1)
            elif s == "z":
                pe.wait_ge(*dve_m.at(i, "ue"))
                pe.wait_ge(*act_m.at(i, "pad"))
                for c in range(EC):
                    mm = nc.tensor.matmul(m_xe_ps[:, c, :], mw["wd2"][:, c * P:c * P + P], m_u[:], start=True, stop=True)
            elif k == "bc":
                pe.wait_ge(*dve_m.at(i, "lo"))
                pe.wait_ge(*m_before(dve_m, i, "bx", g, 2))
                pe.wait_ge(*m_before(act_m, i, "c", g, 2))
                for c in range(2):
                    for n in range(GN):
                        mm = nc.tensor.matmul(m_bcast(g, c)[:, n, :], sel[:, c * NS + g * GN + n, :], m_bc[:, b, :],
                                              start=True, stop=True)
            elif k == "y":
                pe.wait_ge(*pool_m.at(i, f"hc{g}"))
                if g == 0:
                    pe.wait_ge(*dve_m.at(i - 1, "x"))
                for n in range(GN):
                    mm = nc.tensor.matmul(bank[1][:], ident[:], m_hc[:, g % 2, n].rearrange("p c l -> p (c l)"),
                                          start=g == 0 and n == 0, stop=g == NG - 1 and n == GN - 1)
            elif s == "out":
                pe.wait_ge(*dve_m.at(i, "yg"))
                for t in range(T):
                    for c in range(EC):
                        mm = nc.tensor.matmul(bank[1][:, t * P:t * P + P], m_yg[:, c, t * P:t * P + P],
                                              mw["out_w"][:, c, :], start=c == 0, stop=c == EC - 1)
            mm.then_inc(*pe_m.done(s))

        def m_act(act, s, i, b, z_at):
            k, g = s.rstrip("0123456789"), int("0" + s[len(s.rstrip("0123456789")):])
            if s == "sq":
                act.wait_ge(*pool_m.at(i - 1, "rr"))
                for t in range(T):
                    op = nc.scalar.activation(m_sq[:, t, :], tiles(seq(Z, z_at))[:, t, :], ACT.Square,
                                              accum_out=m_ss[:, t:t + 1])
            elif s == "xTe":
                act.wait_ge(*pe_m.at(i, "xT"))
                op = nc.scalar.activation(m_xT[:], m_xT_ps, ACT.Copy, scale=mw["norm_w"][:])
            elif s == "pad":
                act.wait_ge(*pe_m.at(i, "xe"))
                act.wait_ge(*dve_m.at(i - 1, "cv3"))
                op = nc.scalar.activation(m_pad[:, :, CONV - 1:], m_xe_ps, ACT.Copy)
            elif s == "gate":
                act.wait_ge(*pe_m.at(i, "skip"))
                act.wait_ge(*dve_m.at(i - 2, "yg"))
                op = nc.scalar.activation(m_gate[:, b], m_sk_ps, ACT.Silu)
            elif s == "xs":
                act.wait_ge(*dve_m.at(i, "cv3"))
                act.wait_ge(*dve_m.at(i - 2, "ys"))
                op = nc.scalar.activation(m_xs[:, b], m_xc[:, 1], ACT.Silu)
            elif s == "abs":
                act.wait_ge(*pe_m.at(i, "z"))
                for c in range(EC):
                    op = nc.scalar.activation(m_t[:, 0, c, :], m_xe_ps[:, c, :], ACT.Abs, bias=mw["wd2_b"][:, c:c + 1])
            elif s == "exp":
                act.wait_ge(*act_m.at(i, "abs"))
                op = nc.scalar.activation(m_t[:, 1], m_t[:, 0], ACT.Exp, scale=-1.0)
            elif s == "ln":
                act.wait_ge(*act_m.at(i, "exp"))
                act.wait_ge(*dve_m.at(i - 1, "delta"))
                op = nc.scalar.activation(m_t[:, 2], m_t[:, 1], ACT.Ln, bias=ones[:, 0:1])
            elif k == "a":
                act.wait_ge(const_set, 13)
                act.wait_ge(*dve_m.at(i, "delta"))
                act.wait_ge(*m_before(dve_m, i, "h", g, 2))
                for n in range(GN):
                    for c in range(EC):
                        op = nc.scalar.activation(m_a[:, g % 2, n, c, 1:L], m_delta[:, b, c, 1:L], ACT.Exp,
                                                  scale=m_A[:, c, g * GN + n:g * GN + n + 1])
            elif k == "c":
                act.wait_ge(*pe_m.at(i, f"bc{g}"))
                act.wait_ge(*m_before(pool_m, i, "hc", g, 2))
                op = nc.scalar.activation(m_c[:, g % 2], m_bcast(g, 1), ACT.Copy)
            op.then_inc(*act_m.done(s))

        def m_dve(dve, s, i, b, z_at):
            k, g = s.rstrip("0123456789"), int("0" + s[len(s.rstrip("0123456789")):])
            if s == "xr":
                dve.wait_ge(*pool_m.at(i, "rr"))
                dve.wait_ge(*pe_m.at(i - 1, "xT"))
                for t in range(T):
                    op = nc.vector.tensor_scalar(m_xr[:, t, :], tiles(seq(Z, z_at))[:, t, :], m_rr[:, t:t + 1],
                                                 float(D) ** 0.5, ALU.mult, ALU.mult)
            elif k == "cv":
                if g == 0:
                    dve.wait_ge(*act_m.at(i, "pad"))
                    dve.wait_ge(*act_m.at(i - 1, "xs"))
                else:
                    dve.wait_ge(*dve_m.at(i, f"cv{g - 1}"))
                for c in range(EC):
                    tap, x = mw["conv_w"][:, c, g:g + 1], m_pad[:, c, g:g + L]
                    if g == 0:
                        op = nc.vector.tensor_scalar(m_xc[:, 0, c, :], x, tap, mw["conv_b"][:, c:c + 1], ALU.mult, ALU.add)
                    else:
                        op = nc.vector.scalar_tensor_tensor(out=m_xc[:, g % 2, c, :], in0=x, scalar=tap,
                                                            in1=m_xc[:, (g + 1) % 2, c, :], op0=ALU.mult, op1=ALU.add)
            elif s == "ue":
                dve.wait_ge(*pe_m.at(i, "bc"))
                dve.wait_ge(*pe_m.at(i - 1, "z"))
                op = nc.vector.tensor_copy(m_u[:], m_u_ps)
            elif s == "hi":
                dve.wait_ge(*pe_m.at(i, "bc"))
                dve.wait_ge(*pe_m.at(i - 2, f"bc{M_LAST}"))
                op = nc.vector.tensor_copy(m_bc[0:32, b], m_bc_ps)
            elif s == "r1":
                dve.wait_ge(*dve_m.at(i, "hi"))
                op = nc.vector.tensor_tensor(m_r[:, 0], m_bc_ps, m_bc[0:32, b], ALU.subtract)
            elif s == "mid":
                dve.wait_ge(*dve_m.at(i, "r1"))
                op = nc.vector.tensor_copy(m_mid[:], m_r[:, 0])
            elif s == "mid2":
                dve.wait_ge(*dve_m.at(i, "r1"))
                op = nc.vector.tensor_copy(m_bc[32:64, b], m_r[:, 0])
            elif s == "lo":
                dve.wait_ge(*dve_m.at(i, "mid"))
                op = nc.vector.tensor_tensor(m_bc[64:96, b], m_r[:, 0], m_mid[:], ALU.subtract)
            elif s == "pos":
                dve.wait_ge(*act_m.at(i, "abs"))
                for c in range(EC):
                    op = nc.vector.tensor_scalar(m_pos[:, c, :], m_xe_ps[:, c, :], mw["wd2_b"][:, c:c + 1], 0.0,
                                                 ALU.add, ALU.max)
            elif s == "delta":
                dve.wait_ge(*dve_m.at(i, "pos"))
                dve.wait_ge(*act_m.at(i, "ln"))
                dve.wait_ge(*act_m.at(i - 2, f"a{M_LAST}"))
                op = nc.vector.tensor_tensor(m_delta[:, b], m_pos[:], m_t[:, 2], ALU.add)
            elif k == "bx":
                dve.wait_ge(*pe_m.at(i, f"bc{g}"))
                dve.wait_ge(*pool_m.at(i, "dx"))
                dve.wait_ge(*m_before(dve_m, i, "h", g, 2))
                op = nc.vector.tensor_tensor(m_bx[:, g % 2], m_dx[:, b].unsqueeze(1).broadcast_to([P, GN, EC, L]),
                                             m_bcast(g, 0).unsqueeze(2).broadcast_to([P, GN, EC, L]), ALU.mult)
            elif k == "h":
                dve.wait_ge(*dve_m.at(i, f"bx{g}"))
                dve.wait_ge(*act_m.at(i, f"a{g}"))
                dve.wait_ge(*m_before(pool_m, i, "hc", g, 2))
                flat = "p n c l -> p (n c l)"
                op = nc.vector.tensor_tensor_scan(m_h[:, g % 2].rearrange(flat), m_a[:, g % 2].rearrange(flat),
                                                  m_bx[:, g % 2].rearrange(flat), 0.0, ALU.mult, ALU.add)
            elif s == "ys":
                dve.wait_ge(*pe_m.at(i, f"y{M_LAST}"))
                for c in range(EC):
                    op = nc.vector.scalar_tensor_tensor(out=m_y[:, c, :], in0=m_xs[:, b, c, :], scalar=mw["W_D"][:, c:c + 1],
                                                        in1=m_y_ps[:, c, :], op0=ALU.mult, op1=ALU.add)
            elif s == "yg":
                dve.wait_ge(*dve_m.at(i, "ys"))
                dve.wait_ge(*pe_m.at(i - 1, "out"))
                op = nc.vector.tensor_tensor(m_yg[:], m_y[:], m_gate[:, b], ALU.mult)
            elif s == "x":
                dve.wait_ge(*pe_m.at(i, "out"))
                dve.wait_ge(*pool_m.at(i, "xx"))
                op = nc.vector.tensor_tensor(seq(X, z_at), m_xx[:, b], bank[1][:, 0:L], ALU.add)
            op.then_inc(*dve_m.done(s))

        def m_pool(pool, s, i, b, z_at):
            k, g = s.rstrip("0123456789"), int("0" + s[len(s.rstrip("0123456789")):])
            if s == "me":
                pool.wait_ge(*act_m.at(i, "sq"))
                pool.wait_ge(*dve_m.at(i - 1, "xr"))
                op = nc.gpsimd.tensor_tensor(m_rr[:], m_ss[:], eps_sum[:], ALU.add)
            elif s == "rr":
                pool.wait_ge(*pool_m.at(i, "me"))
                op = nc.gpsimd.tensor_tensor(m_rr[:], m_rr[:], mhalf[:, 0:T], ALU.pow)
            elif s == "xx":
                pool.wait_ge(*dve_m.at(i - 2, "x"))
                op = nc.gpsimd.tensor_tensor(m_xx[:, b], seq(X, z_at), seq(Z, z_at), ALU.add)
            elif s == "dx":
                pool.wait_ge(*dve_m.at(i, "delta"))
                pool.wait_ge(*dve_m.at(i - 2, f"bx{M_LAST}"))
                op = nc.gpsimd.tensor_tensor(m_dx[:, b], m_delta[:, b], m_xs[:, b], ALU.mult)
            elif k == "hc":
                pool.wait_ge(*dve_m.at(i, f"h{g}"))
                pool.wait_ge(*act_m.at(i, f"c{g}"))
                pool.wait_ge(*m_before(pe_m, i, "y", g, 2))
                for n in range(GN):
                    op = nc.gpsimd.tensor_tensor(m_hc[:, g % 2, n], m_h[:, g % 2, n],
                                                 m_c[:, g % 2, n].unsqueeze(1).broadcast_to([P, EC, L]), ALU.mult)
            op.then_inc(*pool_m.done(s))

        def ln_dve(dve, i, k, ready, n):
            j = k * NSEQ + i
            dve.wait_ge(*ready)
            for t in range(T):
                ins_ = nc.vector.bn_stats(lst[:, t, :], tiles(seq(X, i))[:, t, :])
            ins_.then_inc(*dve_ln.done("st"))
            dve.wait_ge(dve_ln.sem, dve_ln(j, "st"))
            dve.wait_ge(pool_ln.sem, pool_ln(j - 1, "ve"))
            nc.vector.tensor_copy(carrier[:], eps[:, 0:1])
            for t in range(T):
                ins_ = nc.vector.bn_aggr(lmv[:, t, :], lst[:, t, :])
            ins_.then_inc(*dve_ln.done("mv"))
            dve.wait_ge(pool_ln.sem, pool_ln(j, "rs"))
            for t in range(T):
                ins_ = nc.vector.tensor_scalar(tiles(seq(Z, i))[:, t, :], tiles(seq(X, i))[:, t, :], lmv[:, t, 0:1],
                                               lrs[:, t:t + 1], ALU.subtract, ALU.mult)
            ins_.then_inc(*dve_ln.done("z"))

        def ln_pool(pool, i, k):
            j = k * NSEQ + i
            pool.wait_ge(dve_ln.sem, dve_ln(j, "mv"))
            nc.gpsimd.tensor_tensor(lve[:], lmv[:, :, 1], eps[:], ALU.add).then_inc(*pool_ln.done("ve"))
            pool.wait_ge(pool_ln.sem, pool_ln(j, "ve"))
            nc.gpsimd.tensor_tensor(lrs[:], lve[:], mhalf[:, 0:T], ALU.pow).then_inc(*pool_ln.done("rs"))

        QK = pair[0][:].rearrange("p (x h d) -> p (x h) d", x=2, h=H)
        SC = pair[1][:].rearrange("p (j k) -> p j k", j=4)
        PT_PS = half(pair[2], 0)
        O_PS = half(pair[2], 1)
        KEYS = [(0, P), (P - W, L)]

        def slot(h):
            return (h % 2) * 2 + (h // 2) % 2

        def part_before(t, g):
            return (f"{t}{g - 1}" if g else f"{t - 1}1", 0) if (t, g) != (0, 0) else ("11", 1)

        def f_pe(pe, s, i, b, loads):
            k, a = s.rstrip("0123456789"), [int(x) for x in s[len(s.rstrip("0123456789")):]]
            if s == "xT":
                pe.wait_ge(*dve_f.at(i, "zc"))
                pe.wait_ge(*act_f.at(i - 1, "Te11"))
                for t in range(T):
                    mm = nc.tensor.transpose(bank[0][:, t * P:t * P + P], f_zc[:, t * P:t * P + P], ident[:])
            elif k == "qk":
                t, = a
                pe.wait_ge(*dve_f.at(i, "hT"))
                pe.wait_ge(*(dve_f.at(i, "kn0") if t else dve_f.at(i - 1, "kn1")))
                if t == 0:
                    pe.wait_ge(f_loaded, loads)
                for n in range(2):
                    mm = nc.tensor.matmul(half(pair[0], n), f_hT[:, t * P:t * P + P], fw["wqkv"][:, n * 512:n * 512 + 512],
                                          start=True, stop=True)
            elif k == "v":
                t, = a
                if t:
                    pe.wait_ge(*act_f.at(i, "ve0"))
                else:
                    pe.wait_ge(*dve_f.at(i, "hT"))
                mm = nc.tensor.matmul(bank[0][:], f_hT[:, t * P:t * P + P], fw["wqkv"][:, 1024:1536], start=True, stop=True)
            elif k == "T":
                t, x = a
                pe.wait_ge(*pool_f.at(i, f"qb{t}"))
                pe.wait_ge(*dve_f.at(i, f"qa{t}"))
                pe.wait_ge(*act_f.at(i, "ve1" if (t, x) == (0, 0) else f"Te{t}0" if x else "Te01"))
                for c in range(4):
                    h = x * H + 2 * c
                    for y, start in ((f_qa, True), (f_qb, False)):
                        mm = nc.tensor.matmul(bank[0][:, c * P:c * P + P], y[:, t, h:h + 2, :].rearrange("p h d -> p (h d)"),
                                              ident[:], start=start, stop=not start, is_transpose=True)
            elif k == "s":
                t, g = a
                k0, k1 = KEYS[t]
                pe.wait_ge(*act_f.at(i, "Te11"))
                n, back = part_before(t, g)
                pe.wait_ge(*act_f.at(i - back, "p" + n))
                m0 = k0 - t * P + P
                for j in range(2):
                    nc.tensor.matmul(SC[:, 2 * j:2 * j + 2, k0:k1], identb[:],
                                     band[:, m0:m0 + k1 - k0].unsqueeze(1).broadcast_to([P, 2, k1 - k0]),
                                     start=True, stop=False, skip_group_check=True)
                for h in range(4 * g, 4 * g + 4):
                    r = slice(DH * (h % 2), DH * (h % 2) + DH)
                    mm = nc.tensor.matmul(SC[:, slot(h), k0:k1], f_qkT[r, b, h // 2, t * P:t * P + P],
                                          f_qkT[r, b, 4 + h // 2, k0:k1], start=False, stop=True, skip_group_check=True)
            elif k == "pT":
                t, g, y = a
                pe.wait_ge(*act_f.at(i, f"p{t}{g}"))
                if y:
                    pe.wait_ge(*act_f.at(i, f"pe{t}{g}0"))
                else:
                    n, back = part_before(t, g)
                    pe.wait_ge(*(dve_f.at(i - back, f"pe{n}1") if n[0] == "1" else act_f.at(i - back, f"pe{n}0")))
                for j in range(4):
                    mm = nc.tensor.transpose(PT_PS[:, j * P:j * P + P], f_p[:, t, j, y * P:y * P + P], ident[:])
            elif k == "o":
                t, g = a
                pe.wait_ge(*act_f.at(i, f"pe{t}{g}0"))
                if t:
                    pe.wait_ge(*dve_f.at(i, f"pe{t}{g}1"))
                n, back = part_before(t, g)
                pe.wait_ge(*dve_f.at(i - back, "on" + n))
                for h in range(4 * g, 4 * g + 4):
                    for y in range(t + 1):
                        mm = nc.tensor.matmul(O_PS[:, (h % 4) * (DH + 1):(h % 4 + 1) * (DH + 1)],
                                              f_pT[:, g, 4 * y + slot(h), :], f_v[:, b, y, h, :], start=y == 0, stop=y == t)
            elif k == "oT":
                t, = a
                pe.wait_ge(*dve_f.at(i, f"on{t}1"))
                pe.wait_ge(*(act_f.at(i, "oe0") if t else dve_f.at(i - 1, "z2")))
                for c in range(4):
                    mm = nc.tensor.transpose(bank[1][:, c * P:c * P + P],
                                             f_o[:, b, t, 2 * c:2 * c + 2, :].rearrange("p h d -> p (h d)"), ident[:])
            elif s == "wo":
                pe.wait_ge(*act_f.at(i, "oe1"))
                for t in range(T):
                    for c in range(4):
                        mm = nc.tensor.matmul(bank[1][:, t * P:t * P + P], f_oT[:, c, t * P:t * P + P], fw["wo"][:, c, :],
                                              start=c == 0, stop=c == 3)
            elif s == "sh":
                pe.wait_ge(*dve_f.at(i, "z1"))
                zt = tiles(f_z1[:])
                nc.tensor.matmul(bank[1][:, 0:64], shift[:], zt[:, 0, 64:128], start=True, stop=True)
                nc.tensor.matmul(bank[1][:, 64:128], shift[:], zt[:, 1, 64:128], start=True, stop=False)
                mm = nc.tensor.matmul(bank[1][:, 64:128], carry[:], zt[:, 0, 64:128], start=False, stop=True)
            elif s == "hnT":
                pe.wait_ge(*dve_f.at(i, "hn"))
                for t in range(T):
                    mm = nc.tensor.transpose(bank[1][:, t * P:t * P + P], f_hn[:, t, :], ident[:])
            elif k == "w1a" or k == "w1b" or k == "w1c":
                todo = {"w1a": ((1, 0), (1, 1)), "w1b": ((1, 2), (0, 2)), "w1c": ((0, 0), (0, 1))}[k]
                pe.wait_ge(*{"w1a": act_f.at(i, "he"), "w1b": act_f.at(i, "g0"), "w1c": dve_f.at(i, "u1")}[k])
                for n, (x, c) in enumerate(todo):
                    mm = nc.tensor.matmul(bank[1][0:HR[c], n * L:n * L + L],
                                          fw["w1"][:, x * HID + c * P:x * HID + c * P + HR[c]], f_hnT[:],
                                          start=True, stop=True)
            elif s == "w2":
                pe.wait_ge(*dve_f.at(i, "u0"))
                for t in range(T):
                    for c in range(HC):
                        mm = nc.tensor.matmul(bank[1][:, t * P:t * P + P], f_u[0:HR[c], c, t * P:t * P + P],
                                              fw["w2"][0:HR[c], c, :], start=c == 0, stop=c == HC - 1)
            mm.then_inc(*pe_f.done(s))

        def f_act(act, s, i, b):
            k, a = s.rstrip("0123456789"), [int(x) for x in s[len(s.rstrip("0123456789")):]]
            if k == "sq":
                t, = a
                act.wait_ge(*pe_f.at(i, f"qk{t}"))
                act.wait_ge(*(dve_f.at(i, "ss0") if t else dve_f.at(i - 1, "ss1")))
                op = nc.scalar.activation(f_sq[:], pair[0][:], ACT.Square)
            elif k == "ve":
                t, = a
                act.wait_ge(*pe_f.at(i, f"v{t}"))
                act.wait_ge(*pe_f.at(i - 2, "o11"))
                op = nc.scalar.activation(f_v[:, b, t, :, 0:DH], bank[0][:].rearrange("p (h d) -> p h d", h=H), ACT.Copy)
            elif k == "Te":
                t, x = a
                act.wait_ge(*pe_f.at(i, f"T{t}{x}"))
                act.wait_ge(*pe_f.at(i - 2, "s11"))
                op = nc.scalar.activation(f_qkT[:, b, 4 * x:4 * x + 4, t * P:t * P + P],
                                          bank[0][:].rearrange("p (c k) -> p c k", c=4), ACT.Copy)
            elif k == "p":
                t, g = a
                k0, k1 = KEYS[t]
                act.wait_ge(*dve_f.at(i, f"nm{t}{g}"))
                act.wait_ge(*(pe_f.at(i, f"pT{t}0{t}") if g else pe_f.at(i - 1, f"pT{t}1{t}")))
                for j in range(4):
                    op = nc.scalar.activation(f_p[:, t, j, k0:k1], SC[:, j, k0:k1], ACT.Exp, bias=f_nm[:, g, j:j + 1])
            elif k == "pe":
                t, g, y = a
                act.wait_ge(*pe_f.at(i, "pT" + s[2:]))
                act.wait_ge(*(pe_f.at(i, f"o0{g}") if t else pe_f.at(i - 1, f"o1{g}")))
                op = nc.scalar.activation(f_pT[:, g, 4 * y:4 * y + 4, :], PT_PS.rearrange("p (c k) -> p c k", c=4), ACT.Copy)
            elif k == "oe":
                t, = a
                act.wait_ge(*pe_f.at(i, f"oT{t}"))
                act.wait_ge(*pe_f.at(i - 1, "wo"))
                op = nc.scalar.activation(f_oT[:, :, t * P:t * P + P], bank[1][:].rearrange("p (c k) -> p c k", c=4), ACT.Copy)
            elif s == "hb":
                act.wait_ge(*pe_f.at(i, "sh"))
                nc.scalar.activation(f_hb[:, :, 64:128], bank[1][:, 0:128].rearrange("p (t d) -> p t d", t=T), ACT.Copy)
                op = nc.scalar.activation(f_hb[:, :, 0:64], tiles(f_z1[:])[:, :, 0:64], ACT.Copy)
            elif s == "he":
                act.wait_ge(*pe_f.at(i, "hnT"))
                op = nc.scalar.activation(f_hnT[:], bank[1][:, 0:L], ACT.Identity, bias=fw["lb"][:], scale=fw["lg"][:])
            elif s == "g0" or s == "g1":
                act.wait_ge(*pe_f.at(i, "w1a" if s == "g0" else "w1b"))
                for n, c in ((0, 0), (1, 1)) if s == "g0" else ((0, 2),):
                    op = nc.scalar.activation(f_g[0:HR[c], c, :], bank[1][0:HR[c], n * L:n * L + L], ACT.Gelu,
                                              bias=fw["b1"][0:HR[c], 1, c:c + 1])
            op.then_inc(*act_f.done(s))

        def f_dve(dve, s, i, b, z_at, zdone, tables, before):
            k, a = s.rstrip("0123456789"), [int(x) for x in s[len(s.rstrip("0123456789")):]]
            if s == "zc":
                dve.wait_ge(*pe_f.at(i - 1, "xT"))
                dve.wait_ge(*before)
                dve.wait_ge(*zdone)
                op = nc.vector.tensor_scalar(f_zc[:], seq(Z, z_at), 1.0, None, ALU.mult)
            elif s == "hT":
                dve.wait_ge(*pe_f.at(i, "xT"))
                dve.wait_ge(*pe_f.at(i - 1, "qk1"))
                dve.wait_ge(*pe_f.at(i - 1, "v1"))
                nc.vector.tensor_copy(f_hT[0:64, :], bank[0][0:64, 0:L])
                op = nc.vector.tensor_copy(f_hT[64:128, 1:L], bank[0][64:128, 0:L - 1])
            elif k == "ss":
                t, = a
                dve.wait_ge(*act_f.at(i, f"sq{t}"))
                op = nc.vector.tensor_reduce(f_ss[:], f_sq[:].rearrange("p (h d) -> p h d", h=2 * H), AX.X, ALU.add)
            elif k == "cl":
                t, = a
                dve.wait_ge(*dve_f.at(i, f"ss{t}"))
                dve.wait_ge(*(pool_f.at(i, "rn0") if t else pool_f.at(i - 1, "rn1")))
                op = nc.vector.tensor_scalar(f_cs[:], f_ss[:], 1e-24, None, ALU.max)
            elif k == "kn":
                t, = a
                dve.wait_ge(*pool_f.at(i, f"rn{t}"))
                dve.wait_ge(*pool_f.at(i - 1, f"qb{t}"))
                op = nc.vector.tensor_tensor(f_kn[:, t], QK, f_rn[:].unsqueeze(2).broadcast_to([P, 2 * H, DH]), ALU.mult)
            elif k == "qa":
                t, = a
                dve.wait_ge(*dve_f.at(i, f"kn{t}"))
                dve.wait_ge(f_table, tables)
                dve.wait_ge(*pe_f.at(i - 1, f"T{t}1"))
                op = nc.vector.tensor_tensor(f_qa[:, t].rearrange("p (x h) d -> p x h d", x=2),
                                             f_kn[:, t].rearrange("p (x h) d -> p x h d", x=2),
                                             f_tab[:, t, :, 0].unsqueeze(2).broadcast_to([P, 2, H, DH]), ALU.mult)
            elif k == "nm":
                t, g = a
                k0, k1 = KEYS[t]
                dve.wait_ge(*pe_f.at(i, f"s{t}{g}"))
                dve.wait_ge(*(act_f.at(i, f"p0{g}") if t else act_f.at(i - 1, f"p1{g}")))
                op = nc.vector.tensor_reduce(f_nm[:, g, :], SC[:, :, k0:k1], AX.X, ALU.max, negate=True)
            elif k == "pe":
                t, g, y = a
                dve.wait_ge(*pe_f.at(i, "pT" + s[2:]))
                dve.wait_ge(*(pe_f.at(i, f"o0{g}") if t else pe_f.at(i - 1, f"o1{g}")))
                op = nc.vector.tensor_copy(f_pT[:, g, 4 * y:4 * y + 4, :], PT_PS.rearrange("p (c k) -> p c k", c=4))
            elif k == "rs":
                dve.wait_ge(*pe_f.at(i, "o" + s[2:]))
                op = nc.vector.reciprocal(f_rs[:], O_PS[:, 0:4 * (DH + 1)].rearrange("p (h d) -> p h d", h=4)[:, :, DH])
            elif k == "on":
                t, g = a
                dve.wait_ge(*dve_f.at(i, "rs" + s[2:]))
                dve.wait_ge(*pe_f.at(i - 2, f"oT{t}"))
                op = nc.vector.tensor_tensor(f_o[:, b, t, 4 * g:4 * g + 4, :],
                                             O_PS[:, 0:4 * (DH + 1)].rearrange("p (h d) -> p h d", h=4)[:, :, 0:DH],
                                             f_rs[:].unsqueeze(2).broadcast_to([P, 4, DH]), ALU.mult)
            elif s == "z1":
                dve.wait_ge(*pe_f.at(i, "wo"))
                dve.wait_ge(*pool_f.at(i - 1, "zb"))
                dve.wait_ge(*act_f.at(i - 1, "hb"))
                op = nc.vector.tensor_tensor(f_z1[:], seq(Z, z_at), bank[1][:, 0:L], ALU.add)
            elif s == "st":
                dve.wait_ge(*act_f.at(i, "hb"))
                for t in range(T):
                    op = nc.vector.bn_stats(f_st[:, t, :], f_hb[:, t, :])
            elif s == "mv":
                dve.wait_ge(*dve_f.at(i, "st"))
                dve.wait_ge(*pool_f.at(i - 1, "vv"))
                nc.vector.tensor_copy(carrier[:], eps[:, 0:1])
                for t in range(T):
                    op = nc.vector.bn_aggr(f_mv[:, t, :], f_st[:, t, :])
            elif s == "hn":
                dve.wait_ge(*pool_f.at(i, "rv"))
                dve.wait_ge(*pe_f.at(i - 1, "hnT"))
                for t in range(T):
                    op = nc.vector.tensor_scalar(f_hn[:, t, :], f_hb[:, t, :], f_mv[:, t, 0:1], f_rv[:, t:t + 1],
                                                 ALU.subtract, ALU.mult)
            elif s == "u0" or s == "u1":
                dve.wait_ge(*(act_f.at(i, "g1") if s == "u1" else pe_f.at(i, "w1c")))
                for n, c in ((0, 0), (1, 1)) if s == "u0" else ((1, 2),):
                    r = HR[c]
                    op = nc.vector.scalar_tensor_tensor(out=f_u[0:r, c, :], in0=bank[1][0:r, n * L:n * L + L],
                                                        scalar=fw["b1"][0:r, 0, c:c + 1], in1=f_g[0:r, c, :],
                                                        op0=ALU.add, op1=ALU.mult)
            elif s == "z2":
                dve.wait_ge(*pe_f.at(i, "w2"))
                dve.wait_ge(*pool_f.at(i, "zb"))
                op = nc.vector.tensor_tensor(seq(Z, z_at), f_zb[:], bank[1][:, 0:L], ALU.add)
            op.then_inc(*dve_f.done(s))

        def f_pool(pool, s, i, b):
            k, a = s.rstrip("0123456789"), [int(x) for x in s[len(s.rstrip("0123456789")):]]
            if k == "rn":
                t, = a
                pool.wait_ge(*dve_f.at(i, f"cl{t}"))
                pool.wait_ge(*(dve_f.at(i, "kn0") if t else dve_f.at(i - 1, "kn1")))
                op = nc.gpsimd.tensor_tensor(f_rn[:], f_cs[:], mhalf[:], ALU.pow)
            elif k == "qb":
                t, = a
                pool.wait_ge(*dve_f.at(i, f"kn{t}"))
                pool.wait_ge(*pe_f.at(i - 1, f"T{t}1"))
                for e in range(2):
                    o = slice(32 * e, 32 * e + 32)
                    op = nc.gpsimd.tensor_tensor(
                        f_qb[:, t, :, o].rearrange("p (x h) d -> p x h d", x=2),
                        f_kn[:, t, :, 32 - 32 * e:64 - 32 * e].rearrange("p (x h) d -> p x h d", x=2),
                        f_tab[:, t, :, 1, o].unsqueeze(2).broadcast_to([P, 2, H, 32]), ALU.mult)
            elif s == "vv":
                pool.wait_ge(*dve_f.at(i, "mv"))
                op = nc.gpsimd.tensor_tensor(f_ve[:], f_mv[:, :, 1], eps[:], ALU.add)
            elif s == "rv":
                pool.wait_ge(*pool_f.at(i, "vv"))
                op = nc.gpsimd.tensor_tensor(f_rv[:], f_ve[:], mhalf[:, 0:T], ALU.pow)
            elif s == "zb":
                pool.wait_ge(*dve_f.at(i, "z1"))
                pool.wait_ge(*dve_f.at(i - 1, "z2"))
                op = nc.gpsimd.tensor_tensor(tiles(f_zb[:]), tiles(f_z1[:]),
                                             fw["b2"][:].unsqueeze(1).broadcast_to([P, T, D]), ALU.add)
            op.then_inc(*pool_f.done(s))

        def p_head(g, j):
            return 4 * (2 * (g // 2) + j % 2) + 2 * (g % 2) + j // 2

        def p_before(stages, i, step, t, g, back):
            n = PG * t + g - back
            return stages.at(i if n >= 0 else i - 1, f"{step}{n % (T * PG) // PG}{n % PG}")

        P_LAST = f"{T - 1}{PG - 1}"

        def p_pe(pe, s, i, b):
            k, a = s.rstrip("0123456789"), [int(x) for x in s[len(s.rstrip("0123456789")):]]
            if s == "xT":
                pe.wait_ge(*dve_p.at(i, "zc"))
                pe.wait_ge(*dve_p.at(i - 1, "kc1"))
                for t in range(T):
                    mm = nc.tensor.transpose(bank[0][:, t * P:t * P + P], p_zc[:, t * P:t * P + P], ident[:])
            elif s == "g":
                pe.wait_ge(*act_p.at(i, "xTe"))
                mm = nc.tensor.matmul(bank[0][0:PH, 0:L], pw["wg"][:], p_xT[:], start=True, stop=True)
            elif s == "hgT":
                pe.wait_ge(*dve_p.at(i, "hg"))
                for t in range(T):
                    mm = nc.tensor.matmul(bank[0][:, t * PH:t * PH + PH], p_hg[:, t * P:t * P + P], ident[0:PH, 0:PH],
                                          start=True, stop=True)
            elif s == "v":
                pe.wait_ge(*dve_p.at(i, "he"))
                for t in range(T):
                    mm = nc.tensor.matmul(bank[0][:, t * P:t * P + P], p_xT[:, t * P:t * P + P], pw["wv"][:],
                                          start=True, stop=True)
            elif k == "q" or k == "k":
                y, = a
                pe.wait_ge(*{"q0": dve_p.at(i, "vc"), "q1": act_p.at(i, "qc0"), "k0": act_p.at(i, "qc1"),
                             "k1": dve_p.at(i, "kc0")}[s])
                for g in range(2):
                    mm = nc.tensor.matmul(bank[0][:, g * L:g * L + L], pw["wqk"][:, "qk".index(k), 2 * y + g, :], p_xT[:],
                                          start=True, stop=True)
            elif k == "bc":
                t, g = a
                n = P * (t + 1)
                pe.wait_ge(*dve_p.at(i, "lo"))
                pe.wait_ge(*p_before(act_p, i, "e", t, g, 1))
                for j in range(4):
                    o = pair[0][:, j * L:j * L + n]
                    nc.tensor.matmul(o, sel[:, p_head(g, j), :], p_g3[:, b, 0:n], start=True, stop=False,
                                     skip_group_check=True)
                    mm = nc.tensor.matmul(o[:, n - P:n], identb[:], tri[:], start=False, stop=True, skip_group_check=True)
            elif k == "s":
                t, g = a
                n = P * (t + 1)
                pe.wait_ge(*dve_p.at(i, "kc1"))
                pe.wait_ge(*p_before(act_p, i, "ab", t, g, 1))
                for j in (0, 2, 1, 3):
                    h = p_head(g, j)
                    r0 = 32 * (h % 4)
                    mm = nc.tensor.matmul(pair[1][:, j * L:j * L + n], p_qT[r0:r0 + PS, b, h // 4, t * P:t * P + P],
                                          p_kT[r0:r0 + PS, b, h // 4, 0:n], start=True, stop=True, tile_position=(r0, 0))
            elif k == "pT":
                t, g = a
                pe.wait_ge(*act_p.at(i, f"p{t}{g}"))
                pe.wait_ge(*p_before(dve_p, i, "pe", t, g, 1))
                for j in range(4):
                    for y in range(t + 1):
                        mm = nc.tensor.transpose(pair[2][:, (4 * y + j) * P:(4 * y + j) * P + P],
                                                 p_p[:, g % 2, j, y * P:y * P + P], ident[:])
            elif k == "o":
                t, g = a
                pe.wait_ge(*dve_p.at(i, f"pe{t}{g}"))
                if (t, g) == (0, 0):
                    pe.wait_ge(*dve_p.at(i - 1, "y"))
                for j in range(4):
                    h = p_head(g, j)
                    for y in range(t + 1):
                        mm = nc.tensor.matmul(bank[1][:, (t * PH + h) * (PS + 1):(t * PH + h + 1) * (PS + 1)],
                                              p_pT[:, g % 2, 4 * y + j, :], p_v[:, b, y, h, :], start=y == 0, stop=y == t)
            mm.then_inc(*pe_p.done(s))

        def p_act(act, s, i, b):
            k, a = s.rstrip("0123456789"), [int(x) for x in s[len(s.rstrip("0123456789")):]]
            if s == "xTe":
                act.wait_ge(*pe_p.at(i, "xT"))
                act.wait_ge(*pe_p.at(i - 1, "v"))
                act.wait_ge(*pe_p.at(i - 1, "k1"))
                op = nc.scalar.activation(p_xT[:], bank[0][:, 0:L], ACT.Copy)
            elif s == "abs":
                act.wait_ge(*pe_p.at(i, "g"))
                op = nc.scalar.activation(p_t[:, 0], bank[0][0:PH, 0:L], ACT.Abs)
            elif s == "exp":
                act.wait_ge(*act_p.at(i, "abs"))
                op = nc.scalar.activation(p_t[:, 1], p_t[:, 0], ACT.Exp, scale=-1.0)
            elif s == "ln":
                act.wait_ge(*act_p.at(i, "exp"))
                act.wait_ge(*dve_p.at(i - 1, "lg"))
                op = nc.scalar.activation(p_t[:, 2], p_t[:, 1], ACT.Ln, bias=ones[0:PH, 0:1])
            elif k == "qc":
                y, = a
                act.wait_ge(*pe_p.at(i, f"q{y}"))
                act.wait_ge(*pe_p.at(i - 2, "s" + P_LAST))
                op = nc.scalar.activation(p_qT[:, b, 2 * y:2 * y + 2], bank[0][:].rearrange("p (g l) -> p g l", g=2), ACT.Copy)
            elif k == "e":
                t, g = a
                n = P * (t + 1)
                act.wait_ge(*pe_p.at(i, f"bc{t}{g}"))
                act.wait_ge(*dve_p.at(i, "he"))
                act.wait_ge(*p_before(dve_p, i, "u", t, g, 2))
                for j in range(4):
                    h = p_head(g, j)
                    op = nc.scalar.activation(p_e[:, g % 2, j, 0:n], pair[0][:, j * L:j * L + n], ACT.Exp, scale=-1.0,
                                              bias=p_hgT[:, b, t, h:h + 1])
            elif k == "ab":
                t, g = a
                n = P * (t + 1)
                act.wait_ge(*pe_p.at(i, f"s{t}{g}"))
                act.wait_ge(*p_before(dve_p, i, "u", t, g, 2))
                op = nc.scalar.activation(p_a[:, g % 2, :, 0:n], pair[1][:].rearrange("p (j l) -> p j l", j=4)[:, :, 0:n],
                                          ACT.Abs)
            elif k == "p":
                t, g = a
                n = P * (t + 1)
                act.wait_ge(*dve_p.at(i, f"rm{t}{g}"))
                act.wait_ge(*p_before(pe_p, i, "pT", t, g, 2))
                for j in range(4):
                    op = nc.scalar.activation(p_p[:, g % 2, j, 0:n], p_s[:, g % 2, j, 0:n], ACT.Square,
                                              scale=p_rm[:, g % 2, j:j + 1])
            op.then_inc(*act_p.done(s))

        def p_dve(dve, s, i, b, z_at):
            k, a = s.rstrip("0123456789"), [int(x) for x in s[len(s.rstrip("0123456789")):]]
            if s == "zc":
                dve.wait_ge(dve_ln.sem, dve_ln(3 * NSEQ, "z"))
                dve.wait_ge(*pe_p.at(i - 1, "xT"))
                op = nc.vector.tensor_scalar(p_zc[:], seq(Z, z_at), 1.0, None, ALU.mult)
            elif s == "min":
                dve.wait_ge(*act_p.at(i, "abs"))
                dve.wait_ge(*dve_p.at(i - 1, "hg"))
                op = nc.vector.tensor_scalar(p_t[:, 3], bank[0][0:PH, 0:L], 0.0, None, ALU.min)
            elif s == "lg":
                dve.wait_ge(*act_p.at(i, "ln"))
                dve.wait_ge(*dve_p.at(i, "min"))
                op = nc.vector.tensor_tensor(p_t[:, 4], p_t[:, 3], p_t[:, 2], ALU.subtract)
            elif s == "cum":
                dve.wait_ge(*dve_p.at(i, "lg"))
                op = nc.vector.tensor_tensor_scan(p_t[:, 3], ones[0:PH, :], p_t[:, 4], 0.0, ALU.mult, ALU.add)
            elif s == "hg":
                dve.wait_ge(*dve_p.at(i, "cum"))
                dve.wait_ge(*pe_p.at(i - 1, "hgT"))
                op = nc.vector.tensor_scalar(p_hg[:], p_t[:, 3], 0.5, None, ALU.mult)
            elif s == "hi":
                dve.wait_ge(*dve_p.at(i, "hg"))
                dve.wait_ge(*pe_p.at(i - 2, "bc" + P_LAST))
                op = nc.vector.tensor_copy(p_g3[0:PH, b], p_hg[:])
            elif s == "r1":
                dve.wait_ge(*dve_p.at(i, "hi"))
                op = nc.vector.tensor_tensor(p_t[:, 4], p_hg[:], p_g3[0:PH, b], ALU.subtract)
            elif s == "mid":
                dve.wait_ge(*dve_p.at(i, "r1"))
                op = nc.vector.tensor_copy(p_mid[:], p_t[:, 4])
            elif s == "mid2":
                dve.wait_ge(*dve_p.at(i, "r1"))
                op = nc.vector.tensor_copy(p_g3[32:32 + PH, b], p_t[:, 4])
            elif s == "lo":
                dve.wait_ge(*dve_p.at(i, "mid"))
                op = nc.vector.tensor_tensor(p_g3[64:64 + PH, b], p_t[:, 4], p_mid[:], ALU.subtract)
            elif s == "he":
                dve.wait_ge(*pe_p.at(i, "hgT"))
                dve.wait_ge(*act_p.at(i - 2, "e" + P_LAST))
                op = nc.vector.tensor_copy(p_hgT[:, b], bank[0][:, 0:T * PH].rearrange("p (t h) -> p t h", t=T))
            elif s == "vc":
                dve.wait_ge(*pe_p.at(i, "v"))
                dve.wait_ge(*pe_p.at(i - 2, "o" + P_LAST))
                for t in range(T):
                    op = nc.vector.tensor_copy(p_v[:, b, t, :, 0:PS],
                                               bank[0][:, t * P:t * P + P].rearrange("p (h d) -> p h d", h=PH))
            elif k == "kc":
                y, = a
                dve.wait_ge(*pe_p.at(i, f"k{y}"))
                dve.wait_ge(*pe_p.at(i - 2, "s" + P_LAST))
                op = nc.vector.tensor_copy(p_kT[:, b, 2 * y:2 * y + 2], bank[0][:].rearrange("p (g l) -> p g l", g=2))
            elif k == "u":
                t, g = a
                n = P * (t + 1)
                dve.wait_ge(*act_p.at(i, f"e{t}{g}"))
                dve.wait_ge(*act_p.at(i, f"ab{t}{g}"))
                dve.wait_ge(*p_before(act_p, i, "p", t, g, 2))
                op = nc.vector.scalar_tensor_tensor(out=p_s[:, g % 2, :, 0:n], in0=p_a[:, g % 2, :, 0:n], scalar=1e-7,
                                                    in1=p_e[:, g % 2, :, 0:n], op0=ALU.add, op1=ALU.mult)
            elif k == "m":
                t, g = a
                dve.wait_ge(*dve_p.at(i, f"u{t}{g}"))
                op = nc.vector.tensor_reduce(p_m[:, g % 2], p_s[:, g % 2, :, 0:P * (t + 1)], AX.X, ALU.max)
            elif k == "rm":
                t, g = a
                dve.wait_ge(*dve_p.at(i, f"m{t}{g}"))
                dve.wait_ge(*p_before(act_p, i, "p", t, g, 2))
                op = nc.vector.reciprocal(p_rm[:, g % 2], p_m[:, g % 2])
            elif k == "pe":
                t, g = a
                n = 4 * (t + 1)
                dve.wait_ge(*pe_p.at(i, f"pT{t}{g}"))
                dve.wait_ge(*p_before(pe_p, i, "o", t, g, 2))
                op = nc.vector.tensor_copy(p_pT[:, g % 2, 0:n, :], pair[2][:, 0:n * P].rearrange("p (c k) -> p c k", c=n))
            elif s == "rn":
                dve.wait_ge(*pe_p.at(i, "o" + P_LAST))
                op = nc.vector.reciprocal(p_rn[:], bank[1][:, 0:T * PH * (PS + 1)]
                                          .rearrange("p (t h d) -> p t h d", t=T, h=PH)[:, :, :, PS])
            elif s == "y":
                dve.wait_ge(*dve_p.at(i, "rn"))
                dve.wait_ge(*pool_p.at(i - 1, "x"))
                op = nc.vector.tensor_tensor(p_y[:], bank[1][:, 0:T * PH * (PS + 1)]
                                             .rearrange("p (t h d) -> p t h d", t=T, h=PH)[:, :, :, 0:PS],
                                             p_rn[:].unsqueeze(3).broadcast_to([P, T, PH, PS]), ALU.mult)
            op.then_inc(*dve_p.done(s))

        def p_pool(pool, s, i, b, x_at):
            pool.wait_ge(*dve_p.at(i, "y"))
            nc.gpsimd.tensor_tensor(seq(X, x_at), seq(X, x_at), p_y[:].rearrange("p t h d -> p (t h d)"),
                                    ALU.add).then_inc(*pool_p.done(s))

        block = ctx.enter_context(nc.Block())
        NF = len(fw)

        def weights_of_layer(name, layer):
            return ins["f_" + name][layer]

        FCALLS = [0, 1] if PHASES >= 4 else ([0] if PHASES >= 2 else [])

        @block.sync
        def _(sp):
            for t, name in consts:
                sp.dma_start(t, ins[name]).then_inc(loaded, 16)
            xv = ins["x"].rearrange("b (t p) d -> p b t d", p=P)
            for c in range(4):
                n = NSEQ // 4
                for b in range(n * c, n * c + n):
                    sp.dma_start(tiles(X[:, b, :]), xv[:, b]).then_inc(x_loaded, 16)
            for call in FCALLS:
                with sp.Fori(0, 2) as layer:
                    w = call * 2 * NSEQ
                    sp.wait_ge(*dve_f.at(layer * NSEQ + w, "z2"))
                    for name, t in fw.items():
                        sp.dma_start(t[:], weights_of_layer(name, layer)).then_inc(f_loaded, 16)
            ov = out.rearrange("b (t p) d -> p b t d", p=P)
            sp.wait_ge(x_done, NSEQ * max(1, len(FCALLS)))
            for b in range(NSEQ):
                sp.dma_start(ov[:, b], tiles(X[:, b, :])).then_inc(stored, 16)
            sp.wait_ge(stored, 16 * NSEQ)

        NC = len(consts)

        @block.tensor
        def _(pe):
            credit(pe, pe_m, pe_f, pe_p)
            pe.wait_ge(loaded, 16 * NC)
            run_windows(pe, pe_m, lambda s, i, b: m_pe(pe, s, i, b), NSEQ)
            for call in FCALLS:
                if call:
                    run_windows(pe, pe_p, lambda s, i, b: p_pe(pe, s, i, b), NSEQ)
                with pe.Fori(0, 2) as layer:
                    base, loads = (call * 2 + layer) * NSEQ, (call * 2 + layer + 1) * 16 * NF
                    run_windows(pe, pe_f, lambda s, i, b: f_pe(pe, s, base + i, b, loads), NSEQ)

        @block.scalar
        def _(act):
            credit(act, act_m, act_f, act_p)
            act.wait_ge(loaded, 16 * NC)
            act.wait_ge(const_set, 11)
            nc.scalar.activation(m_A[:], mw["A_log"][:], ACT.Exp).then_inc(const_set, 1)
            act.wait_ge(dve_ln.sem, dve_ln(NSEQ, "z"))
            run_windows(act, act_m, lambda s, i, b: m_act(act, s, i, b, i), NSEQ)
            for call in FCALLS:
                if call:
                    run_windows(act, act_p, lambda s, i, b: p_act(act, s, i, b), NSEQ)
                with act.Fori(0, 2) as layer:
                    base = (call * 2 + layer) * NSEQ
                    run_windows(act, act_f, lambda s, i, b: f_act(act, s, base + i, b), NSEQ)

        @block.vector
        def _(dve):
            credit(dve, dve_m, dve_ln, dve_f, dve_p)
            dve.wait_ge(loaded, 16 * NC)
            dve.wait_ge(const_set, 12)
            nc.vector.tensor_scalar(m_A[:], m_A[:], -1.0, None, ALU.mult).then_inc(const_set, 1)
            with dve.Fori(1, NSEQ + 1) as i:
                ln_dve(dve, i, 0, (x_loaded, 16 * NSEQ), 0)
            run_windows(dve, dve_m, lambda s, i, b: m_dve(dve, s, i, b, i), NSEQ)
            with dve.Fori(1, NSEQ + 1) as i:
                ln_dve(dve, i, 1, dve_m.at(NSEQ, "x"), 0)
            for call in FCALLS:
                if call:
                    run_windows(dve, dve_p, lambda s, i, b: p_dve(dve, s, i, b, i), NSEQ)
                    with dve.Fori(1, NSEQ + 1) as i:
                        ln_dve(dve, i, 3, pool_p.at(NSEQ, "x"), 0)
                with dve.Fori(0, 2) as layer:
                    dve.wait_ge(f_loaded, (call * 2 + layer + 1) * 16 * NF)
                    for t in range(T):
                        for x in range(2):
                            qs = fw["qs"][:, x, :]
                            nc.vector.tensor_tensor(f_tab[:, t, x, 0], rot[:, t, x, 0], qs, ALU.mult)
                            for e in range(2):
                                o = slice(32 * e, 32 * e + 32)
                                ins_ = nc.vector.tensor_tensor(f_tab[:, t, x, 1, o], rot[:, t, x, 1, o],
                                                               qs[:, 32 - 32 * e:64 - 32 * e], ALU.mult)
                    ins_.then_inc(f_table, 1)
                    base = (call * 2 + layer) * NSEQ
                    zdone, tables = (dve_ln.sem, dve_ln((2 + 2 * call) * NSEQ, "z")), call * 2 + layer + 1
                    run_windows(dve, dve_f, lambda s, i, b: f_dve(dve, s, base + i, b, i, zdone, tables,
                                                                  dve_f.at(base, "z2")), NSEQ)
                dve.wait_ge(*dve_f.at((call + 1) * 2 * NSEQ, "z2"))
                with dve.Fori(1, NSEQ + 1) as i:
                    nc.vector.tensor_tensor(seq(X, i), seq(X, i), seq(Z, i), ALU.add).then_inc(x_done, 1)
                if call == 0 and PHASES > 2:
                    with dve.Fori(1, NSEQ + 1) as i:
                        ln_dve(dve, i, 2, (x_done, NSEQ), 0)
            if not FCALLS:
                dve.wait_ge(dve_ln.sem, dve_ln.all(2 * NSEQ))
                dve.drain().then_inc(x_done, NSEQ)

        @block.gpsimd
        def _(pool):
            credit(pool, pool_m, pool_ln, pool_f, pool_p)
            nc.gpsimd.memset(ones[:], 1.0).then_inc(const_set, 1)
            nc.gpsimd.memset(mhalf[:], -0.5).then_inc(const_set, 1)
            nc.gpsimd.memset(m_pad[:, :, 0:CONV - 1], 0.0).then_inc(const_set, 1)
            nc.gpsimd.memset(m_a[:, :, :, :, 0:1], 0.0).then_inc(const_set, 1)
            nc.gpsimd.memset(f_hT[:, 0:1], 0.0).then_inc(const_set, 1)
            nc.gpsimd.memset(f_v[:, :, :, :, DH:DH + 1].rearrange("p b t h d -> p (b t) h d"), 1.0).then_inc(const_set, 1)
            nc.gpsimd.memset(f_p[:], 0.0).then_inc(const_set, 1)
            nc.gpsimd.memset(p_v[:, :, :, :, PS:PS + 1].rearrange("p b t h d -> p (b t) h d"), 1.0).then_inc(const_set, 1)
            nc.gpsimd.memset(p_g3[:], 0.0).then_inc(const_set, 1)
            nc.gpsimd.memset(eps[:], LN_EPS).then_inc(const_set, 1)
            nc.gpsimd.memset(eps_sum[:], LN_EPS * D).then_inc(const_set, 1)
            pool.wait_ge(const_set, 11)
            with pool.Fori(1, NSEQ + 1) as i:
                ln_pool(pool, i, 0)
            run_windows(pool, pool_m, lambda s, i, b: m_pool(pool, s, i, b, i), NSEQ)
            with pool.Fori(1, NSEQ + 1) as i:
                ln_pool(pool, i, 1)
            for call in FCALLS:
                if call:
                    run_windows(pool, pool_p, lambda s, i, b: p_pool(pool, s, i, b, i), NSEQ)
                    with pool.Fori(1, NSEQ + 1) as i:
                        ln_pool(pool, i, 3)
                with pool.Fori(0, 2) as layer:
                    base = (call * 2 + layer) * NSEQ
                    run_windows(pool, pool_f, lambda s, i, b: f_pool(pool, s, base + i, b), NSEQ)
                if call == 0 and PHASES > 2:
                    with pool.Fori(1, NSEQ + 1) as i:
                        ln_pool(pool, i, 2)


def shape_constants(np, bf16):
    k = np.arange(P)
    big = 1e30
    sel = np.zeros((96, 32, P), np.float32)
    for r in range(96):
        sel[r, r % 32, :] = 1
    kk = np.arange(L)
    band = np.where((kk[None] > k[:, None] + P) | (kk[None] < k[:, None] + P - W), -big, 0.0)
    tri = np.where(k[None] > k[:, None], big, 0.0)
    half_idx = np.arange(0, DH, 2, dtype=np.float32)
    inv = (1.0 / np.float32(10000.0) ** (half_idx / np.float32(DH))).astype(np.float32)
    t = np.arange(L, dtype=np.float32)
    f = t[:, None] * inv[None]
    f = np.concatenate([f, f], -1)
    base = (half_idx + np.float32(0.4 * DH)) / np.float32(1.4 * DH)
    power = (t - L // 2) / np.float32(W // 2)
    scale = (base[None] ** power[:, None]).astype(np.float32)
    scale = np.concatenate([scale, scale], -1)
    cos, sin = np.cos(f), np.sin(f)
    sgn = np.concatenate([-np.ones(DH // 2), np.ones(DH // 2)])
    rot = np.stack([np.stack([8 * cos * scale, 8 * sin * scale * sgn], 1),
                    np.stack([cos / scale, sin / scale * sgn], 1)], 1)
    rot = rot.reshape(T, P, 2, 2, DH).transpose(1, 0, 2, 3, 4)
    f32 = np.float32
    return {"ident": np.eye(P, dtype=f32), "identb": np.eye(P, dtype=f32).astype(bf16), "sel": sel.astype(bf16),
            "band": band.astype(f32).astype(bf16), "tri": tri.astype(f32).astype(bf16),
            "shift": np.eye(P, k=1, dtype=f32), "carry": np.where((k[:, None] == P - 1) & (k[None] == 0), 1, 0).astype(f32),
            "rot": np.ascontiguousarray(rot.astype(f32))}


def lay_out(np, a):
    def chunks(w):
        return w.reshape(-1, P, w.shape[-1]).transpose(1, 0, 2)

    def col(v):
        return v.reshape(-1, P).T

    m, f = "L0_attn_a_", "L0_ffn_"
    out = {"x": a[m + "resid"]}
    out["m_in_w"] = a[m + "in_w"].T
    out["m_skip_w"] = a[m + "skip_w"].T
    out["m_wd1"] = chunks(a[m + "wd1"].T)
    out["m_wbc"] = chunks(np.concatenate([a[m + "wb"], a[m + "wc"]], 0).T)
    out["m_wd2"] = a[m + "wd2"].T
    out["m_out_w"] = chunks(a[m + "out_w"].T)
    out["m_norm_w"] = a[m + "norm_w"][:, None]
    out["m_conv_w"] = chunks(a[m + "conv_w"][:, 0, :])
    out["m_conv_b"] = col(a[m + "conv_b"])
    out["m_wd2_b"] = col(a[m + "wd2_b"])
    out["m_A_log"] = chunks(a[m + "A_log"])
    out["m_W_D"] = col(a[m + "W_D"])
    w = a["L0_attn_b_W"]
    qk = np.zeros((P, 2, PG, P), w.dtype)
    for x in range(2):
        for h in range(PH):
            qk[:, x, h // 4, 32 * (h % 4):32 * (h % 4) + PS] = w[x * D + h * PS:x * D + (h + 1) * PS].T
    out["p_wqk"] = qk
    out["p_wv"] = w[2 * D:3 * D].T
    out["p_wg"] = w[3 * D:].T
    out["f_wqkv"] = a[f + "wqkv"]
    out["f_wo"] = np.stack([chunks(x) for x in a[f + "wo"]])
    out["f_w1"] = a[f + "w1"]
    pad = np.zeros((2, HC * P - HID, D), w.dtype)
    out["f_w2"] = np.stack([chunks(x) for x in np.concatenate([a[f + "w2"], pad], 1)])
    out["f_b2"] = np.broadcast_to(a[f + "b2"][:, None, :], (2, P, D))
    qs = np.stack([a[f + "q_scale"], a[f + "k_scale"]], 1)
    out["f_qs"] = np.broadcast_to(qs[:, None], (2, P, 2, DH))
    out["f_lg"] = a[f + "ln_g"][:, :, None]
    out["f_lb"] = a[f + "ln_b"][:, :, None]
    b1 = a[f + "b1"].reshape(2, 2, HID)
    b1 = np.concatenate([b1, np.zeros((2, 2, HC * P - HID), b1.dtype)], -1)
    out["f_b1"] = b1.reshape(2, 2, HC, P).transpose(0, 3, 1, 2)
    return out


def kernel(**inputs):
    import numpy as np
    import concourse.bacc as bacc
    from concourse import mybir as mb
    from concourse.bass_utils import run_bass_kernel_spmd as run

    nc = bacc.Bacc("TRN2", target_bir_lowering=False, num_devices=1)
    arrays = lay_out(np, {k: np.asarray(v) for k, v in inputs.items()})
    arrays.update(shape_constants(np, mb.dt.np(mb.dt.bfloat16)))
    feeds, ins = {}, {}
    for name, v in arrays.items():
        v = np.ascontiguousarray(v)
        feeds[f"in_{name}"] = v
        ins[name] = nc.dram_tensor(f"in_{name}", v.shape, mb.dt.from_np(v.dtype), kind="ExternalInput").ap()
    out = nc.dram_tensor("out_x", (NSEQ, L, D), F32, kind="ExternalOutput").ap()
    build(nc, ins, out)
    r = run(nc, [feeds], core_ids=[0])
    return r.results[0]["out_x"]
```

```python
from contextlib import ExitStack

import concourse.bass as bass
from concourse import mybir

P = 128
F32 = mybir.dt.float32
BF16 = mybir.dt.bfloat16
ALU = mybir.AluOpType
ACT = mybir.ActivationFunctionType
AX = mybir.AxisListType

NSEQ, L, D = 16, 256, 128
T = L // P
E, NS, DD, CONV = 256, 16, 64, 4
EC = E // P
GN = 2
NG = NS // GN
H, DH, W = 8, 64, 64
INNER = H * DH
HID = int(D * 4 * 2 / 3)
HC = (HID + P - 1) // P
HR = [min(P, HID - c * P) for c in range(HC)]
PH, PS = 16, 8
PG = PH // 4
LN_EPS = 1e-5
AHEAD = 2
LN_PARTS = 2
LN_PART = NSEQ // LN_PARTS
CALLS = 2


class Stream:

    def __init__(self, sem, steps):
        self.sem, self.steps = sem, steps
        self.index = {s: n for n, s in enumerate(steps)}
        assert len(self.index) == len(steps)
        self.at = 0
        self.credit = AHEAD * len(steps)

    def __call__(self, i, step):
        return (i + (AHEAD - 1)) * len(self.steps) + (self.index[step] + 1)

    def all(self, i):
        return (i + AHEAD) * len(self.steps)

    def done(self, step):
        assert self.steps[self.at % len(self.steps)] == step, (self.steps[self.at % len(self.steps)], step)
        self.at += 1
        return self.sem, 1


class Stages:

    def __init__(self, new_sem, name, order, stages):
        self.order = order.split()
        self.stage = {s: n for n, st in enumerate(stages) for s in st.split()}
        self.streams = [Stream(new_sem(f"{name}_{n}"), mine) if mine else None for n, mine in
                        enumerate([[s for s in self.order if self.stage[s] == n] for n in range(len(stages))])]

    def at(self, i, step):
        stream = self.streams[self.stage[step]]
        return stream.sem, stream(i, step)

    def done(self, step):
        return self.streams[self.stage[step]].done(step)


def run_windows(eng, stages, step, count):
    n = 1 + max(stages.stage.values())

    def window(k, parity, live):
        for s in stages.order:
            lag = stages.stage[s]
            if lag in live:
                step(s, k - lag, (parity - lag) % 2)

    odd = (count - n + 1) % 2
    for k in range(1, n + odd):
        window(k, k % 2, range(min(k, n)))
    with eng.Fori(0, (count - n + 1) // 2) as p:
        for b in range(2):
            window(2 * p + (n + odd + b), (n + odd + b) % 2, range(n))
    for k in range(count + 1, count + n):
        window(k, k % 2, range(k - count, n))


F_STAGES = [
    "zc xT hT qk0 v0 sq0 ve0 v1 ve1 ss0 cl0 rn0 kn0 qa0 qb0 qs0 qk1 sq1 ss1 cl1 rn1 kn1 qa1 qb1 qs1 T00 "
    "Te00 T01 Te01 T10 Te10 T11 Te11",
    "s00 nm00 p00 pT000 pe000 o00 rs00 on00 s01 nm01 p01 pT010 pe010 o01 rs01 on01 s10 nm10 p10 pT100 "
    "pe100 pT101 pe101 o10 rs10 on10 s11 nm11 p11 pT110 pe110 pT111 pe111 o11 rs11 on11",
    "oT0 oe0 oT1 oe1 wo z1 sh hb st mv vv rv zb hn hnT he w1a g0 w1b g1 u1 w1c u0 w2 z2"]
F_ORDER = {
    "dve": "zc hT nm00 z1 ss0 cl0 nm01 rs00 st mv kn0 nm10 qa0 hn on00 ss1 cl1 nm11 pe101 rs01 on01 qs0 kn1 qa1 "
        "u1 rs10 on10 pe111 qs1 u0 rs11 on11 z2",
    "pe": "oT0 xT s00 oT1 qk0 wo pT000 v0 s01 sh o00 v1 s10 pT010 qk1 pT100 s11 pT101 hnT o01 w1a pT110 o10 w1b "
        "pT111 T00 w1c T01 o11 T10 w2 T11",
    "act": "oe0 oe1 p00 sq0 ve0 pe000 hb p01 pe010 p10 sq1 ve1 pe100 he p11 g0 pe110 g1 Te00 Te01 Te10 Te11",
    "pool": "rn0 vv rv qb0 rn1 qb1 zb"}

P_STAGES = [
    "zc xT xTe g abs min exp ln lg cum hg hi r1 mid mid2 lo hgT he v vc q0 qc0 q1 qc1 k0 kc0 k1 kc1",
    "bc00 e00 s00 ab00 u00 m00 rm00 p00 pT00 pe00 o00 bc01 e01 s01 ab01 u01 m01 rm01 p01 pT01 pe01 o01 "
    "bc02 e02 s02 ab02 u02 m02 rm02 p02 pT02 pe02 o02 bc03 e03 s03 ab03 u03 m03 rm03 p03 pT03 pe03 o03 "
    "bc10 e10 s10 ab10 u10 m10 rm10 p10 pT10 pe10 o10 bc11 e11 s11 ab11 u11 m11 rm11 p11 pT11 pe11 o11 "
    "bc12 e12 s12 ab12 u12 m12 rm12 p12 pT12 pe12 o12 bc13 e13 s13 ab13 u13 m13 rm13 p13 pT13 pe13 o13 rn "
    "y x"]
P_ORDER = {
    "dve": "zc u00 m00 rm00 u01 m01 u02 m02 rm01 pe00 min u03 rm02 pe01 m03 lg cum rm03 hg hi u10 pe02 m10 he "
        "rm10 u11 vc r1 pe03 m11 rm11 u12 m12 pe10 u13 rm12 pe11 m13 mid mid2 rm13 pe12 kc0 pe13 lo kc1 rn y",
    "pe": "bc00 s00 xT bc01 s01 bc02 g s02 bc03 s03 bc10 pT00 s10 o00 pT01 s11 o01 pT02 hgT bc11 s12 pT03 v "
        "bc12 s13 o02 o03 pT10 bc13 q0 pT11 o10 q1 pT12 o11 k0 pT13 o12 k1 o13",
    "act": "e00 ab00 e01 xTe ab01 e02 p00 ab02 abs e03 ab03 p01 exp ln ab10 p02 e10 ab11 p03 e11 ab12 e12 p10 "
        "ab13 p11 e13 qc0 p12 qc1 p13",
    "pool": "x"}

M_STAGES = [
    "sq me rr xr xT xTe xe pad skip gate cv0 cv1 cv2 cv3 xs u bc ue hi r1 mid mid2 lo z abs exp ln pos "
    "delta xx dx",
    "bc0 a0 c0 bx0 h0 hc0 y0 bc1 a1 c1 bx1 h1 hc1 y1 bc2 a2 c2 bx2 h2 hc2 y2 bc3 a3 c3 bx3 h3 hc3 y3 bc4 "
    "a4 c4 bx4 h4 hc4 y4 bc5 a5 c5 bx5 h5 hc5 y5 bc6 a6 c6 bx6 h6 hc6 y6 bc7 a7 c7 bx7 h7 hc7 y7 ys yg "
    "out x"]
M_ORDER = {
    "dve": "bx0 xr bx1 h0 h1 bx2 cv0 bx3 h2 h3 bx4 cv1 h4 bx5 cv2 h5 cv3 bx6 h6 bx7 ue h7 hi r1 mid2 pos mid lo "
        "delta ys yg x",
    "pe": "bc0 bc1 bc2 xT xe bc3 skip y0 bc4 bc5 y1 y2 y3 bc6 bc7 y4 u bc y5 z y6 y7 out",
    "act": "sq a0 c0 a1 c1 xTe a2 pad c2 a3 c3 a4 c4 a5 a6 c5 gate c6 xs a7 c7 abs exp ln",
    "pool": "me rr hc0 hc1 hc2 hc3 hc4 hc5 hc6 hc7 xx dx"}


def run_layers(eng, stages, step, count):
    n = 1 + max(stages.stage.values())
    assert n == 3 and count % 2 == 0

    def window(k, parity, live, layer_of):
        for s in stages.order:
            lag = stages.stage[s]
            if lag in live:
                layer = layer_of(lag)
                step(s, layer, k - lag - layer * count, (parity - lag) % 2)

    for k in (1, 2):
        window(k, k % 2, range(k), lambda lag: 0)
    for layer in range(2):
        with eng.Fori(0, (count - 2) // 2) as p:
            for b in (1, 0):
                window(2 * p + (layer * count + 4 - b), b, range(n), lambda lag: layer)
        if layer == 0:
            for k in (count + 1, count + 2):
                window(k, k % 2, range(n), lambda lag: int(k - lag > count))
    for k in (2 * count + 1, 2 * count + 2):
        window(k, k % 2, range(k - 2 * count, n), lambda lag: 1)


def build(nc, ins, out):
    with ExitStack() as ctx:
        def sb(name, shape, dt=F32):
            return ctx.enter_context(nc.sbuf_tensor(name, shape, dt))

        m_ctx = ExitStack()

        def m_sb(name, shape, dt=F32):
            return m_ctx.enter_context(nc.sbuf_tensor(name, shape, dt))

        def sem(name):
            return ctx.enter_context(nc.semaphore(name))

        bank = [ctx.enter_context(nc.psum_tensor(f"bank{n}", [P, 512], F32)) for n in range(2)]
        pair = [ctx.enter_context(nc.psum_tensor(f"pair{n}", [P, 1024], F32)) for n in range(3)]

        X = sb("X", [P, NSEQ, L])
        Z = sb("Z", [P, NSEQ, L])
        ident = sb("ident", [P, P])
        identb = sb("identb", [P, P], BF16)
        sel = sb("sel", [96, 32, P], BF16)
        band = sb("band", [P, L], BF16)
        tri = sb("tri", [P, P], BF16)
        shift = sb("shift", [P, P])
        carry = sb("carry", [P, P])
        ones = sb("ones", [P, L])
        mhalf = sb("mhalf", [P, 2 * H])
        eps = sb("eps", [P, LN_PART * T])
        eps_sum = sb("eps_sum", [P, T])
        carrier = sb("carrier", [P, 1])
        lst = sb("lst", [P, NSEQ, T, 6])
        lmv = sb("lmv", [P, NSEQ, T, 2])
        lve = sb("lve", [P, NSEQ, T])
        lrs = sb("lrs", [P, NSEQ, T])

        loaded = sem("loaded")
        x_loaded = sem("x_loaded")
        const_set = sem("const_set")
        stored = sem("stored")

        consts = [(ident[:], "ident"), (identb[:], "identb"), (sel[:], "sel"), (band[:], "band"), (tri[:], "tri"),
                  (shift[:], "shift"), (carry[:], "carry")]

        mw = dict(
            in_w=sb("m_in_w", [P, E]), skip_w=sb("m_skip_w", [P, E]), wd1=sb("m_wd1", [P, EC, DD]),
            wbc=sb("m_wbc", [P, EC, 2 * NS]), wd2=sb("m_wd2", [DD, E]), out_w=sb("m_out_w", [P, EC, D]),
            norm_w=sb("m_norm_w", [P, 1]), conv_w=sb("m_conv_w", [P, EC, CONV]), conv_b=sb("m_conv_b", [P, EC]),
            wd2_b=sb("m_wd2_b", [P, EC]), A_log=sb("m_A_log", [P, EC, NS]), W_D=sb("m_W_D", [P, EC]))
        consts += [(t[:], "m_" + n) for n, t in mw.items()]
        m_A = sb("m_A", [P, EC, NS])
        m_pad = sb("m_pad", [P, EC, CONV - 1 + L])
        m_a = sb("m_a", [P, 2, GN, EC, L])

        pe_m, act_m, dve_m, pool_m = (Stages(sem, "m_" + e, M_ORDER[e], M_STAGES) for e in ("pe", "act", "dve", "pool"))

        ln_stats, ln_z = sem("ln_stats"), sem("ln_z")
        ln_moments, ln_var, ln_centred, ln_rstd = (sem("ln_" + n) for n in ("moments", "var", "centred", "rstd"))

        fw = dict(
            wqkv=sb("f_wqkv", [P, 3 * INNER]), wo=sb("f_wo", [P, INNER // P, D]), w1=sb("f_w1", [P, 2 * HID]),
            w2=sb("f_w2", [P, HC, D]), b2=sb("f_b2", [P, D]), qs=sb("f_qs", [P, 2, DH]), lg=sb("f_lg", [P, 1]),
            lb=sb("f_lb", [P, 1]), b1=sb("f_b1", [P, 2, HC]))
        rot = sb("rot", [P, T, 2, 2, DH])
        consts += [(rot[:], "rot")]
        f_tab = sb("f_tab", [P, T, 2, 2, DH])
        f_hT = sb("f_hT", [P, L])
        f_v = sb("f_v", [P, 2, T, H, DH + 1])
        f_p = sb("f_p", [P, T, 4, L])

        pe_f, act_f, dve_f, pool_f = (Stages(sem, "f_" + e, F_ORDER[e], F_STAGES) for e in ("pe", "act", "dve", "pool"))
        f_first, f_last = ["wqkv", "qs"], ["wo", "w1", "w2", "b2", "lg", "lb", "b1"]
        assert sorted(fw) == sorted(f_first + f_last)
        f_first_loaded = sem("f_first_loaded")
        f_last_loaded = sem("f_last_loaded")
        f_table = sem("f_table")
        zeroed = sem("zeroed")
        x_done = sem("x_done")

        pw = dict(wqk=sb("p_wqk", [P, 2, PG, P]), wv=sb("p_wv", [P, D]), wg=sb("p_wg", [P, PH]))
        consts += [(t[:], "p_" + n) for n, t in pw.items()]
        p_v = sb("p_v", [P, 2, T, PH, PS + 1])
        p_g3 = sb("p_g3", [96, 2, L], BF16)
        m_sq = m_sb("m_sq", [P, T, P])
        m_ss = m_sb("m_ss", [P, T])
        m_rr = m_sb("m_rr", [P, T])
        m_xr = m_sb("m_xr", [P, T, P])
        m_xT = m_sb("m_xT", [P, L])
        m_xc = m_sb("m_xc", [P, 2, EC, L])
        m_xs = m_sb("m_xs", [P, 2, EC, L])
        m_gate = m_sb("m_gate", [P, 2, EC, L])
        m_u = m_sb("m_u", [DD, L])
        m_r = m_sb("m_r", [32, 2, L])
        m_mid = m_sb("m_mid", [32, L], BF16)
        m_bc = m_sb("m_bc", [96, 2, L], BF16)
        m_t = m_sb("m_t", [P, 3, EC, L])
        m_pos = m_sb("m_pos", [P, EC, L])
        m_delta = m_sb("m_delta", [P, 2, EC, L])
        m_dx = m_sb("m_dx", [P, 2, EC, L])
        m_xx = m_sb("m_xx", [P, 2, L])
        m_bx = m_sb("m_bx", [P, 2, GN, EC, L])
        m_h = m_sb("m_h", [P, 2, GN, EC, L])
        m_c = m_sb("m_c", [P, 2, GN, L])
        m_hc = m_sb("m_hc", [P, 2, GN, EC, L])
        m_y = m_sb("m_y", [P, EC, L])
        m_yg = m_sb("m_yg", [P, EC, L])
        m_ctx.close()
        f_zc = m_sb("f_zc", [P, L])
        f_z1 = m_sb("f_z1", [P, L])
        f_sq = m_sb("f_sq", [P, 2 * INNER])
        f_ss = m_sb("f_ss", [P, 2 * H])
        f_cs = m_sb("f_cs", [P, 2 * H])
        f_rn = m_sb("f_rn", [P, 2 * H])
        f_kn = m_sb("f_kn", [P, 2, 2 * H, DH])
        f_qa = m_sb("f_qa", [P, 2, 2 * H, DH])
        f_qb = m_sb("f_qb", [P, 2, 2 * H, DH])
        f_qT = m_sb("f_qT", [P, 2, H, L])
        f_kT = m_sb("f_kT", [P, 2, H // 2, L])
        f_nm = m_sb("f_nm", [P, 2, 4])
        f_pT = m_sb("f_pT", [P, 2, 8, P])
        f_rs = m_sb("f_rs", [P, 4])
        f_o = m_sb("f_o", [P, 2, T, H, DH])
        f_oT = m_sb("f_oT", [P, INNER // P, L])
        f_hb = m_sb("f_hb", [P, T, P])
        f_st = m_sb("f_st", [P, T, 6])
        f_mv = m_sb("f_mv", [P, T, 2])
        f_ve = m_sb("f_ve", [P, T])
        f_rv = m_sb("f_rv", [P, T])
        f_hn = m_sb("f_hn", [P, T, P])
        f_hnT = m_sb("f_hnT", [P, L])
        f_g = m_sb("f_g", [P, HC, L])
        f_u = m_sb("f_u", [P, HC, L])
        f_zb = m_sb("f_zb", [P, L])
        m_ctx.close()
        p_zc = sb("p_zc", [P, L])
        p_xT = sb("p_xT", [P, L])
        p_qT = sb("p_qT", [P, 2, PH, L])
        p_kT = sb("p_kT", [P, 2, PG, L])
        p_t = sb("p_t", [PH, 5, L])
        p_hg = sb("p_hg", [PH, L])
        p_hgT = sb("p_hgT", [P, 2, T, PH])
        p_mid = sb("p_mid", [PH, L], BF16)
        p_e = sb("p_e", [P, 2, 4, L])
        p_a = sb("p_a", [P, 2, 4, L])
        p_s = sb("p_s", [P, 2, 4, L])
        p_m = sb("p_m", [P, 2, 4])
        p_rm = sb("p_rm", [P, 2, 4])
        p_p = sb("p_p", [P, 2, 4, L])
        p_pT = sb("p_pT", [P, 2, 8, P])
        p_rn = sb("p_rn", [P, T, PH])
        p_y = sb("p_y", [P, T, PH, PS])
        pe_p, act_p, dve_p, pool_p = (Stages(sem, "p_" + e, P_ORDER[e], P_STAGES) for e in ("pe", "act", "dve", "pool"))

        def credit(eng, *streams):
            for s in streams:
                for t in s.streams if isinstance(s, Stages) else [s]:
                    if t:
                        eng.sem_inc(t.sem, t.credit)

        def half(t, k):
            return t[:, 512 * k:512 * k + 512]

        m_xe_ps = half(pair[0], 0).rearrange("p (c l) -> p c l", c=EC)
        m_sk_ps = half(pair[0], 1).rearrange("p (c l) -> p c l", c=EC)
        m_xT_ps = bank[0][:, 0:L]
        m_u_ps = bank[0][0:DD, 0:L]
        m_bc_ps = bank[0][0:2 * NS, L:2 * L]
        m_y_ps = bank[1][:].rearrange("p (c l) -> p c l", c=EC)

        def m_bcast(g, k):
            return half(pair[1 + g % 2], k).rearrange("p (n l) -> p n l", n=GN)

        def seq(t, i):
            return t[:, i - 1, :]

        def tiles(ap):
            return ap.rearrange("p (t d) -> p t d", t=T)

        def m_before(stages, i, step, g, back):
            return stages.at(i if g >= back else i - 1, f"{step}{(g - back) % NG}")

        M_LAST = NG - 1

        def m_pe(pe, s, i, b):
            k, g = s.rstrip("0123456789"), int("0" + s[len(s.rstrip("0123456789")):])
            if s == "xT":
                pe.wait_ge(*dve_m.at(i, "xr"))
                pe.wait_ge(*dve_m.at(i - 1, "lo"))
                for t in range(T):
                    mm = nc.tensor.transpose(m_xT_ps[:, t * P:t * P + P], m_xr[:, t, :], ident[:])
            elif s == "xe" or s == "skip":
                pe.wait_ge(*act_m.at(i, "xTe"))
                pe.wait_ge(*(dve_m.at(i - 1, "pos") if s == "xe" else act_m.at(i - 1, "gate")))
                o, w = (m_xe_ps, mw["in_w"]) if s == "xe" else (m_sk_ps, mw["skip_w"])
                for c in range(EC):
                    mm = nc.tensor.matmul(o[:, c, :], w[:, c * P:c * P + P], m_xT[:], start=True, stop=True)
            elif s == "u" or s == "bc":
                pe.wait_ge(*act_m.at(i, "xs"))
                o, w = (m_u_ps, mw["wd1"]) if s == "u" else (m_bc_ps, mw["wbc"])
                for c in range(EC):
                    mm = nc.tensor.matmul(o, w[:, c, :], m_xs[:, b, c, :], start=c == 0, stop=c == EC - 1)
            elif s == "z":
                pe.wait_ge(*dve_m.at(i, "ue"))
                pe.wait_ge(*act_m.at(i, "pad"))
                for c in range(EC):
                    mm = nc.tensor.matmul(m_xe_ps[:, c, :], mw["wd2"][:, c * P:c * P + P], m_u[:], start=True, stop=True)
            elif k == "bc":
                pe.wait_ge(*dve_m.at(i, "lo"))
                pe.wait_ge(*m_before(dve_m, i, "bx", g, 2))
                pe.wait_ge(*m_before(act_m, i, "c", g, 2))
                for c in range(2):
                    for n in range(GN):
                        mm = nc.tensor.matmul(m_bcast(g, c)[:, n, :], sel[:, c * NS + g * GN + n, :], m_bc[:, b, :],
                                              start=True, stop=True)
            elif k == "y":
                pe.wait_ge(*pool_m.at(i, f"hc{g}"))
                if g == 0:
                    pe.wait_ge(*dve_m.at(i - 1, "x"))
                for n in range(GN):
                    mm = nc.tensor.matmul(bank[1][:], ident[:], m_hc[:, g % 2, n].rearrange("p c l -> p (c l)"),
                                          start=g == 0 and n == 0, stop=g == NG - 1 and n == GN - 1)
            elif s == "out":
                pe.wait_ge(*dve_m.at(i, "yg"))
                for t in range(T):
                    for c in range(EC):
                        mm = nc.tensor.matmul(bank[1][:, t * P:t * P + P], m_yg[:, c, t * P:t * P + P],
                                              mw["out_w"][:, c, :], start=c == 0, stop=c == EC - 1)
            mm.then_inc(*pe_m.done(s))

        def m_act(act, s, i, b, z_at):
            k, g = s.rstrip("0123456789"), int("0" + s[len(s.rstrip("0123456789")):])
            if s == "sq":
                act.wait_ge(*pool_m.at(i - 1, "rr"))
                for t in range(T):
                    op = nc.scalar.activation(m_sq[:, t, :], tiles(seq(Z, z_at))[:, t, :], ACT.Square,
                                              accum_out=m_ss[:, t:t + 1])
            elif s == "xTe":
                act.wait_ge(*pe_m.at(i, "xT"))
                op = nc.scalar.activation(m_xT[:], m_xT_ps, ACT.Copy, scale=mw["norm_w"][:])
            elif s == "pad":
                act.wait_ge(*pe_m.at(i, "xe"))
                act.wait_ge(*dve_m.at(i - 1, "cv3"))
                op = nc.scalar.activation(m_pad[:, :, CONV - 1:], m_xe_ps, ACT.Copy)
            elif s == "gate":
                act.wait_ge(*pe_m.at(i, "skip"))
                act.wait_ge(*dve_m.at(i - 2, "yg"))
                op = nc.scalar.activation(m_gate[:, b], m_sk_ps, ACT.Silu)
            elif s == "xs":
                act.wait_ge(*dve_m.at(i, "cv3"))
                act.wait_ge(*dve_m.at(i - 2, "ys"))
                op = nc.scalar.activation(m_xs[:, b], m_xc[:, 1], ACT.Silu)
            elif s == "abs":
                act.wait_ge(*pe_m.at(i, "z"))
                for c in range(EC):
                    op = nc.scalar.activation(m_t[:, 0, c, :], m_xe_ps[:, c, :], ACT.Abs, bias=mw["wd2_b"][:, c:c + 1])
            elif s == "exp":
                act.wait_ge(*act_m.at(i, "abs"))
                op = nc.scalar.activation(m_t[:, 1], m_t[:, 0], ACT.Exp, scale=-1.0)
            elif s == "ln":
                act.wait_ge(*act_m.at(i, "exp"))
                act.wait_ge(*dve_m.at(i - 1, "delta"))
                op = nc.scalar.activation(m_t[:, 2], m_t[:, 1], ACT.Ln, bias=ones[:, 0:1])
            elif k == "a":
                act.wait_ge(const_set, 13)
                act.wait_ge(*dve_m.at(i, "delta"))
                act.wait_ge(*m_before(dve_m, i, "h", g, 2))
                for n in range(GN):
                    for c in range(EC):
                        op = nc.scalar.activation(m_a[:, g % 2, n, c, 1:L], m_delta[:, b, c, 1:L], ACT.Exp,
                                                  scale=m_A[:, c, g * GN + n:g * GN + n + 1])
            elif k == "c":
                act.wait_ge(*pe_m.at(i, f"bc{g}"))
                act.wait_ge(*m_before(pool_m, i, "hc", g, 2))
                op = nc.scalar.activation(m_c[:, g % 2], m_bcast(g, 1), ACT.Copy)
            op.then_inc(*act_m.done(s))

        def m_dve(dve, s, i, b, z_at):
            k, g = s.rstrip("0123456789"), int("0" + s[len(s.rstrip("0123456789")):])
            if s == "xr":
                dve.wait_ge(*pool_m.at(i, "rr"))
                dve.wait_ge(*pe_m.at(i - 1, "xT"))
                for t in range(T):
                    op = nc.vector.tensor_scalar(m_xr[:, t, :], tiles(seq(Z, z_at))[:, t, :], m_rr[:, t:t + 1],
                                                 float(D) ** 0.5, ALU.mult, ALU.mult)
            elif k == "cv":
                if g == 0:
                    dve.wait_ge(*act_m.at(i, "pad"))
                    dve.wait_ge(*act_m.at(i - 1, "xs"))
                else:
                    dve.wait_ge(*dve_m.at(i, f"cv{g - 1}"))
                for c in range(EC):
                    tap, x = mw["conv_w"][:, c, g:g + 1], m_pad[:, c, g:g + L]
                    if g == 0:
                        op = nc.vector.tensor_scalar(m_xc[:, 0, c, :], x, tap, mw["conv_b"][:, c:c + 1], ALU.mult, ALU.add)
                    else:
                        op = nc.vector.scalar_tensor_tensor(out=m_xc[:, g % 2, c, :], in0=x, scalar=tap,
                                                            in1=m_xc[:, (g + 1) % 2, c, :], op0=ALU.mult, op1=ALU.add)
            elif s == "ue":
                dve.wait_ge(*pe_m.at(i, "bc"))
                dve.wait_ge(*pe_m.at(i - 1, "z"))
                op = nc.vector.tensor_copy(m_u[:], m_u_ps)
            elif s == "hi":
                dve.wait_ge(*pe_m.at(i, "bc"))
                dve.wait_ge(*pe_m.at(i - 2, f"bc{M_LAST}"))
                op = nc.vector.tensor_copy(m_bc[0:32, b], m_bc_ps)
            elif s == "r1":
                dve.wait_ge(*dve_m.at(i, "hi"))
                op = nc.vector.tensor_tensor(m_r[:, 0], m_bc_ps, m_bc[0:32, b], ALU.subtract)
            elif s == "mid":
                dve.wait_ge(*dve_m.at(i, "r1"))
                op = nc.vector.tensor_copy(m_mid[:], m_r[:, 0])
            elif s == "mid2":
                dve.wait_ge(*dve_m.at(i, "r1"))
                op = nc.vector.tensor_copy(m_bc[32:64, b], m_r[:, 0])
            elif s == "lo":
                dve.wait_ge(*dve_m.at(i, "mid"))
                op = nc.vector.tensor_tensor(m_bc[64:96, b], m_r[:, 0], m_mid[:], ALU.subtract)
            elif s == "pos":
                dve.wait_ge(*act_m.at(i, "abs"))
                for c in range(EC):
                    op = nc.vector.tensor_scalar(m_pos[:, c, :], m_xe_ps[:, c, :], mw["wd2_b"][:, c:c + 1], 0.0,
                                                 ALU.add, ALU.max)
            elif s == "delta":
                dve.wait_ge(*dve_m.at(i, "pos"))
                dve.wait_ge(*act_m.at(i, "ln"))
                dve.wait_ge(*act_m.at(i - 2, f"a{M_LAST}"))
                op = nc.vector.tensor_tensor(m_delta[:, b], m_pos[:], m_t[:, 2], ALU.add)
            elif k == "bx":
                dve.wait_ge(*pe_m.at(i, f"bc{g}"))
                dve.wait_ge(*pool_m.at(i, "dx"))
                dve.wait_ge(*m_before(dve_m, i, "h", g, 2))
                op = nc.vector.tensor_tensor(m_bx[:, g % 2], m_dx[:, b].unsqueeze(1).broadcast_to([P, GN, EC, L]),
                                             m_bcast(g, 0).unsqueeze(2).broadcast_to([P, GN, EC, L]), ALU.mult)
            elif k == "h":
                dve.wait_ge(*dve_m.at(i, f"bx{g}"))
                dve.wait_ge(*act_m.at(i, f"a{g}"))
                dve.wait_ge(*m_before(pool_m, i, "hc", g, 2))
                flat = "p n c l -> p (n c l)"
                op = nc.vector.tensor_tensor_scan(m_h[:, g % 2].rearrange(flat), m_a[:, g % 2].rearrange(flat),
                                                  m_bx[:, g % 2].rearrange(flat), 0.0, ALU.mult, ALU.add)
            elif s == "ys":
                dve.wait_ge(*pe_m.at(i, f"y{M_LAST}"))
                for c in range(EC):
                    op = nc.vector.scalar_tensor_tensor(out=m_y[:, c, :], in0=m_xs[:, b, c, :], scalar=mw["W_D"][:, c:c + 1],
                                                        in1=m_y_ps[:, c, :], op0=ALU.mult, op1=ALU.add)
            elif s == "yg":
                dve.wait_ge(*dve_m.at(i, "ys"))
                dve.wait_ge(*pe_m.at(i - 1, "out"))
                op = nc.vector.tensor_tensor(m_yg[:], m_y[:], m_gate[:, b], ALU.mult)
            elif s == "x":
                dve.wait_ge(*pe_m.at(i, "out"))
                dve.wait_ge(*pool_m.at(i, "xx"))
                op = nc.vector.tensor_tensor(seq(X, z_at), m_xx[:, b], bank[1][:, 0:L], ALU.add)
            op.then_inc(*dve_m.done(s))

        def m_pool(pool, s, i, b, z_at):
            k, g = s.rstrip("0123456789"), int("0" + s[len(s.rstrip("0123456789")):])
            if s == "me":
                pool.wait_ge(*act_m.at(i, "sq"))
                pool.wait_ge(*dve_m.at(i - 1, "xr"))
                op = nc.gpsimd.tensor_tensor(m_rr[:], m_ss[:], eps_sum[:], ALU.add)
            elif s == "rr":
                pool.wait_ge(*pool_m.at(i, "me"))
                op = nc.gpsimd.tensor_tensor(m_rr[:], m_rr[:], mhalf[:, 0:T], ALU.pow)
            elif s == "xx":
                pool.wait_ge(*dve_m.at(i - 2, "x"))
                op = nc.gpsimd.tensor_tensor(m_xx[:, b], seq(X, z_at), seq(Z, z_at), ALU.add)
            elif s == "dx":
                pool.wait_ge(*dve_m.at(i, "delta"))
                pool.wait_ge(*dve_m.at(i - 2, f"bx{M_LAST}"))
                op = nc.gpsimd.tensor_tensor(m_dx[:, b], m_delta[:, b], m_xs[:, b], ALU.mult)
            elif k == "hc":
                pool.wait_ge(*dve_m.at(i, f"h{g}"))
                pool.wait_ge(*act_m.at(i, f"c{g}"))
                pool.wait_ge(*m_before(pe_m, i, "y", g, 2))
                for n in range(GN):
                    op = nc.gpsimd.tensor_tensor(m_hc[:, g % 2, n], m_h[:, g % 2, n],
                                                 m_c[:, g % 2, n].unsqueeze(1).broadcast_to([P, EC, L]), ALU.mult)
            op.then_inc(*pool_m.done(s))

        def ln_dve(dve, k, ready):
            dve.wait_ge(*ready)
            for i in range(NSEQ):
                for t in range(T):
                    op = nc.vector.bn_stats(lst[:, i, t, :], tiles(X[:, i, :])[:, t, :])
                op.then_inc(ln_stats, 1)
            for half_ in range(LN_PARTS):
                dve.wait_ge(ln_stats, k * NSEQ + (half_ + 1) * LN_PART)
                for i in range(half_ * LN_PART, (half_ + 1) * LN_PART):
                    for t in range(T):
                        op = nc.vector.bn_aggr(lmv[:, i, t, :], lst[:, i, t, :])
                op.then_inc(ln_moments, 1)
            for half_ in range(LN_PARTS):
                q = slice(half_ * LN_PART, (half_ + 1) * LN_PART)
                x, z = (v[:, q, :].rearrange("p i (t d) -> p (i t) d", t=T) for v in (X, Z))
                wide = [P, LN_PART * T, D]
                dve.wait_ge(ln_moments, k * LN_PARTS + half_ + 1)
                nc.vector.tensor_tensor(z, x, lmv[:, q, :, 0].rearrange("p i t -> p (i t)").unsqueeze(2)
                                        .broadcast_to(wide), ALU.subtract).then_inc(ln_centred, 1)
                dve.wait_ge(ln_centred, k * LN_PARTS + half_ + 1)
                dve.wait_ge(ln_rstd, k * LN_PARTS + half_ + 1)
                nc.vector.tensor_tensor(z, z, lrs[:, q, :].rearrange("p i t -> p (i t)").unsqueeze(2)
                                        .broadcast_to(wide), ALU.mult).then_inc(ln_z, LN_PART)

        def ln_pool(pool, k):
            for half_ in range(LN_PARTS):
                q = slice(half_ * LN_PART, (half_ + 1) * LN_PART)
                pool.wait_ge(ln_moments, k * LN_PARTS + half_ + 1)
                nc.gpsimd.tensor_tensor(lve[:, q, :], lmv[:, q, :, 1], eps[:].rearrange("p (i t) -> p i t", t=T),
                                        ALU.add).then_inc(ln_var, 1)
                pool.wait_ge(ln_var, k * LN_PARTS + half_ + 1)
                nc.gpsimd.tensor_tensor(lrs[:, q, :].rearrange("p i t -> p (i t)"),
                                        lve[:, q, :].rearrange("p i t -> p (i t)"),
                                        mhalf[:, 0:LN_PART * T], ALU.pow).then_inc(ln_rstd, 1)

        QK = pair[0][:].rearrange("p (x h d) -> p (x h) d", x=2, h=H)
        SC = pair[1][:].rearrange("p (j k) -> p j k", j=4)
        PT_PS = half(pair[2], 0)
        O_PS = half(pair[2], 1)
        KEYS = [(0, P), (P - W, L)]

        def slot(h):
            return (h % 2) * 2 + (h // 2) % 2

        def part_before(t, g):
            return (f"{t}{g - 1}" if g else f"{t - 1}1", 0) if (t, g) != (0, 0) else ("11", 1)

        def f_pe(pe, s, i, b, n):
            k, a = s.rstrip("0123456789"), [int(x) for x in s[len(s.rstrip("0123456789")):]]
            if s == "xT":
                pe.wait_ge(*dve_f.at(i, "zc"))
                pe.wait_ge(*act_f.at(i - 1, "Te11"))
                for t in range(T):
                    mm = nc.tensor.transpose(bank[0][:, t * P:t * P + P], f_zc[:, t * P:t * P + P], ident[:])
            elif k == "qk":
                t, = a
                pe.wait_ge(*dve_f.at(i, "hT"))
                pe.wait_ge(*(dve_f.at(i, "kn0") if t else dve_f.at(i - 1, "kn1")))
                if t == 0:
                    pe.wait_ge(f_first_loaded, 16 * len(f_first) * n)
                for n in range(2):
                    mm = nc.tensor.matmul(half(pair[0], n), f_hT[:, t * P:t * P + P], fw["wqkv"][:, n * 512:n * 512 + 512],
                                          start=True, stop=True)
            elif k == "v":
                t, = a
                if t:
                    pe.wait_ge(*act_f.at(i, "ve0"))
                else:
                    pe.wait_ge(*dve_f.at(i, "hT"))
                mm = nc.tensor.matmul(bank[0][:], f_hT[:, t * P:t * P + P], fw["wqkv"][:, 1024:1536], start=True, stop=True)
            elif k == "T":
                t, x = a
                pe.wait_ge(*dve_f.at(i, f"qs{t}"))
                pe.wait_ge(*act_f.at(i, "ve1" if (t, x) == (0, 0) else f"Te{t}0" if x else "Te01"))
                for c in range(4):
                    h = x * H + 2 * c
                    mm = nc.tensor.transpose(bank[0][:, c * P:c * P + P],
                                             f_qa[:, t, h:h + 2, :].rearrange("p h d -> p (h d)"), ident[:])
            elif k == "s":
                t, g = a
                k0, k1 = KEYS[t]
                pe.wait_ge(*act_f.at(i, "Te11"))
                n, back = part_before(t, g)
                pe.wait_ge(*act_f.at(i - back, "p" + n))
                m0 = k0 - t * P + P
                for j in range(2):
                    nc.tensor.matmul(SC[:, 2 * j:2 * j + 2, k0:k1], identb[:],
                                     band[:, m0:m0 + k1 - k0].unsqueeze(1).broadcast_to([P, 2, k1 - k0]),
                                     start=True, stop=False, skip_group_check=True)
                for h in range(4 * g, 4 * g + 4):
                    mm = nc.tensor.matmul(SC[:, slot(h), k0:k1], f_qT[:, b, h, t * P:t * P + P],
                                          f_kT[:, b, h // 2, k0:k1], start=False, stop=True, skip_group_check=True)
            elif k == "pT":
                t, g, y = a
                pe.wait_ge(*act_f.at(i, f"p{t}{g}"))
                if y:
                    pe.wait_ge(*act_f.at(i, f"pe{t}{g}0"))
                else:
                    n, back = part_before(t, g)
                    pe.wait_ge(*(dve_f.at(i - back, f"pe{n}1") if n[0] == "1" else act_f.at(i - back, f"pe{n}0")))
                for j in range(4):
                    mm = nc.tensor.transpose(PT_PS[:, j * P:j * P + P], f_p[:, t, j, y * P:y * P + P], ident[:])
            elif k == "o":
                t, g = a
                pe.wait_ge(*act_f.at(i, f"pe{t}{g}0"))
                if t:
                    pe.wait_ge(*dve_f.at(i, f"pe{t}{g}1"))
                n, back = part_before(t, g)
                pe.wait_ge(*dve_f.at(i - back, "on" + n))
                for h in range(4 * g, 4 * g + 4):
                    for y in range(t + 1):
                        mm = nc.tensor.matmul(O_PS[:, (h % 4) * (DH + 1):(h % 4 + 1) * (DH + 1)],
                                              f_pT[:, g, 4 * y + slot(h), :], f_v[:, b, y, h, :], start=y == 0, stop=y == t)
            elif k == "oT":
                t, = a
                pe.wait_ge(*dve_f.at(i, f"on{t}1"))
                pe.wait_ge(*(act_f.at(i, "oe0") if t else dve_f.at(i - 1, "z2")))
                for c in range(4):
                    mm = nc.tensor.transpose(bank[1][:, c * P:c * P + P],
                                             f_o[:, b, t, 2 * c:2 * c + 2, :].rearrange("p h d -> p (h d)"), ident[:])
            elif s == "wo":
                pe.wait_ge(f_last_loaded, 16 * len(f_last) * n)
                pe.wait_ge(*act_f.at(i, "oe1"))
                for t in range(T):
                    for c in range(4):
                        mm = nc.tensor.matmul(bank[1][:, t * P:t * P + P], f_oT[:, c, t * P:t * P + P], fw["wo"][:, c, :],
                                              start=c == 0, stop=c == 3)
            elif s == "sh":
                pe.wait_ge(*dve_f.at(i, "z1"))
                zt = tiles(f_z1[:])
                nc.tensor.matmul(bank[1][:, 0:64], shift[:], zt[:, 0, 64:128], start=True, stop=True)
                nc.tensor.matmul(bank[1][:, 64:128], shift[:], zt[:, 1, 64:128], start=True, stop=False)
                mm = nc.tensor.matmul(bank[1][:, 64:128], carry[:], zt[:, 0, 64:128], start=False, stop=True)
            elif s == "hnT":
                pe.wait_ge(*dve_f.at(i, "hn"))
                for t in range(T):
                    mm = nc.tensor.transpose(bank[1][:, t * P:t * P + P], f_hn[:, t, :], ident[:])
            elif k == "w1a" or k == "w1b" or k == "w1c":
                todo = {"w1a": ((1, 0), (1, 1)), "w1b": ((1, 2), (0, 2)), "w1c": ((0, 0), (0, 1))}[k]
                pe.wait_ge(*{"w1a": act_f.at(i, "he"), "w1b": act_f.at(i, "g0"), "w1c": dve_f.at(i, "u1")}[k])
                for n, (x, c) in enumerate(todo):
                    mm = nc.tensor.matmul(bank[1][0:HR[c], n * L:n * L + L],
                                          fw["w1"][:, x * HID + c * P:x * HID + c * P + HR[c]], f_hnT[:],
                                          start=True, stop=True)
            elif s == "w2":
                pe.wait_ge(*dve_f.at(i, "u0"))
                for t in range(T):
                    for c in range(HC):
                        mm = nc.tensor.matmul(bank[1][:, t * P:t * P + P], f_u[0:HR[c], c, t * P:t * P + P],
                                              fw["w2"][0:HR[c], c, :], start=c == 0, stop=c == HC - 1)
            mm.then_inc(*pe_f.done(s))

        def f_act(act, s, i, b):
            k, a = s.rstrip("0123456789"), [int(x) for x in s[len(s.rstrip("0123456789")):]]
            if k == "sq":
                t, = a
                act.wait_ge(*pe_f.at(i, f"qk{t}"))
                act.wait_ge(*(dve_f.at(i, "ss0") if t else dve_f.at(i - 1, "ss1")))
                op = nc.scalar.activation(f_sq[:], pair[0][:], ACT.Square)
            elif k == "ve":
                t, = a
                act.wait_ge(*pe_f.at(i, f"v{t}"))
                act.wait_ge(*pe_f.at(i - 2, "o11"))
                op = nc.scalar.activation(f_v[:, b, t, :, 0:DH], bank[0][:].rearrange("p (h d) -> p h d", h=H), ACT.Copy)
            elif k == "Te":
                t, x = a
                act.wait_ge(*pe_f.at(i, f"T{t}{x}"))
                act.wait_ge(*pe_f.at(i - 2, "s11"))
                T_PS = bank[0][:].rearrange("p (c k) -> p c k", c=4)
                if x:
                    op = nc.scalar.activation(f_kT[:, b, :, t * P:t * P + P], T_PS, ACT.Copy)
                else:
                    for e in range(2):
                        r = slice(DH * e, DH * e + DH)
                        op = nc.scalar.activation(
                            f_qT[r, b].rearrange("p (c e) l -> p c e l", e=2)[:, :, e, t * P:t * P + P], T_PS[r], ACT.Copy)
            elif k == "p":
                t, g = a
                k0, k1 = KEYS[t]
                act.wait_ge(*dve_f.at(i, f"nm{t}{g}"))
                act.wait_ge(*(pe_f.at(i, f"pT{t}0{t}") if g else pe_f.at(i - 1, f"pT{t}1{t}")))
                for j in range(4):
                    op = nc.scalar.activation(f_p[:, t, j, k0:k1], SC[:, j, k0:k1], ACT.Exp, bias=f_nm[:, g, j:j + 1])
            elif k == "pe":
                t, g, y = a
                act.wait_ge(*pe_f.at(i, "pT" + s[2:]))
                act.wait_ge(*(pe_f.at(i, f"o0{g}") if t else pe_f.at(i - 1, f"o1{g}")))
                op = nc.scalar.activation(f_pT[:, g, 4 * y:4 * y + 4, :], PT_PS.rearrange("p (c k) -> p c k", c=4), ACT.Copy)
            elif k == "oe":
                t, = a
                act.wait_ge(*pe_f.at(i, f"oT{t}"))
                act.wait_ge(*pe_f.at(i - 1, "wo"))
                op = nc.scalar.activation(f_oT[:, :, t * P:t * P + P], bank[1][:].rearrange("p (c k) -> p c k", c=4), ACT.Copy)
            elif s == "hb":
                act.wait_ge(*pe_f.at(i, "sh"))
                nc.scalar.activation(f_hb[:, :, 64:128], bank[1][:, 0:128].rearrange("p (t d) -> p t d", t=T), ACT.Copy)
                op = nc.scalar.activation(f_hb[:, :, 0:64], tiles(f_z1[:])[:, :, 0:64], ACT.Copy)
            elif s == "he":
                act.wait_ge(*pe_f.at(i, "hnT"))
                op = nc.scalar.activation(f_hnT[:], bank[1][:, 0:L], ACT.Identity, bias=fw["lb"][:], scale=fw["lg"][:])
            elif s == "g0" or s == "g1":
                act.wait_ge(*pe_f.at(i, "w1a" if s == "g0" else "w1b"))
                for n, c in ((0, 0), (1, 1)) if s == "g0" else ((0, 2),):
                    op = nc.scalar.activation(f_g[0:HR[c], c, :], bank[1][0:HR[c], n * L:n * L + L], ACT.Gelu,
                                              bias=fw["b1"][0:HR[c], 1, c:c + 1])
            op.then_inc(*act_f.done(s))

        def rotary_table(dve, n):
            dve.wait_ge(f_first_loaded, 16 * len(f_first) * n)
            dve.wait_ge(*dve_f.at((n - 1) * NSEQ, "qa1"))
            dve.wait_ge(*pool_f.at((n - 1) * NSEQ, "qb1"))
            for t in range(T):
                for x in range(2):
                    qs = fw["qs"][:, x, :]
                    nc.vector.tensor_tensor(f_tab[:, t, x, 0], rot[:, t, x, 0], qs, ALU.mult)
                    for e in range(2):
                        o = slice(32 * e, 32 * e + 32)
                        op = nc.vector.tensor_tensor(f_tab[:, t, x, 1, o], rot[:, t, x, 1, o],
                                                     qs[:, 32 - 32 * e:64 - 32 * e], ALU.mult)
            op.then_inc(f_table, 1)

        def f_dve(dve, s, i, b, z_at, n):
            k, a = s.rstrip("0123456789"), [int(x) for x in s[len(s.rstrip("0123456789")):]]
            if s == "kn0" and isinstance(z_at, int) and z_at == 1:
                rotary_table(dve, n)
            if s == "zc":
                dve.wait_ge(*pe_f.at(i - 1, "xT"))
                op = nc.vector.tensor_scalar(f_zc[:], seq(Z, z_at), 1.0, None, ALU.mult)
            elif s == "hT":
                dve.wait_ge(*pe_f.at(i, "xT"))
                dve.wait_ge(*pe_f.at(i - 1, "qk1"))
                dve.wait_ge(*pe_f.at(i - 1, "v1"))
                nc.vector.tensor_copy(f_hT[0:64, :], bank[0][0:64, 0:L])
                op = nc.vector.tensor_copy(f_hT[64:128, 1:L], bank[0][64:128, 0:L - 1])
            elif k == "ss":
                t, = a
                dve.wait_ge(*act_f.at(i, f"sq{t}"))
                op = nc.vector.tensor_reduce(f_ss[:], f_sq[:].rearrange("p (h d) -> p h d", h=2 * H), AX.X, ALU.add)
            elif k == "cl":
                t, = a
                dve.wait_ge(*dve_f.at(i, f"ss{t}"))
                dve.wait_ge(*(pool_f.at(i, "rn0") if t else pool_f.at(i - 1, "rn1")))
                op = nc.vector.tensor_scalar(f_cs[:], f_ss[:], 1e-24, None, ALU.max)
            elif k == "kn":
                t, = a
                dve.wait_ge(*pool_f.at(i, f"rn{t}"))
                dve.wait_ge(*pool_f.at(i - 1, f"qb{t}"))
                op = nc.vector.tensor_tensor(f_kn[:, t], QK, f_rn[:].unsqueeze(2).broadcast_to([P, 2 * H, DH]), ALU.mult)
            elif k == "qa":
                t, = a
                dve.wait_ge(*dve_f.at(i, f"kn{t}"))
                dve.wait_ge(f_table, n)
                dve.wait_ge(*pe_f.at(i - 1, f"T{t}1"))
                op = nc.vector.tensor_tensor(f_qa[:, t].rearrange("p (x h) d -> p x h d", x=2),
                                             f_kn[:, t].rearrange("p (x h) d -> p x h d", x=2),
                                             f_tab[:, t, :, 0].unsqueeze(2).broadcast_to([P, 2, H, DH]), ALU.mult)
            elif k == "qs":
                t, = a
                dve.wait_ge(*dve_f.at(i, f"qa{t}"))
                dve.wait_ge(*pool_f.at(i, f"qb{t}"))
                op = nc.vector.tensor_tensor(f_qa[:, t], f_qa[:, t], f_qb[:, t], ALU.add)
            elif k == "nm":
                t, g = a
                k0, k1 = KEYS[t]
                dve.wait_ge(*pe_f.at(i, f"s{t}{g}"))
                dve.wait_ge(*(act_f.at(i, f"p0{g}") if t else act_f.at(i - 1, f"p1{g}")))
                op = nc.vector.tensor_reduce(f_nm[:, g, :], SC[:, :, k0:k1], AX.X, ALU.max, negate=True)
            elif k == "pe":
                t, g, y = a
                dve.wait_ge(*pe_f.at(i, "pT" + s[2:]))
                dve.wait_ge(*(pe_f.at(i, f"o0{g}") if t else pe_f.at(i - 1, f"o1{g}")))
                op = nc.vector.tensor_copy(f_pT[:, g, 4 * y:4 * y + 4, :], PT_PS.rearrange("p (c k) -> p c k", c=4))
            elif k == "rs":
                dve.wait_ge(*pe_f.at(i, "o" + s[2:]))
                op = nc.vector.reciprocal(f_rs[:], O_PS[:, 0:4 * (DH + 1)].rearrange("p (h d) -> p h d", h=4)[:, :, DH])
            elif k == "on":
                t, g = a
                dve.wait_ge(*dve_f.at(i, "rs" + s[2:]))
                dve.wait_ge(*pe_f.at(i - 2, f"oT{t}"))
                op = nc.vector.tensor_tensor(f_o[:, b, t, 4 * g:4 * g + 4, :],
                                             O_PS[:, 0:4 * (DH + 1)].rearrange("p (h d) -> p h d", h=4)[:, :, 0:DH],
                                             f_rs[:].unsqueeze(2).broadcast_to([P, 4, DH]), ALU.mult)
            elif s == "z1":
                dve.wait_ge(*pe_f.at(i, "wo"))
                dve.wait_ge(*pool_f.at(i - 1, "zb"))
                dve.wait_ge(*act_f.at(i - 1, "hb"))
                op = nc.vector.tensor_tensor(f_z1[:], seq(Z, z_at), bank[1][:, 0:L], ALU.add)
            elif s == "st":
                dve.wait_ge(*act_f.at(i, "hb"))
                for t in range(T):
                    op = nc.vector.bn_stats(f_st[:, t, :], f_hb[:, t, :])
            elif s == "mv":
                dve.wait_ge(*dve_f.at(i, "st"))
                dve.wait_ge(*pool_f.at(i - 1, "vv"))
                nc.vector.tensor_copy(carrier[:], eps[:, 0:1])
                for t in range(T):
                    op = nc.vector.bn_aggr(f_mv[:, t, :], f_st[:, t, :])
            elif s == "hn":
                dve.wait_ge(*pool_f.at(i, "rv"))
                dve.wait_ge(*pe_f.at(i - 1, "hnT"))
                for t in range(T):
                    op = nc.vector.tensor_scalar(f_hn[:, t, :], f_hb[:, t, :], f_mv[:, t, 0:1], f_rv[:, t:t + 1],
                                                 ALU.subtract, ALU.mult)
            elif s == "u0" or s == "u1":
                dve.wait_ge(*(act_f.at(i, "g1") if s == "u1" else pe_f.at(i, "w1c")))
                for n, c in ((0, 0), (1, 1)) if s == "u0" else ((1, 2),):
                    r = HR[c]
                    op = nc.vector.scalar_tensor_tensor(out=f_u[0:r, c, :], in0=bank[1][0:r, n * L:n * L + L],
                                                        scalar=fw["b1"][0:r, 0, c:c + 1], in1=f_g[0:r, c, :],
                                                        op0=ALU.add, op1=ALU.mult)
            elif s == "z2":
                dve.wait_ge(*pe_f.at(i, "w2"))
                dve.wait_ge(*pool_f.at(i, "zb"))
                op = nc.vector.tensor_tensor(seq(Z, z_at), f_zb[:], bank[1][:, 0:L], ALU.add)
            op.then_inc(*dve_f.done(s))

        def f_pool(pool, s, i, b):
            k, a = s.rstrip("0123456789"), [int(x) for x in s[len(s.rstrip("0123456789")):]]
            if k == "rn":
                t, = a
                pool.wait_ge(*dve_f.at(i, f"cl{t}"))
                pool.wait_ge(*(dve_f.at(i, "kn0") if t else dve_f.at(i - 1, "kn1")))
                op = nc.gpsimd.tensor_tensor(f_rn[:], f_cs[:], mhalf[:], ALU.pow)
            elif k == "qb":
                t, = a
                pool.wait_ge(*dve_f.at(i, f"kn{t}"))
                pool.wait_ge(*dve_f.at(i - 1, f"qs{t}"))
                for e in range(2):
                    o = slice(32 * e, 32 * e + 32)
                    op = nc.gpsimd.tensor_tensor(
                        f_qb[:, t, :, o].rearrange("p (x h) d -> p x h d", x=2),
                        f_kn[:, t, :, 32 - 32 * e:64 - 32 * e].rearrange("p (x h) d -> p x h d", x=2),
                        f_tab[:, t, :, 1, o].unsqueeze(2).broadcast_to([P, 2, H, 32]), ALU.mult)
            elif s == "vv":
                pool.wait_ge(*dve_f.at(i, "mv"))
                op = nc.gpsimd.tensor_tensor(f_ve[:], f_mv[:, :, 1], eps[:, 0:T], ALU.add)
            elif s == "rv":
                pool.wait_ge(*pool_f.at(i, "vv"))
                op = nc.gpsimd.tensor_tensor(f_rv[:], f_ve[:], mhalf[:, 0:T], ALU.pow)
            elif s == "zb":
                pool.wait_ge(*dve_f.at(i, "z1"))
                pool.wait_ge(*dve_f.at(i - 1, "z2"))
                op = nc.gpsimd.tensor_tensor(tiles(f_zb[:]), tiles(f_z1[:]),
                                             fw["b2"][:].unsqueeze(1).broadcast_to([P, T, D]), ALU.add)
            op.then_inc(*pool_f.done(s))

        def p_head(g, j):
            return 4 * (2 * (g // 2) + j % 2) + 2 * (g % 2) + j // 2

        def p_before(stages, i, step, t, g, back):
            n = PG * t + g - back
            return stages.at(i if n >= 0 else i - 1, f"{step}{n % (T * PG) // PG}{n % PG}")

        P_LAST = f"{T - 1}{PG - 1}"

        def p_pe(pe, s, i, b):
            k, a = s.rstrip("0123456789"), [int(x) for x in s[len(s.rstrip("0123456789")):]]
            if s == "xT":
                pe.wait_ge(*dve_p.at(i, "zc"))
                pe.wait_ge(*dve_p.at(i - 1, "kc1"))
                for t in range(T):
                    mm = nc.tensor.transpose(bank[0][:, t * P:t * P + P], p_zc[:, t * P:t * P + P], ident[:])
            elif s == "g":
                pe.wait_ge(*act_p.at(i, "xTe"))
                mm = nc.tensor.matmul(bank[0][0:PH, 0:L], pw["wg"][:], p_xT[:], start=True, stop=True)
            elif s == "hgT":
                pe.wait_ge(*dve_p.at(i, "hg"))
                for t in range(T):
                    mm = nc.tensor.matmul(bank[0][:, t * PH:t * PH + PH], p_hg[:, t * P:t * P + P], ident[0:PH, 0:PH],
                                          start=True, stop=True)
            elif s == "v":
                pe.wait_ge(*dve_p.at(i, "he"))
                for t in range(T):
                    mm = nc.tensor.matmul(bank[0][:, t * P:t * P + P], p_xT[:, t * P:t * P + P], pw["wv"][:],
                                          start=True, stop=True)
            elif k == "q" or k == "k":
                y, = a
                pe.wait_ge(*{"q0": dve_p.at(i, "vc"), "q1": act_p.at(i, "qc0"), "k0": act_p.at(i, "qc1"),
                             "k1": dve_p.at(i, "kc0")}[s])
                for g in range(2):
                    mm = nc.tensor.matmul(bank[0][:, g * L:g * L + L], pw["wqk"][:, "qk".index(k), 2 * y + g, :], p_xT[:],
                                          start=True, stop=True)
            elif k == "bc":
                t, g = a
                n = P * (t + 1)
                pe.wait_ge(*dve_p.at(i, "lo"))
                pe.wait_ge(*p_before(act_p, i, "e", t, g, 1))
                for j in range(4):
                    o = pair[0][:, j * L:j * L + n]
                    nc.tensor.matmul(o, sel[:, p_head(g, j), :], p_g3[:, b, 0:n], start=True, stop=False,
                                     skip_group_check=True)
                    mm = nc.tensor.matmul(o[:, n - P:n], identb[:], tri[:], start=False, stop=True, skip_group_check=True)
            elif k == "s":
                t, g = a
                n = P * (t + 1)
                pe.wait_ge(*dve_p.at(i, "kc1"))
                pe.wait_ge(*p_before(act_p, i, "ab", t, g, 1))
                for j in (0, 2, 1, 3):
                    h = p_head(g, j)
                    mm = nc.tensor.matmul(pair[1][:, j * L:j * L + n], p_qT[:, b, h, t * P:t * P + P],
                                          p_kT[:, b, h // 4, 0:n], start=True, stop=True)
            elif k == "pT":
                t, g = a
                pe.wait_ge(*act_p.at(i, f"p{t}{g}"))
                pe.wait_ge(*p_before(dve_p, i, "pe", t, g, 1))
                for j in range(4):
                    for y in range(t + 1):
                        mm = nc.tensor.transpose(pair[2][:, (4 * y + j) * P:(4 * y + j) * P + P],
                                                 p_p[:, g % 2, j, y * P:y * P + P], ident[:])
            elif k == "o":
                t, g = a
                pe.wait_ge(*dve_p.at(i, f"pe{t}{g}"))
                if (t, g) == (0, 0):
                    pe.wait_ge(*dve_p.at(i - 1, "y"))
                for j in range(4):
                    h = p_head(g, j)
                    for y in range(t + 1):
                        mm = nc.tensor.matmul(bank[1][:, (t * PH + h) * (PS + 1):(t * PH + h + 1) * (PS + 1)],
                                              p_pT[:, g % 2, 4 * y + j, :], p_v[:, b, y, h, :], start=y == 0, stop=y == t)
            mm.then_inc(*pe_p.done(s))

        def p_act(act, s, i, b):
            k, a = s.rstrip("0123456789"), [int(x) for x in s[len(s.rstrip("0123456789")):]]
            if s == "xTe":
                act.wait_ge(*pe_p.at(i, "xT"))
                act.wait_ge(*pe_p.at(i - 1, "v"))
                act.wait_ge(*pe_p.at(i - 1, "k1"))
                op = nc.scalar.activation(p_xT[:], bank[0][:, 0:L], ACT.Copy)
            elif s == "abs":
                act.wait_ge(*pe_p.at(i, "g"))
                op = nc.scalar.activation(p_t[:, 0], bank[0][0:PH, 0:L], ACT.Abs)
            elif s == "exp":
                act.wait_ge(*act_p.at(i, "abs"))
                op = nc.scalar.activation(p_t[:, 1], p_t[:, 0], ACT.Exp, scale=-1.0)
            elif s == "ln":
                act.wait_ge(*act_p.at(i, "exp"))
                act.wait_ge(*dve_p.at(i - 1, "lg"))
                op = nc.scalar.activation(p_t[:, 2], p_t[:, 1], ACT.Ln, bias=ones[0:PH, 0:1])
            elif k == "qc":
                y, = a
                act.wait_ge(*pe_p.at(i, f"q{y}"))
                act.wait_ge(*pe_p.at(i - 2, "s" + P_LAST))
                for x in range(4):
                    r = slice(32 * x, 32 * x + 32)
                    op = nc.scalar.activation(p_qT[r, b].rearrange("p (g x) l -> p g x l", x=4)[:, 2 * y:2 * y + 2, x, :],
                                              bank[0][r, :].rearrange("p (g l) -> p g l", g=2), ACT.Copy)
            elif k == "e":
                t, g = a
                n = P * (t + 1)
                act.wait_ge(*pe_p.at(i, f"bc{t}{g}"))
                act.wait_ge(*dve_p.at(i, "he"))
                act.wait_ge(*p_before(dve_p, i, "u", t, g, 2))
                for j in range(4):
                    h = p_head(g, j)
                    op = nc.scalar.activation(p_e[:, g % 2, j, 0:n], pair[0][:, j * L:j * L + n], ACT.Exp, scale=-1.0,
                                              bias=p_hgT[:, b, t, h:h + 1])
            elif k == "ab":
                t, g = a
                n = P * (t + 1)
                act.wait_ge(*pe_p.at(i, f"s{t}{g}"))
                act.wait_ge(*p_before(dve_p, i, "u", t, g, 2))
                op = nc.scalar.activation(p_a[:, g % 2, :, 0:n], pair[1][:].rearrange("p (j l) -> p j l", j=4)[:, :, 0:n],
                                          ACT.Abs)
            elif k == "p":
                t, g = a
                n = P * (t + 1)
                act.wait_ge(*dve_p.at(i, f"rm{t}{g}"))
                act.wait_ge(*p_before(pe_p, i, "pT", t, g, 2))
                for j in range(4):
                    op = nc.scalar.activation(p_p[:, g % 2, j, 0:n], p_s[:, g % 2, j, 0:n], ACT.Square,
                                              scale=p_rm[:, g % 2, j:j + 1])
            op.then_inc(*act_p.done(s))

        def p_dve(dve, s, i, b, z_at):
            k, a = s.rstrip("0123456789"), [int(x) for x in s[len(s.rstrip("0123456789")):]]
            if s == "zc":
                dve.wait_ge(ln_z, 3 * NSEQ)
                dve.wait_ge(*pe_p.at(i - 1, "xT"))
                op = nc.vector.tensor_scalar(p_zc[:], seq(Z, z_at), 1.0, None, ALU.mult)
            elif s == "min":
                dve.wait_ge(*act_p.at(i, "abs"))
                dve.wait_ge(*dve_p.at(i - 1, "hg"))
                op = nc.vector.tensor_scalar(p_t[:, 3], bank[0][0:PH, 0:L], 0.0, None, ALU.min)
            elif s == "lg":
                dve.wait_ge(*act_p.at(i, "ln"))
                dve.wait_ge(*dve_p.at(i, "min"))
                op = nc.vector.tensor_tensor(p_t[:, 4], p_t[:, 3], p_t[:, 2], ALU.subtract)
            elif s == "cum":
                dve.wait_ge(*dve_p.at(i, "lg"))
                op = nc.vector.tensor_tensor_scan(p_t[:, 3], ones[0:PH, :], p_t[:, 4], 0.0, ALU.mult, ALU.add)
            elif s == "hg":
                dve.wait_ge(*dve_p.at(i, "cum"))
                dve.wait_ge(*pe_p.at(i - 1, "hgT"))
                op = nc.vector.tensor_scalar(p_hg[:], p_t[:, 3], 0.5, None, ALU.mult)
            elif s == "hi":
                dve.wait_ge(*dve_p.at(i, "hg"))
                dve.wait_ge(*pe_p.at(i - 2, "bc" + P_LAST))
                op = nc.vector.tensor_copy(p_g3[0:PH, b], p_hg[:])
            elif s == "r1":
                dve.wait_ge(*dve_p.at(i, "hi"))
                op = nc.vector.tensor_tensor(p_t[:, 4], p_hg[:], p_g3[0:PH, b], ALU.subtract)
            elif s == "mid":
                dve.wait_ge(*dve_p.at(i, "r1"))
                op = nc.vector.tensor_copy(p_mid[:], p_t[:, 4])
            elif s == "mid2":
                dve.wait_ge(*dve_p.at(i, "r1"))
                op = nc.vector.tensor_copy(p_g3[32:32 + PH, b], p_t[:, 4])
            elif s == "lo":
                dve.wait_ge(*dve_p.at(i, "mid"))
                op = nc.vector.tensor_tensor(p_g3[64:64 + PH, b], p_t[:, 4], p_mid[:], ALU.subtract)
            elif s == "he":
                dve.wait_ge(*pe_p.at(i, "hgT"))
                dve.wait_ge(*act_p.at(i - 2, "e" + P_LAST))
                op = nc.vector.tensor_copy(p_hgT[:, b], bank[0][:, 0:T * PH].rearrange("p (t h) -> p t h", t=T))
            elif s == "vc":
                dve.wait_ge(*pe_p.at(i, "v"))
                dve.wait_ge(*pe_p.at(i - 2, "o" + P_LAST))
                for t in range(T):
                    op = nc.vector.tensor_copy(p_v[:, b, t, :, 0:PS],
                                               bank[0][:, t * P:t * P + P].rearrange("p (h d) -> p h d", h=PH))
            elif k == "kc":
                y, = a
                dve.wait_ge(*pe_p.at(i, f"k{y}"))
                dve.wait_ge(*pe_p.at(i - 2, "s" + P_LAST))
                op = nc.vector.tensor_copy(p_kT[:, b, 2 * y:2 * y + 2], bank[0][:].rearrange("p (g l) -> p g l", g=2))
            elif k == "u":
                t, g = a
                n = P * (t + 1)
                dve.wait_ge(*act_p.at(i, f"e{t}{g}"))
                dve.wait_ge(*act_p.at(i, f"ab{t}{g}"))
                dve.wait_ge(*p_before(act_p, i, "p", t, g, 2))
                op = nc.vector.scalar_tensor_tensor(out=p_s[:, g % 2, :, 0:n], in0=p_a[:, g % 2, :, 0:n], scalar=1e-7,
                                                    in1=p_e[:, g % 2, :, 0:n], op0=ALU.add, op1=ALU.mult)
            elif k == "m":
                t, g = a
                dve.wait_ge(*dve_p.at(i, f"u{t}{g}"))
                op = nc.vector.tensor_reduce(p_m[:, g % 2], p_s[:, g % 2, :, 0:P * (t + 1)], AX.X, ALU.max)
            elif k == "rm":
                t, g = a
                dve.wait_ge(*dve_p.at(i, f"m{t}{g}"))
                dve.wait_ge(*p_before(act_p, i, "p", t, g, 2))
                op = nc.vector.reciprocal(p_rm[:, g % 2], p_m[:, g % 2])
            elif k == "pe":
                t, g = a
                n = 4 * (t + 1)
                dve.wait_ge(*pe_p.at(i, f"pT{t}{g}"))
                dve.wait_ge(*p_before(pe_p, i, "o", t, g, 2))
                op = nc.vector.tensor_copy(p_pT[:, g % 2, 0:n, :], pair[2][:, 0:n * P].rearrange("p (c k) -> p c k", c=n))
            elif s == "rn":
                dve.wait_ge(*pe_p.at(i, "o" + P_LAST))
                op = nc.vector.reciprocal(p_rn[:], bank[1][:, 0:T * PH * (PS + 1)]
                                          .rearrange("p (t h d) -> p t h d", t=T, h=PH)[:, :, :, PS])
            elif s == "y":
                dve.wait_ge(*dve_p.at(i, "rn"))
                dve.wait_ge(*pool_p.at(i - 1, "x"))
                op = nc.vector.tensor_tensor(p_y[:], bank[1][:, 0:T * PH * (PS + 1)]
                                             .rearrange("p (t h d) -> p t h d", t=T, h=PH)[:, :, :, 0:PS],
                                             p_rn[:].unsqueeze(3).broadcast_to([P, T, PH, PS]), ALU.mult)
            op.then_inc(*dve_p.done(s))

        def p_pool(pool, s, i, b, x_at):
            pool.wait_ge(*dve_p.at(i, "y"))
            nc.gpsimd.tensor_tensor(seq(X, x_at), seq(X, x_at), p_y[:].rearrange("p t h d -> p (t h d)"),
                                    ALU.add).then_inc(*pool_p.done(s))

        block = ctx.enter_context(nc.Block())

        @block.sync
        def _(sp):
            xv = ins["x"].rearrange("b (t p) d -> p b t d", p=P)
            for b in range(NSEQ):
                sp.dma_start(tiles(X[:, b, :]), xv[:, b]).then_inc(x_loaded, 16)
            for t, name in consts:
                sp.dma_start(t, ins[name]).then_inc(loaded, 16)
            for call in range(CALLS):
                for layer in range(2):
                    before = (call * 2 + layer) * NSEQ
                    sp.wait_ge(*pe_f.at(before, "v1"))
                    sp.wait_ge(*pe_f.at(before, "qk1"))
                    sp.wait_ge(f_table, call * 2 + layer)
                    for name in f_first:
                        sp.dma_start(fw[name][:], ins["f_" + name][layer]).then_inc(f_first_loaded, 16)
                    sp.wait_ge(*dve_f.at(before, "z2"))
                    for name in f_last:
                        sp.dma_start(fw[name][:], ins["f_" + name][layer]).then_inc(f_last_loaded, 16)
            ov = out.rearrange("b (t p) d -> p b t d", p=P)
            for b in range(NSEQ):
                if b % LN_PART == 0:
                    sp.wait_ge(x_done, NSEQ * (CALLS - 1) + b + LN_PART)
                sp.dma_start(ov[:, b], tiles(X[:, b, :])).then_inc(stored, 16)
            sp.wait_ge(stored, 16 * NSEQ)

        NC = len(consts)

        @block.tensor
        def _(pe):
            credit(pe, pe_m, pe_f, pe_p)
            pe.wait_ge(loaded, 16 * NC)
            run_windows(pe, pe_m, lambda s, i, b: m_pe(pe, s, i, b), NSEQ)
            for call in range(CALLS):
                if call:
                    run_windows(pe, pe_p, lambda s, i, b: p_pe(pe, s, i, b), NSEQ)
                run_layers(pe, pe_f, lambda s, layer, at, b: f_pe(pe, s, (2 * call + layer) * NSEQ + at, b,
                                                                  2 * call + layer + 1), NSEQ)

        @block.scalar
        def _(act):
            credit(act, act_m, act_f, act_p)
            act.wait_ge(loaded, 16 * NC)
            act.wait_ge(const_set, 11)
            nc.scalar.activation(m_A[:], mw["A_log"][:], ACT.Exp).then_inc(const_set, 1)
            act.wait_ge(ln_z, NSEQ)
            run_windows(act, act_m, lambda s, i, b: m_act(act, s, i, b, i), NSEQ)
            for call in range(CALLS):
                if call:
                    act.wait_ge(zeroed, 4)
                    run_windows(act, act_p, lambda s, i, b: p_act(act, s, i, b), NSEQ)
                act.wait_ge(zeroed, 6 if call else 2)
                run_layers(act, act_f, lambda s, layer, at, b: f_act(act, s, (2 * call + layer) * NSEQ + at, b), NSEQ)

        @block.vector
        def _(dve):
            credit(dve, dve_m, dve_f, dve_p)
            ln_dve(dve, 0, (x_loaded, 16 * NSEQ))
            dve.wait_ge(loaded, 16 * NC)
            dve.wait_ge(const_set, 12)
            nc.vector.tensor_scalar(m_A[:], m_A[:], -1.0, None, ALU.mult).then_inc(const_set, 1)
            run_windows(dve, dve_m, lambda s, i, b: m_dve(dve, s, i, b, i), NSEQ)
            ln_dve(dve, 1, dve_m.at(NSEQ, "x"))
            for call in range(CALLS):
                if call:
                    run_windows(dve, dve_p, lambda s, i, b: p_dve(dve, s, i, b, i), NSEQ)
                    ln_dve(dve, 3, pool_p.at(NSEQ, "x"))
                dve.wait_ge(ln_z, (2 + 2 * call) * NSEQ)
                run_layers(dve, dve_f, lambda s, layer, at, b: f_dve(dve, s, (2 * call + layer) * NSEQ + at, b, at,
                                                                     2 * call + layer + 1), NSEQ)
                dve.wait_ge(*dve_f.at((call + 1) * 2 * NSEQ, "z2"))
                for half_ in range(LN_PARTS):
                    q = slice(half_ * LN_PART, (half_ + 1) * LN_PART)
                    nc.vector.tensor_tensor(X[:, q, :], X[:, q, :], Z[:, q, :], ALU.add).then_inc(x_done, LN_PART)
                if call == 0:
                    ln_dve(dve, 2, (x_done, NSEQ))

        @block.gpsimd
        def _(pool):
            credit(pool, pool_m, pool_f, pool_p)
            nc.gpsimd.memset(ones[:], 1.0).then_inc(const_set, 1)
            nc.gpsimd.memset(mhalf[:], -0.5).then_inc(const_set, 1)
            nc.gpsimd.memset(m_pad[:, :, 0:CONV - 1], 0.0).then_inc(const_set, 1)
            nc.gpsimd.memset(m_a[:, :, :, :, 0:1], 0.0).then_inc(const_set, 1)
            nc.gpsimd.memset(f_hT[:, 0:1], 0.0).then_inc(const_set, 1)
            nc.gpsimd.memset(f_v[:, :, :, :, DH:DH + 1].rearrange("p b t h d -> p (b t) h d"), 1.0).then_inc(const_set, 1)
            nc.gpsimd.memset(f_p[:], 0.0).then_inc(const_set, 1)
            nc.gpsimd.memset(p_v[:, :, :, :, PS:PS + 1].rearrange("p b t h d -> p (b t) h d"), 1.0).then_inc(const_set, 1)
            nc.gpsimd.memset(p_g3[:], 0.0).then_inc(const_set, 1)
            nc.gpsimd.memset(eps[:], LN_EPS).then_inc(const_set, 1)
            nc.gpsimd.memset(eps_sum[:], LN_EPS * D).then_inc(const_set, 1)
            pool.wait_ge(const_set, 11)
            ln_pool(pool, 0)
            run_windows(pool, pool_m, lambda s, i, b: m_pool(pool, s, i, b, i), NSEQ)
            ln_pool(pool, 1)
            for call in range(CALLS):
                if call:
                    run_windows(pool, pool_p, lambda s, i, b: p_pool(pool, s, i, b, i), NSEQ)
                    ln_pool(pool, 3)
                pool.wait_ge(*(pool_p.at(NSEQ, "x") if call else dve_m.at(NSEQ, "x")))
                for b in range(2):
                    nc.gpsimd.memset(f_qT[:, b], 0.0).then_inc(zeroed, 1)
                run_layers(pool, pool_f, lambda s, layer, at, b: f_pool(pool, s, (2 * call + layer) * NSEQ + at, b), NSEQ)
                if call == 0:
                    pool.wait_ge(*dve_f.at(2 * NSEQ, "z2"))
                    for b in range(2):
                        nc.gpsimd.memset(p_qT[:, b], 0.0).then_inc(zeroed, 1)
                    ln_pool(pool, 2)


def shape_constants(np, bf16):
    k = np.arange(P)
    big = 1e30
    sel = np.zeros((96, 32, P), np.float32)
    for r in range(96):
        sel[r, r % 32, :] = 1
    kk = np.arange(L)
    band = np.where((kk[None] > k[:, None] + P) | (kk[None] < k[:, None] + P - W), -big, 0.0)
    tri = np.where(k[None] > k[:, None], big, 0.0)
    half_idx = np.arange(0, DH, 2, dtype=np.float32)
    inv = (1.0 / np.float32(10000.0) ** (half_idx / np.float32(DH))).astype(np.float32)
    t = np.arange(L, dtype=np.float32)
    f = t[:, None] * inv[None]
    f = np.concatenate([f, f], -1)
    base = (half_idx + np.float32(0.4 * DH)) / np.float32(1.4 * DH)
    power = (t - L // 2) / np.float32(W // 2)
    scale = (base[None] ** power[:, None]).astype(np.float32)
    scale = np.concatenate([scale, scale], -1)
    cos, sin = np.cos(f), np.sin(f)
    sgn = np.concatenate([-np.ones(DH // 2), np.ones(DH // 2)])
    rot = np.stack([np.stack([8 * cos * scale, 8 * sin * scale * sgn], 1),
                    np.stack([cos / scale, sin / scale * sgn], 1)], 1)
    rot = rot.reshape(T, P, 2, 2, DH).transpose(1, 0, 2, 3, 4)
    f32 = np.float32
    return {"ident": np.eye(P, dtype=f32), "identb": np.eye(P, dtype=f32).astype(bf16), "sel": sel.astype(bf16),
            "band": band.astype(f32).astype(bf16), "tri": tri.astype(f32).astype(bf16),
            "shift": np.eye(P, k=1, dtype=f32), "carry": np.where((k[:, None] == P - 1) & (k[None] == 0), 1, 0).astype(f32),
            "rot": np.ascontiguousarray(rot.astype(f32))}


def lay_out(np, a):
    def chunks(w):
        return w.reshape(-1, P, w.shape[-1]).transpose(1, 0, 2)

    def col(v):
        return v.reshape(-1, P).T

    m, f = "L0_attn_a_", "L0_ffn_"
    out = {"x": a[m + "resid"]}
    out["m_in_w"] = a[m + "in_w"].T
    out["m_skip_w"] = a[m + "skip_w"].T
    out["m_wd1"] = chunks(a[m + "wd1"].T)
    out["m_wbc"] = chunks(np.concatenate([a[m + "wb"], a[m + "wc"]], 0).T)
    out["m_wd2"] = a[m + "wd2"].T
    out["m_out_w"] = chunks(a[m + "out_w"].T)
    out["m_norm_w"] = a[m + "norm_w"][:, None]
    out["m_conv_w"] = chunks(a[m + "conv_w"][:, 0, :])
    out["m_conv_b"] = col(a[m + "conv_b"])
    out["m_wd2_b"] = col(a[m + "wd2_b"])
    out["m_A_log"] = chunks(a[m + "A_log"])
    out["m_W_D"] = col(a[m + "W_D"])
    w = a["L0_attn_b_W"]
    qk = np.zeros((P, 2, PG, P), w.dtype)
    for x in range(2):
        for h in range(PH):
            qk[:, x, h // 4, 32 * (h % 4):32 * (h % 4) + PS] = w[x * D + h * PS:x * D + (h + 1) * PS].T
    out["p_wqk"] = qk
    out["p_wv"] = w[2 * D:3 * D].T
    out["p_wg"] = w[3 * D:].T
    out["f_wqkv"] = a[f + "wqkv"]
    out["f_wo"] = np.stack([chunks(x) for x in a[f + "wo"]])
    out["f_w1"] = a[f + "w1"]
    pad = np.zeros((2, HC * P - HID, D), w.dtype)
    out["f_w2"] = np.stack([chunks(x) for x in np.concatenate([a[f + "w2"], pad], 1)])
    out["f_b2"] = np.broadcast_to(a[f + "b2"][:, None, :], (2, P, D))
    qs = np.stack([a[f + "q_scale"], a[f + "k_scale"]], 1)
    out["f_qs"] = np.broadcast_to(qs[:, None], (2, P, 2, DH))
    out["f_lg"] = a[f + "ln_g"][:, :, None]
    out["f_lb"] = a[f + "ln_b"][:, :, None]
    b1 = a[f + "b1"].reshape(2, 2, HID)
    b1 = np.concatenate([b1, np.zeros((2, 2, HC * P - HID), b1.dtype)], -1)
    out["f_b1"] = b1.reshape(2, 2, HC, P).transpose(0, 3, 1, 2)
    return out


def kernel(**inputs):
    import numpy as np
    import concourse.bacc as bacc
    from concourse import mybir as mb
    from concourse.bass_utils import run_bass_kernel_spmd as run

    nc = bacc.Bacc("TRN2", target_bir_lowering=False, num_devices=1)
    arrays = lay_out(np, {k: np.asarray(v) for k, v in inputs.items()})
    arrays.update(shape_constants(np, mb.dt.np(mb.dt.bfloat16)))
    feeds, ins = {}, {}
    for name, v in arrays.items():
        v = np.ascontiguousarray(v)
        feeds[f"in_{name}"] = v
        ins[name] = nc.dram_tensor(f"in_{name}", v.shape, mb.dt.from_np(v.dtype), kind="ExternalInput").ap()
    out = nc.dram_tensor("out_x", (NSEQ, L, D), F32, kind="ExternalOutput").ap()
    build(nc, ins, out)
    r = run(nc, [feeds], core_ids=[0])
    return r.results[0]["out_x"]
```
